# Optimizing a Trainium2 kernel written in Bass

```python
import numpy as np
import jax
import jax.numpy as jnp

def _softmax(x, axis=-1):
    return jax.nn.softmax(x, axis=axis)

def _gelu(x):
    return jax.nn.gelu(x, approximate=True)

def _silu(x):
    return jax.nn.silu(x)

def _sigmoid(x):
    return jax.nn.sigmoid(x)

def _layernorm(x, axis=-1, eps=1e-05):
    m = jnp.mean(x, axis=axis, keepdims=True)
    v = jnp.var(x, axis=axis, keepdims=True)
    return (x - m) / jnp.sqrt(v + eps)

def _scatter_add(tgt, idx, src, axis=0):
    return tgt.at[idx].add(src)

def _segment_sum(src, seg, n):
    return jax.ops.segment_sum(src, seg, n)
kernel_name = 'mk_flamingo_gated_d1_seqx_r4_8be621'

def setup_inputs(seed: int=0):
    np.random.seed(seed)
    _w = jnp.asarray

    def _rec_inputs():
        import jax
        import jax.numpy as jnp
        _rk = jax.random.key(seed)
        x = 7.22e-05 + 1 * jax.random.normal(jax.random.fold_in(_rk, 1), (16, 128, 512), jnp.float32)
        _lenS = 128 - jax.random.randint(jax.random.fold_in(_rk, 7), (16,), 0, max(1, 128 // 4) + 1, jnp.int32)
        _lenS2 = 128 - jax.random.randint(jax.random.fold_in(_rk, 8), (16,), 0, max(1, 128 // 4) + 1, jnp.int32)
        _ctx_1024P = jax.random.normal(jax.random.fold_in(_rk, 11), (16, 16, 256), jnp.float32)
        _ctx_1024c = jax.random.dirichlet(jax.random.fold_in(_rk, 511), 0.3 * jnp.ones((16,), jnp.float32), (16, 128))
        _ctx_1024t = jnp.einsum('bsk,bkd->bsd', _ctx_1024c, _ctx_1024P)
        _ctx_1024t = _ctx_1024t * jax.lax.rsqrt(jnp.mean(jnp.square(_ctx_1024t)) + 1e-12) * 0.953939
        ctx_1024 = -1.39393e-06 + 0.999914 * (_ctx_1024t + 0.3 * jax.random.normal(jax.random.fold_in(_rk, 611), (16, 128, 256), jnp.float32))
        fside_BxSx2_0 = jax.random.uniform(jax.random.fold_in(_rk, 12), (16, 128, 2), jnp.float32, 0.0, 0.999707)
        _g = jax.random.normal(jax.random.fold_in(_rk, 9001), (2, 1), jnp.float32)
        _g = jnp.sign(_g) * jnp.maximum(jnp.abs(_g), 1.0) + (_g == 0) * 1.0
        g_xattn = _g[0]
        g_ffn = _g[1]
        return (x, ctx_1024, fside_BxSx2_0, g_xattn, g_ffn)
    x, ctx_1024, fside_BxSx2_0, g_xattn, g_ffn = _rec_inputs()

    def _L0_xattn_setup():
        import jax, jax.numpy as jnp
        import numpy as np
        DIM = 512
        CTX_DIM = 256
        N_HEADS = 32
        HEAD_DIM = DIM // N_HEADS
        POS_DIM = 2
        B, N, CTXN = (2, 512, 512)
        ROPE_BASE = 10000.0

        def apply_axial_rope(x, pos):
            b, n, h, d = x.shape
            p = pos.shape[-1]
            dpa = d // p
            half = dpa // 2
            freqs = ROPE_BASE ** (-jnp.arange(half, dtype=x.dtype) / half)
            ang = pos[..., :, None] * freqs
            cos = jnp.cos(ang)[:, :, None, :, :]
            sin = jnp.sin(ang)[:, :, None, :, :]
            xr = x.reshape(b, n, h, p, half, 2)
            x1, x2 = (xr[..., 0], xr[..., 1])
            out = jnp.stack([x1 * cos - x2 * sin, x1 * sin + x2 * cos], axis=-1)
            return out.reshape(b, n, h, d)
        key = jax.random.key(seed)
        ks = jax.random.split(key, 8)
        x = jax.random.normal(ks[0], (B, N, DIM), jnp.float32)
        ctx = jax.random.normal(ks[1], (B, CTXN, CTX_DIM), jnp.float32)
        pos_map = jax.random.uniform(ks[2], (B, N, POS_DIM), jnp.float32)
        ctx_pos_map = jax.random.uniform(ks[3], (B, CTXN, POS_DIM), jnp.float32)
        Wq = jax.random.normal(ks[4], (DIM, DIM), jnp.float32) / np.sqrt(DIM)
        Wkv = jax.random.normal(ks[5], (CTX_DIM, 2 * DIM), jnp.float32) / np.sqrt(CTX_DIM)
        Wout = jax.random.normal(ks[6], (DIM, DIM), jnp.float32) / np.sqrt(DIM)
        bout = jnp.zeros((DIM,), jnp.float32)
        return {'x': x, 'ctx': ctx, 'pos_map': pos_map, 'ctx_pos_map': ctx_pos_map, 'Wq': Wq, 'Wkv': Wkv, 'Wout': Wout, 'bout': bout}
    _L0_xattn_all = _L0_xattn_setup()
    _L0_xattn_in = {k: v for k, v in _L0_xattn_all.items() if k in ('Wq', 'Wkv', 'Wout', 'bout')}
    del _L0_xattn_all

    def _L0_ffn_setup():
        import jax, jax.numpy as jnp
        import numpy as np
        H, I, E, TOP_K = (512, 352, 16, 6)
        IS = 704
        NORM_TOPK_PROB = False

        def _silu_and_mul(gate_up):
            d = gate_up.shape[-1] // 2
            g, u = (gate_up[..., :d], gate_up[..., d:])
            return jax.nn.silu(g) * u
        key = jax.random.key(seed)
        ks = jax.random.split(key, 6)
        s = 0.02
        return {'x': jax.random.normal(ks[0], (1, 512, H), jnp.float32), 'gate_w': jax.random.normal(ks[1], (E, H), jnp.float32) * s, 'w1': jax.random.normal(ks[2], (E, 2 * I, H), jnp.float32) * s, 'w2': jax.random.normal(ks[3], (E, H, I), jnp.float32) * s, 'shared_w1': jax.random.normal(ks[4], (2 * IS, H), jnp.float32) * s, 'shared_w2': jax.random.normal(ks[5], (H, IS), jnp.float32) * s}
    _L0_ffn_all = _L0_ffn_setup()
    _L0_ffn_in = {k: v for k, v in _L0_ffn_all.items() if k in ('gate_w', 'w1', 'w2', 'shared_w1', 'shared_w2')}
    del _L0_ffn_all
    return {'x': x, 'ctx_1024': ctx_1024, 'fside_BxSx2_0': fside_BxSx2_0, 'g_xattn': g_xattn, 'g_ffn': g_ffn, 'L0_xattn_Wq': _L0_xattn_in['Wq'], 'L0_xattn_Wkv': _L0_xattn_in['Wkv'], 'L0_xattn_Wout': _L0_xattn_in['Wout'], 'L0_xattn_bout': _L0_xattn_in['bout'], 'L0_ffn_gate_w': _L0_ffn_in['gate_w'], 'L0_ffn_w1': _L0_ffn_in['w1'], 'L0_ffn_w2': _L0_ffn_in['w2'], 'L0_ffn_shared_w1': _L0_ffn_in['shared_w1'], 'L0_ffn_shared_w2': _L0_ffn_in['shared_w2']}

def reference(x, ctx_1024, fside_BxSx2_0, g_xattn, g_ffn, L0_xattn_Wq, L0_xattn_Wkv, L0_xattn_Wout, L0_xattn_bout, L0_ffn_gate_w, L0_ffn_w1, L0_ffn_w2, L0_ffn_shared_w1, L0_ffn_shared_w2):
    import jax
    import jax.numpy as jnp

    def _L0_xattn_ref(x, ctx, pos_map, ctx_pos_map, Wq, Wkv, Wout, bout):
        import jax, jax.numpy as jnp
        import numpy as np
        DIM = 512
        CTX_DIM = 256
        N_HEADS = 32
        HEAD_DIM = DIM // N_HEADS
        POS_DIM = 2
        B, N, CTXN = (2, 512, 512)
        ROPE_BASE = 10000.0

        def apply_axial_rope(x, pos):
            b, n, h, d = x.shape
            p = pos.shape[-1]
            dpa = d // p
            half = dpa // 2
            freqs = ROPE_BASE ** (-jnp.arange(half, dtype=x.dtype) / half)
            ang = pos[..., :, None] * freqs
            cos = jnp.cos(ang)[:, :, None, :, :]
            sin = jnp.sin(ang)[:, :, None, :, :]
            xr = x.reshape(b, n, h, p, half, 2)
            x1, x2 = (xr[..., 0], xr[..., 1])
            out = jnp.stack([x1 * cos - x2 * sin, x1 * sin + x2 * cos], axis=-1)
            return out.reshape(b, n, h, d)
        b, n, _ = x.shape
        ctx_n = ctx.shape[1]
        q = (x @ Wq).reshape(b, n, N_HEADS, HEAD_DIM)
        k, v = jnp.split(ctx @ Wkv, 2, axis=-1)
        k = k.reshape(b, ctx_n, N_HEADS, HEAD_DIM)
        v = v.reshape(b, ctx_n, N_HEADS, HEAD_DIM)
        q = apply_axial_rope(q, pos_map)
        k = apply_axial_rope(k, ctx_pos_map)
        scale = 1.0 / np.sqrt(HEAD_DIM).astype(np.float32)
        logits = jnp.einsum('bqhd,bkhd->bhqk', q, k) * scale
        w = jax.nn.softmax(logits, axis=-1)
        attn = jnp.einsum('bhqk,bkhd->bqhd', w, v)
        attn = attn.reshape(b, n, N_HEADS * HEAD_DIM)
        return attn @ Wout + bout

    def _L0_ffn_ref(x, gate_w, w1, w2, shared_w1, shared_w2):
        import jax, jax.numpy as jnp
        import numpy as np
        H, I, E, TOP_K = (512, 352, 16, 6)
        IS = 704
        NORM_TOPK_PROB = False

        def _silu_and_mul(gate_up):
            d = gate_up.shape[-1] // 2
            g, u = (gate_up[..., :d], gate_up[..., d:])
            return jax.nn.silu(g) * u
        B, S, Hd = x.shape
        xf = x.reshape(-1, Hd)
        T = xf.shape[0]
        shared_out = _silu_and_mul(xf @ shared_w1.T) @ shared_w2.T
        logits = xf @ gate_w.T
        probs = jax.nn.softmax(logits.astype(jnp.float32), axis=-1)
        routing_weights, selected = jax.lax.top_k(probs, TOP_K)
        if NORM_TOPK_PROB:
            routing_weights = routing_weights / routing_weights.sum(-1, keepdims=True)
        combine = jnp.zeros((T, E), jnp.float32).at[jnp.arange(T)[:, None], selected].add(routing_weights).astype(x.dtype)
        gate_up = jnp.einsum('th,eoh->teo', xf, w1)
        act = _silu_and_mul(gate_up)
        moe_out = jnp.einsum('te,tei,ehi->th', combine, act, w2)
        return (moe_out + shared_out).reshape(B, S, Hd)
    x = x + jnp.tanh(g_xattn[0]) * _L0_xattn_ref(_layernorm(x, axis=-1), ctx_1024, fside_BxSx2_0, fside_BxSx2_0, L0_xattn_Wq, L0_xattn_Wkv, L0_xattn_Wout, L0_xattn_bout)
    x = x + jnp.tanh(g_ffn[0]) * _L0_ffn_ref(_layernorm(x, axis=-1), L0_ffn_gate_w, L0_ffn_w1, L0_ffn_w2, L0_ffn_shared_w1, L0_ffn_shared_w2)
    return x

_drawn_inputs = setup_inputs


def setup_inputs(seed=0):
    import zlib

    import numpy as np

    out = dict(_drawn_inputs(seed))
    spreads = {'L0_xattn_bout': (0.0, 0.1)}
    factors = {'L0_ffn_gate_w': 8.0,
     'L0_ffn_w1': 6.553,
     'L0_ffn_w2': 6.59,
     'L0_ffn_shared_w1': 8.0,
     'L0_ffn_shared_w2': 8.0}
    for name, (base, spread) in spreads.items():
        noise = np.random.default_rng([zlib.crc32(name.encode()), seed]).standard_normal(out[name].shape)
        drawn = base * np.exp(spread * noise) if base else spread * noise
        out[name] = jnp.asarray(drawn.astype(out[name].dtype))
    for name, factor in factors.items():
        out[name] = (out[name] * factor).astype(out[name].dtype)
    return out
```

```python
from contextlib import ExitStack

import concourse.bass as bass
from concourse import mybir

F32 = mybir.dt.float32
F32R = mybir.dt.float32r
I32 = mybir.dt.int32
U32 = mybir.dt.uint32
ALU = mybir.AluOpType
ACT = mybir.ActivationFunctionType
AX = mybir.AxisListType

P = 128
BATCHES = 16
D = 512
DC = D // P
CTX = 256
CC = CTX // P
HEADS = 32
HD = D // HEADS
ANG = 8
GROUPS = 8
TOKENS = BATCHES * P
EXPERTS = 16
TOPK = 6
WIDTH = 352
WC = [(0, 128), (128, 128), (256, 96)]
SHARED = 2
BLOCK = 256
SUB = BLOCK // P
CAP = TOKENS + BLOCK
NAT = EXPERTS * CAP + BLOCK
ROWS = NAT + TOKENS
SHARED_BLOCKS = SHARED * TOKENS // BLOCK
ROUTED_BLOCKS = TOKENS * TOPK // BLOCK + EXPERTS
BLOCKS = SHARED_BLOCKS + ROUTED_BLOCKS
ROW_W = D
ROW_ID = D + EXPERTS + SHARED
ROW = ROW_ID + 2
EPS = 1e-5
SCALE = HD ** -0.5
TWO_PI = 6.283185307179586
TWO_PI_HI = 6.28125
NEWTON = 3
RSQRT_BITS = 1597463007.0
ROUND = 12582912.0

C_ID, C_UP, C_ONE = 0, 128, 256
C_IOTA = 384
C_CAP = C_IOTA + 16
C_THR = C_CAP + 16
C_TRI = C_THR + 8
C_EVEN = C_TRI + 256
C_ODD = C_EVEN + 1
C_G = C_ODD + 1
C_SE = C_G + 1
C_SROW = C_SE + 1
C_SM = C_SROW + 1
C_RM = C_SM + 1
C_P = C_RM + 1
C_FREQ = C_P + 1
C_N = C_FREQ + 8
K_ID, K_PAD, K_N = 0, BATCHES, BATCHES + SUB


def constants():
    import numpy as np
    c = np.zeros((P, C_N), np.float32)
    p = np.arange(P)
    c[:, C_ID:C_ID + P] = np.eye(P)
    c[:, C_UP:C_UP + P] = p[:, None] < p[None, :]
    c[:, C_ONE:C_ONE + P] = 1
    c[:, C_IOTA:C_IOTA + 16] = np.arange(16)
    c[:, C_CAP:C_CAP + 16] = np.arange(16) * CAP
    c[:, C_THR:C_THR + 8] = np.arange(8) * BLOCK
    c[:, C_TRI:C_TRI + 256] = (np.arange(16)[None, :] <= np.arange(16)[:, None]).reshape(1, 256)
    c[:, C_EVEN] = (p // HD) % 2 == 0
    c[:, C_ODD] = (p // HD) % 2 == 1
    c[:, C_G] = p - SHARED_BLOCKS
    c[:, C_SE] = EXPERTS + p // (TOKENS // BLOCK)
    c[:, C_SROW] = NAT + (p % (TOKENS // BLOCK)) * BLOCK
    c[:, C_SM] = p < SHARED_BLOCKS
    c[:, C_RM] = p >= SHARED_BLOCKS
    c[:, C_P] = p
    c[:, C_FREQ:C_FREQ + 8] = np.tile(np.float32(10000.0) ** (-np.arange(4, dtype=np.float32) / 4), 2)
    k = np.zeros((P, K_N), np.int32)
    k[:, K_ID:K_ID + BATCHES] = np.arange(BATCHES)[None, :] * P + p[:, None]
    k[:, K_PAD:K_PAD + SUB] = TOKENS + np.arange(SUB)[None, :] * P + p[:, None]
    return c, k


def need(eng, sem, value):
    if isinstance(value, int) and value <= 0:
        return
    eng.wait_ge(sem, value)


def waits_apart(eng, passed, *waits):
    for sem, v in waits:
        need(eng, sem, v)
    if any(not isinstance(v, int) for _, v in waits):
        eng.sem_inc(passed, 1)


class Chain:

    def __init__(self, eng, sem, per, block):
        self.eng, self.sem, self.per, self.base, self.k = eng, sem, per, block * per, 0

    def step(self, instruction):
        self.k += 1
        instruction.then_inc(self.sem, 1)

    def sync(self, passed=None, *others):
        if passed:
            waits_apart(self.eng, passed, (self.sem, self.base + self.k), *others)
        else:
            need(self.eng, self.sem, self.base + self.k)

    def end(self):
        assert self.k == self.per, (self.k, self.per)


def rounds(eng, blocks, stages):
    depth = len(stages)
    for r in range(4):
        for k, stage in enumerate(stages):
            if r - k >= 0:
                stage(r - k, (r - k) % 2, (r - k) // 2)
    with eng.Fori(2, blocks // 2) as i:
        for r in range(2):
            for k, stage in enumerate(stages):
                stage(2 * i + (r - k), (r - k) % 2, i + (r - k) // 2)
    for r in range(blocks, blocks + depth - 1):
        for k, stage in enumerate(stages):
            if r - k < blocks:
                stage(r - k, (r - k) % 2, (r - k) // 2)


def build(nc, x, ctx_t, pos, wq, wkv, wout, bout, gates, gate_w, w1, w2, cf, ci, out):
    rows = nc.dram_tensor("expert_rows", (ROWS, ROW), F32, kind="Internal").ap()
    table_dram = nc.dram_tensor("block_table", (BLOCKS, 2), I32, kind="Internal").ap()

    with ExitStack() as whole:
        def sb(stack, name, shape, dt=F32):
            return stack.enter_context(nc.sbuf_tensor(name, shape, dt))

        def sem(name):
            return whole.enter_context(nc.semaphore(name))

        bank = [whole.enter_context(nc.psum_tensor(f"bank{i}", [P, 512], F32)) for i in range(8)]
        w1_raw = [sb(whole, f"w1_raw{j}", [P, DC, 2 * WIDTH]) for j in range(2)]
        w2_raw = [sb(whole, f"w2_raw{j}", [P, 3, D]) for j in range(2)]
        const = sb(whole, "const", [P, C_N])
        table = sb(whole, "table", [1, 2 * BLOCKS], I32)
        ident = const[:, C_ID:C_ID + P]

        w1_in = [sem(f"w1_in{j}") for j in range(2)]
        w2_in = [sem(f"w2_in{j}") for j in range(2)]
        table_in = sem("table_in")

        def load_weights(sp, e, j):
            sp.dma_start(w1_raw[j][:], w1[e]).then_inc(w1_in[j], 16)
            sp.dma_start(w2_raw[j][:, 0:2, :], w2[e, 0:2].rearrange("c p n -> p c n")).then_inc(w2_in[j], 16)
            sp.dma_start(w2_raw[j][0:96, 2, :], w2[e, 2, 0:96]).then_inc(w2_in[j], 16)

        phase_a(nc, sb, sem, bank, const, ident, table, table_in, load_weights,
                x, ctx_t, pos, wq, wkv, wout, bout, gates, gate_w, cf, ci, out, rows, table_dram)
        phase_b(nc, sb, sem, bank, ident, table, table_in, load_weights,
                w1_raw, w2_raw, w1_in, w2_in, out, rows, w1, w2)


def phase_a(nc, sb, sem, bank, const, ident, table, table_in, load_weights,
            x, ctx_t, pos, wq, wkv, wout, bout, gates, gate_w, cf, ci, out, rows, table_dram):
    with ExitStack() as st:
        def t(name, shape, dt=F32):
            return sb(st, name, shape, dt)

        def two(name, shape, dt=F32):
            return [sb(st, f"{name}{j}", shape, dt) for j in range(2)]

        w_raw = t("w_raw", [P, 6144])
        w_hi = t("w_hi", [P, 6144], F32R)
        w_lo = t("w_lo", [P, 6144], F32R)
        parts = {"q": (0, 2048), "kv": (2048, 4096), "o": (4096, 6144)}
        q_w = [w[:, 0:2048].rearrange("p (c n) -> p c n", c=DC) for w in (w_hi, w_lo)]
        kv_w = [w[:, 2048:4096].rearrange("p (c n) -> p c n", c=CC) for w in (w_hi, w_lo)]
        o_w = [w[:, 4096:6144].rearrange("p (c n) -> p c n", c=DC) for w in (w_hi, w_lo)]
        gate_t = t("gate_t", [P, DC, EXPERTS])
        bout_b = t("bout_b", [P, D])
        gate2 = t("gate2", [P, 2])
        tanh2 = t("tanh2", [P, 2])
        ids = t("ids", [P, K_N], I32)
        pos_in = t("pos_in", [P, BATCHES, 2])
        ang = t("ang", [P, 2, BATCHES, ANG])
        turn = t("turn", [P, 2, BATCHES, ANG])
        sincos = t("sincos", [P, 2, BATCHES, ANG])
        pad_row = t("pad_row", [P, SUB, ROW])
        x_sb = two("x_sb", [P, D])
        c_raw = two("c_raw", [P, CC, P])
        c_hi = t("c_hi", [P, CC, P], F32R)
        c_lo = t("c_lo", [P, CC, P], F32R)
        stats = t("stats", [P, 6])
        mean1 = t("mean1", [P, 2])
        rstd1 = t("rstd1", [P, 1])
        xn = t("xn", [P, D])
        xt_hi = t("xt_hi", [P, DC, P], F32R)
        xt_lo = t("xt_lo", [P, DC, P], F32R)
        q_cos, q_sin = t("q_cos", [P, D]), t("q_sin", [P, D])
        k_cos, k_sin = t("k_cos", [P, D]), t("k_sin", [P, D])
        q_rope, k_rope = t("q_rope", [P, D]), t("k_rope", [P, D])
        v_one = two("v_one", [P, HEADS, HD + 1])
        q_t = two("q_t", [P, DC, P])
        k_t = two("k_t", [P, DC, 2, P])
        smax = two("smax", [P, 4])
        soft = two("soft", [P, 4, P])
        soft_t = two("soft_t", [P, 4, P])
        rsum = t("rsum", [P, HEADS])
        attn = t("attn", [P, HEADS, HD])
        at_hi = t("at_hi", [P, DC, P], F32R)
        at_lo = t("at_lo", [P, DC, P], F32R)
        proj = t("proj", [P, D])
        x1 = two("x1", [P, D])
        stats2 = t("stats2", [P, 6])
        mean2 = t("mean2", [P, 2])
        rstd2 = t("rstd2", [P, 1])
        row = two("row", [P, ROW])
        x2_t = t("x2_t", [P, DC, P])
        gmax, gneg, gsum, grec = (t(n, [P, 1]) for n in ("gmax", "gneg", "gsum", "grec"))
        gexp, prob = t("gexp", [P, EXPERTS]), t("prob", [P, EXPERTS])
        top, top_i, top_f = t("top", [P, 8]), t("top_i", [P, 8], U32), t("top_f", [P, 8])
        pick = t("pick", [P, TOPK, EXPERTS])
        pick_slot = t("pick_slot", [P, TOPK, EXPERTS])
        mask = t("mask", [P, EXPERTS])
        seen = t("seen", [P, EXPERTS])
        slot_e = t("slot_e", [P, EXPERTS])
        slot_f = t("slot_f", [P, 8])
        slots = two("slots", [P, 8], U32)
        cnt = t("cnt", [P, EXPERTS])
        over = t("over", [P, EXPERTS, 8])
        nblk = t("nblk", [P, EXPERTS])
        ends3 = t("ends3", [P, EXPERTS, EXPERTS])
        ends = t("ends", [P, EXPERTS])
        past = t("past", [P, EXPERTS])
        past_end = t("past_end", [P, EXPERTS])
        tb = t("tb", [P, 8])
        table_p = t("table_p", [P, 2], I32)
        pad_f = t("pad_f", [P, SUB, EXPERTS + 1])
        pad_slots = t("pad_slots", [P, SUB, EXPERTS + 1], U32)

        small_in, w_in = sem("small_in"), sem("w_in")
        w_hi_done, w_lo_done = sem("w_hi_done"), sem("w_lo_done")
        init_done, ones_done = sem("init_done"), sem("ones_done")
        angles, sincos_done, tanh_done, init_v = sem("angles"), sem("sincos_done"), sem("tanh_done"), sem("init_v")
        x_in = [sem(f"x_in{j}") for j in range(2)]
        c_in = [sem(f"c_in{j}") for j in range(2)]
        var1, rstd1_done, xn_done = sem("var1"), sem("rstd1_done"), sem("xn_done")
        c_hi_done, c_lo_done = sem("c_hi_done"), sem("c_lo_done")
        xt_mm, xt_hi_done, xt_lo_done = sem("xt_mm"), sem("xt_hi_done"), sem("xt_lo_done")
        q_mm, k_mm, v_mm = sem("q_mm"), sem("k_mm"), sem("v_mm")
        q_rot, k_rot, q_rope_done, k_rope_done = sem("q_rot"), sem("k_rot"), sem("q_rope_done"), sem("k_rope_done")
        v_done, qt_mm, qt_done, kt_mm, kt_done = (sem(n) for n in ("v_done", "qt_mm", "qt_done", "kt_mm", "kt_done"))
        score_mm, shifted, exp_done, prob_mm, prob_done, pv_mm = (
            sem(n) for n in ("score_mm", "shifted", "exp_done", "prob_mm", "prob_done", "pv_mm"))
        attn_done, at_mm, at_hi_done, at_lo_done, o_mm, x1_done = (
            sem(n) for n in ("attn_done", "at_mm", "at_hi_done", "at_lo_done", "o_mm", "x1_done"))
        x1_out = [sem(f"x1_out{j}") for j in range(2)]
        nat_out = [sem(f"nat_out{j}") for j in range(2)]
        scattered = [sem(f"scattered{j}") for j in range(2)]
        var2, rstd2_done, row_done, x2_mm, x2_done, gate_mm = (
            sem(n) for n in ("var2", "rstd2_done", "row_done", "x2_mm", "x2_done", "gate_mm"))
        gneg_done, gexp_done, mask_done, rank_mm, slot_done, seen_done, wrow_done = (
            sem(n) for n in ("gneg_done", "gexp_done", "mask_done", "rank_mm", "slot_done", "seen_done", "wrow_done"))
        chain1, chain2, rope_q_chain, rope_k_chain = (
            sem(n) for n in ("chain1", "chain2", "rope_q_chain", "rope_k_chain"))
        count_mm, table_done, pads_done, pads_out, trash_out, table_out = (
            sem(n) for n in ("count_mm", "table_done", "pads_done", "pads_out", "trash_out", "table_out"))

        neg_half, vpos, newt = t("neg_half", [P, 1]), t("vpos", [P, 1]), t("newt", [P, 1])
        newton1, newton2 = sem("newton1"), sem("newton2")
        passed_v, passed_p = sem("passed_v"), sem("passed_p")
        CHAIN1 = 4
        CHAIN2 = 3 + GROUPS + 1 + 1 + 12
        block = st.enter_context(nc.Block())

        @block.sync
        def _(sp):
            sp.dma_start(const[:], cf).then_inc(small_in, 16)
            sp.dma_start(ids[:], ci).then_inc(small_in, 16)
            sp.dma_start(pos_in[:], pos).then_inc(small_in, 16)
            sp.dma_start(gate2[:], gates).then_inc(small_in, 16)
            sp.dma_start(bout_b[:], bout).then_inc(small_in, 16)
            sp.dma_start(gate_t[:], gate_w).then_inc(small_in, 16)

            def load(b, j, n):
                need(sp, x1_done, b - 1)
                need(sp, c_lo_done, b - 1)
                sp.dma_start(x_sb[j][:], x[b]).then_inc(x_in[j], 16)
                sp.dma_start(c_raw[j][:], ctx_t[b]).then_inc(c_in[j], 16)
                if isinstance(b, int) and b == 0:
                    for name, w in (("q", wq), ("kv", wkv), ("o", wout)):
                        a, z = parts[name]
                        sp.dma_start(w_raw[:, a:z], w).then_inc(w_in, 16)
                if isinstance(b, int) and b < 2:
                    load_weights(sp, EXPERTS, b)

            def store(b, j, n):
                sp.wait_ge(x1_done, b + 1)
                sp.dma_start(out[b], x1[j][:]).then_inc(x1_out[j], 16)
                sp.wait_ge(wrow_done, b + 1)
                sp.dma_start(rows[bass.ds(b * P + NAT, P), :], row[j][:]).then_inc(nat_out[j], 16)

            rounds(sp, BATCHES, (load, store))
            for j in range(2):
                sp.wait_ge(x1_out[j], 8 * 16)
                sp.wait_ge(nat_out[j], 8 * 16)
            sp.wait_ge(pads_done, 1)
            for s in range(SUB):
                sp.dma_start(out[BATCHES + s], pad_row[:, s, 0:D]).then_inc(trash_out, 16)
            sp.wait_ge(table_done, 1)
            sp.dma_start(table_dram, table_p[0:BLOCKS, :]).then_inc(table_out, 16)
            sp.wait_ge(table_out, 16)
            sp.dma_start(table[:], table_dram.rearrange("(a g) c -> a (g c)", a=1)).then_inc(table_in, 16)
            sp.wait_ge(table_in, 16)
            sp.wait_ge(trash_out, 16 * SUB)

        @block.gpsimd
        def _(pool):
            g = nc.gpsimd
            for j in range(2):
                g.memset(v_one[j][:], 1.0).then_inc(ones_done, 1)
                g.memset(row[j][:], 0.0).then_inc(init_done, 1)
            g.memset(pad_row[:], 0.0).then_inc(init_done, 1)
            g.memset(seen[:], 0.0).then_inc(init_done, 1)
            g.memset(slot_f[:], 0.0).then_inc(init_done, 1)

            def pairs(out_t, cos, sin, chain, done, b):
                o = out_t[:].rearrange("p (a c) -> p a c", c=2)
                c = cos[:].rearrange("p (a c) -> p a c", c=2)
                s = sin[:].rearrange("p (a c) -> p a c", c=2)
                g.tensor_tensor(o[:, :, 0], c[:, :, 0], s[:, :, 1], ALU.subtract).then_inc(chain, 1)
                need(pool, chain, b + 1)
                g.tensor_tensor(o[:, :, 1], s[:, :, 0], c[:, :, 1], ALU.add).then_inc(done, 1)

            def rsqrt(stat, y, chain_sem, done, b):
                ch = Chain(pool, chain_sem, 2 + 3 * NEWTON, b)
                ch.step(g.tensor_scalar(neg_half[:], stat[:, 1:2], EPS, -0.5, ALU.add, ALU.mult))
                ch.sync(passed_p)
                ch.step(g.tensor_scalar(vpos[:], neg_half[:], -2.0, None, ALU.mult))
                ch.sync(passed_p)
                ch.step(g.tensor_scalar(y[:].bitcast(I32), vpos[:].bitcast(I32), -0.5, RSQRT_BITS, ALU.mult, ALU.add))
                ch.sync()
                for k in range(NEWTON):
                    ch.step(g.tensor_tensor(newt[:], y[:], y[:], ALU.mult))
                    ch.sync(passed_p)
                    ch.step(g.tensor_scalar(newt[:], newt[:], neg_half[:, 0:1], 1.5, ALU.mult, ALU.add))
                    ch.sync()
                    last = g.tensor_tensor(y[:], y[:], newt[:], ALU.mult)
                    if k < NEWTON - 1:
                        ch.step(last)
                        ch.sync()
                    else:
                        last.then_inc(done, 1)
                ch.end()

            def project(b, j, n):
                waits_apart(pool, passed_p, (var1, b + 1), (xn_done, b))
                rsqrt(mean1, rstd1, newton1, rstd1_done, b)
                pool.wait_ge(q_rot, b + 1)
                need(pool, qt_mm, b)
                pairs(q_rope, q_cos, q_sin, rope_q_chain, q_rope_done, b)
                pool.wait_ge(k_rot, b + 1)
                need(pool, kt_mm, b)
                pairs(k_rope, k_cos, k_sin, rope_k_chain, k_rope_done, b)

            def attend(b, j, n):
                waits_apart(pool, passed_p, (var2, b + 1), (row_done, b))
                rsqrt(mean2, rstd2, newton2, rstd2_done, b)
                waits_apart(pool, passed_p, (slot_done, b + 1), (wrow_done, b + 1))
                for k in range(TOPK):
                    g.indirect_dma_start(rows, bass.IndirectOffsetOnAxis(slots[j][:, k:k + 1], 0), row[j][:], None)\
                        .then_inc(scattered[j], 16)

            rounds(pool, BATCHES, (project, attend))
            pool.wait_ge(pads_done, 2)
            for e in range(EXPERTS + 1):
                for s in range(SUB):
                    g.indirect_dma_start(rows, bass.IndirectOffsetOnAxis(pad_slots[:, s, e:e + 1], 0),
                                         pad_row[:, s, :], None).then_inc(pads_out, 16)
            pool.wait_ge(pads_out, 16 * SUB * (EXPERTS + 1))
            for j in range(2):
                pool.wait_ge(scattered[j], 16 * TOPK * BATCHES // 2)

        @block.scalar
        def _(act):
            a = nc.scalar
            act.wait_ge(small_in, 16 * 6)
            a.activation(tanh2[:], gate2[:], ACT.Tanh).then_inc(tanh_done, 1)
            act.wait_ge(angles, 7)
            a.activation(sincos[:], turn[:], ACT.Sin).then_inc(sincos_done, 1)
            act.wait_ge(w_in, 48)
            for name in ("q", "kv", "o"):
                lo, hi = parts[name]
                a.activation(w_hi[:, lo:hi], w_raw[:, lo:hi], ACT.Copy).then_inc(w_hi_done, 1)

            def project(b, j, n):
                act.wait_ge(c_in[j], 16 * (n + 1))
                need(act, v_mm, b)
                need(act, c_lo_done, b)
                a.activation(c_hi[:], c_raw[j][:], ACT.Copy).then_inc(c_hi_done, 1)
                act.wait_ge(xt_mm, b + 1)
                need(act, q_mm, b)
                a.activation(xt_hi[:].rearrange("p c n -> p (c n)"), bank[0][:], ACT.Copy).then_inc(xt_hi_done, 1)
                act.wait_ge(v_mm, b + 1)
                need(act, pv_mm, (b - 1) * GROUPS)
                act.wait_ge(ones_done, 2)
                a.activation(v_one[j][:, :, 0:HD], bank[1][:].rearrange("p (h d) -> p h d", h=HEADS), ACT.Copy)\
                    .then_inc(v_done, 1)
                act.wait_ge(qt_mm, b + 1)
                need(act, score_mm, (b - 1) * GROUPS)
                a.activation(q_t[j][:].rearrange("p c n -> p (c n)"), bank[0][:], ACT.Copy).then_inc(qt_done, 1)

            def attend(b, j, n):
                for u in range(GROUPS + 1):
                    if u < GROUPS:
                        act.wait_ge(shifted, b * GROUPS + u + 1)
                        a.activation(soft[u % 2][:], soft[u % 2][:], ACT.Exp, scale=SCALE).then_inc(exp_done, 1)
                    if u >= 1:
                        v = u - 1
                        act.wait_ge(prob_mm, b * GROUPS + v + 1)
                        need(act, pv_mm, b * GROUPS + v - 1)
                        a.activation(soft_t[v % 2][:].rearrange("p c n -> p (c n)"), bank[4 + v % 2][:], ACT.Copy)\
                            .then_inc(prob_done, 1)
                act.wait_ge(at_mm, b + 1)
                need(act, o_mm, b)
                a.activation(at_hi[:].rearrange("p c n -> p (c n)"), bank[4][:], ACT.Copy).then_inc(at_hi_done, 1)
                act.wait_ge(x2_mm, b + 1)
                need(act, gate_mm, b)
                a.activation(x2_t[:].rearrange("p c n -> p (c n)"), bank[4][:], ACT.Copy).then_inc(x2_done, 1)
                act.wait_ge(gneg_done, b + 1)
                a.activation(gexp[:], bank[5][:, 0:EXPERTS], ACT.Exp, bias=gneg[:, 0:1], accum_out=gsum[:, 0:1])\
                    .then_inc(gexp_done, 1)

            rounds(act, BATCHES, (project, attend))

        @block.tensor
        def _(pe):
            def three(dst, lhs, rhs, chunks, lhs_at, rhs_at):
                n = 0
                for c in range(chunks):
                    for l, r in ((0, 0), (0, 1), (1, 0)):
                        last = nc.tensor.matmul(dst, lhs_at(lhs[l], c), rhs_at(rhs[r], c),
                                                start=(n == 0), stop=(n == 3 * chunks - 1))
                        n += 1
                return last

            def four_transposes(dst, src):
                for c in range(DC):
                    last = nc.tensor.transpose(dst[:, c * P:(c + 1) * P], src[:, c * P:(c + 1) * P], ident)
                return last

            xt, ct, at = (xt_hi, xt_lo), (c_hi, c_lo), (at_hi, at_lo)
            pe.wait_ge(small_in, 16 * 6)
            pe.wait_ge(w_hi_done, 3)
            pe.wait_ge(w_lo_done, 3)
            pe.wait_ge(ones_done, 4 // 2)

            def project(b, j, n):
                pe.wait_ge(xn_done, b + 1)
                need(pe, qt_done, b)
                four_transposes(bank[0], xn).then_inc(xt_mm, 1)
                pe.wait_ge(xt_lo_done, b + 1)
                need(pe, kt_done, b)
                three(bank[1][:], xt, q_w, DC, lambda t, c: t[:, c, :], lambda w, c: w[:, c, :]).then_inc(q_mm, 1)
                pe.wait_ge(c_lo_done, b + 1)
                three(bank[0][:], ct, kv_w, CC, lambda t, c: t[:, c, :], lambda w, c: w[:, c, 0:D]).then_inc(k_mm, 1)
                pe.wait_ge(q_rot, b + 1)
                three(bank[1][:], ct, kv_w, CC, lambda t, c: t[:, c, :], lambda w, c: w[:, c, D:2 * D])\
                    .then_inc(v_mm, 1)
                pe.wait_ge(q_rope_done, b + 1)
                pe.wait_ge(k_rot, b + 1)
                four_transposes(bank[0], q_rope).then_inc(qt_mm, 1)
                pe.wait_ge(k_rope_done, b + 1)
                pe.wait_ge(v_done, b + 1)
                four_transposes(bank[1], k_rope).then_inc(kt_mm, 1)

            def attend(b, j, n):
                pe.wait_ge(qt_done, b + 1)
                pe.wait_ge(kt_done, b + 1)
                for u in range(GROUPS + 2):
                    if u < GROUPS:
                        r = 32 * (u % 4)
                        need(pe, shifted, b * GROUPS + u - 1)
                        for c in range(2):
                            ch = 2 * (u // 4) + c
                            last = nc.tensor.matmul(bank[2 + u % 2][:, c * 2 * P:(c + 1) * 2 * P],
                                                    q_t[j][r:r + 32, ch, :],
                                                    k_t[j][r:r + 32, ch].rearrange("p e n -> p (e n)"),
                                                    start=True, stop=True)
                        last.then_inc(score_mm, 1)
                    if 1 <= u <= GROUPS:
                        v = u - 1
                        pe.wait_ge(exp_done, b * GROUPS + v + 1)
                        need(pe, prob_done, b * GROUPS + v - 1)
                        if v == 0:
                            need(pe, x2_done, b)
                            need(pe, slot_done, b)
                        for h in range(4):
                            last = nc.tensor.transpose(bank[4 + v % 2][:, h * P:(h + 1) * P], soft[v % 2][:, h, :],
                                                       ident)
                        last.then_inc(prob_mm, 1)
                    if u >= 2:
                        v = u - 2
                        pe.wait_ge(prob_done, b * GROUPS + v + 1)
                        if v == 0:
                            need(pe, attn_done, b)
                        for i in range(4):
                            h = (2 * (v // 4) + i // 2) * 8 + (v % 4) * 2 + i % 2
                            at_col = (h % 16) * (HD + 1)
                            last = nc.tensor.matmul(bank[6 + h // 16][:, at_col:at_col + HD + 1],
                                                    soft_t[v % 2][:, i, :], v_one[j][:, h, :],
                                                    start=True, stop=True)
                        last.then_inc(pv_mm, 1)
                pe.wait_ge(attn_done, b + 1)
                pe.wait_ge(prob_done, (b + 1) * GROUPS)
                four_transposes(bank[4], attn[:].rearrange("p h d -> p (h d)")).then_inc(at_mm, 1)
                pe.wait_ge(at_lo_done, b + 1)
                three(bank[5][:], at, o_w, DC, lambda t, c: t[:, c, :], lambda w, c: w[:, c, :]).then_inc(o_mm, 1)
                pe.wait_ge(row_done, b + 1)
                four_transposes(bank[4], row[j]).then_inc(x2_mm, 1)
                pe.wait_ge(x2_done, b + 1)
                for c in range(DC):
                    last = nc.tensor.matmul(bank[5][:, 0:EXPERTS], x2_t[:, c, :], gate_t[:, c, :],
                                            start=(c == 0), stop=(c == DC - 1))
                last.then_inc(gate_mm, 1)
                pe.wait_ge(mask_done, b + 1)
                need(pe, seen_done, b)
                nc.tensor.matmul(bank[5][:, 32:32 + EXPERTS], const[:, C_UP:C_UP + P], mask[:], start=True, stop=False)
                nc.tensor.matmul(bank[5][:, 32:32 + EXPERTS], const[:, C_ONE:C_ONE + P], seen[:],
                                 start=False, stop=True).then_inc(rank_mm, 1)

            rounds(pe, BATCHES, (project, attend))
            pe.wait_ge(seen_done, BATCHES)
            nc.tensor.matmul(bank[4][:, 0:EXPERTS], const[:, C_ONE:C_ONE + P], seen[:], start=True, stop=True)\
                .then_inc(count_mm, 1)

        @block.vector
        def _(dve):
            v = nc.vector

            def b16(ap, n):
                return ap

            dve.wait_ge(small_in, 16 * 6)
            for p in range(2):
                o = ang[:, 0, :, 4 * p:4 * p + 4]
                v.tensor_tensor(o, pos_in[:, :, p:p + 1].to_broadcast([P, BATCHES, 4]),
                                const[:, None, C_FREQ:C_FREQ + 4].to_broadcast([P, BATCHES, 4]), ALU.mult)\
                    .then_inc(angles, 1)
            dve.wait_ge(angles, 2)
            v.tensor_scalar(ang[:, 1], ang[:, 0], TWO_PI / 4, None, ALU.add).then_inc(angles, 1)
            dve.wait_ge(angles, 3)
            v.tensor_scalar(turn[:], ang[:], 1 / TWO_PI, ROUND, ALU.mult, ALU.add).then_inc(angles, 1)
            dve.wait_ge(angles, 4)
            v.tensor_scalar(turn[:], turn[:], -ROUND, None, ALU.add).then_inc(angles, 1)
            dve.wait_ge(angles, 5)
            v.scalar_tensor_tensor(out=ang[:], in0=turn[:], scalar=-TWO_PI_HI, in1=ang[:], op0=ALU.mult, op1=ALU.add)\
                .then_inc(angles, 1)
            dve.wait_ge(angles, 6)
            v.scalar_tensor_tensor(out=turn[:], in0=turn[:], scalar=-(TWO_PI - TWO_PI_HI), in1=ang[:],
                                   op0=ALU.mult, op1=ALU.add).then_inc(angles, 1)
            for n, name in enumerate(("q", "kv", "o")):
                lo, hi = parts[name]
                dve.wait_ge(w_hi_done, n + 1)
                v.tensor_tensor(w_lo[:, lo:hi], w_raw[:, lo:hi], w_hi[:, lo:hi].bitcast(F32), ALU.subtract)\
                    .then_inc(w_lo_done, 1)
            dve.wait_ge(init_done, 5)
            dve.wait_ge(tanh_done, 1)
            for j in range(2):
                for s in range(SHARED):
                    v.tensor_copy(row[j][:, ROW_W + EXPERTS + s:ROW_W + EXPERTS + s + 1], tanh2[:, 1:2]).then_inc(init_v, 1)
            dve.wait_ge(init_v, 2 * SHARED)
            dve.wait_ge(sincos_done, 1)

            def rotate(src, cos_o, sin_o, b, chain, done):
                s4 = src.rearrange("p (h a c) -> p h a c", h=HEADS, c=2)

                def table4(k):
                    one = sincos[:, k, bass.ds(b, 1), :] if not isinstance(b, int) else sincos[:, k, b:b + 1, :]
                    return one.rearrange("p o a -> p (o a)")[:, None, :, None].to_broadcast([P, HEADS, ANG, 2])

                chain.step(v.tensor_tensor(cos_o[:].rearrange("p (h a c) -> p h a c", h=HEADS, c=2), s4, table4(1),
                                           ALU.mult))
                chain.sync()
                v.tensor_tensor(sin_o[:].rearrange("p (h a c) -> p h a c", h=HEADS, c=2), s4, table4(0), ALU.mult)\
                    .then_inc(done, 1)

            def project(b, j, n):
                ch = Chain(dve, chain1, CHAIN1, b)
                dve.wait_ge(x_in[j], 16 * (n + 1))
                ch.step(v.bn_stats(stats[:], x_sb[j][:]))
                ch.sync(passed_v, (xn_done, b))
                v.bn_aggr(mean1[:], stats[:]).then_inc(var1, 1)
                dve.wait_ge(c_hi_done, b + 1)
                need(dve, v_mm, b)
                v.tensor_tensor(c_lo[:], c_raw[j][:], c_hi[:].bitcast(F32), ALU.subtract).then_inc(c_lo_done, 1)
                dve.wait_ge(var1, b + 1)
                dve.wait_ge(rstd1_done, b + 1)
                need(dve, xt_mm, b)
                v.tensor_scalar(xn[:], x_sb[j][:], mean1[:, 0:1], rstd1[:, 0:1], ALU.subtract, ALU.mult)\
                    .then_inc(xn_done, 1)
                dve.wait_ge(xt_hi_done, b + 1)
                need(dve, q_mm, b)
                v.tensor_tensor(xt_lo[:].rearrange("p c n -> p (c n)"), bank[0][:],
                                xt_hi[:].rearrange("p c n -> p (c n)").bitcast(F32), ALU.subtract).then_inc(xt_lo_done, 1)
                dve.wait_ge(q_mm, b + 1)
                need(dve, q_rope_done, b)
                rotate(bank[1][:], q_cos, q_sin, b, ch, q_rot)
                dve.wait_ge(k_mm, b + 1)
                need(dve, k_rope_done, b)
                rotate(bank[0][:], k_cos, k_sin, b, ch, k_rot)
                dve.wait_ge(kt_mm, b + 1)
                need(dve, score_mm, (b - 1) * GROUPS)
                k4 = bank[1][:].rearrange("p (c n) -> p c n", c=DC)
                ch.step(v.tensor_scalar(k_t[j][:, :, 0, :], k4, const[:, C_EVEN:C_EVEN + 1], None, ALU.mult))
                ch.sync()
                v.tensor_scalar(k_t[j][:, :, 1, :], k4, const[:, C_ODD:C_ODD + 1], None, ALU.mult).then_inc(kt_done, 1)
                ch.end()

            def attend(b, j, n):
                ch = Chain(dve, chain2, CHAIN2, b)
                for u in range(GROUPS):
                    dve.wait_ge(score_mm, b * GROUPS + u + 1)
                    s3 = bank[2 + u % 2][:].rearrange("p (h n) -> p h n", h=4)
                    ch.step(v.tensor_reduce(smax[u % 2][:], s3, AX.X, ALU.max))
                    ch.sync()
                    need(dve, prob_mm, b * GROUPS + u - 1)
                    v.tensor_tensor(soft[u % 2][:], s3, smax[u % 2][:, :, None].to_broadcast([P, 4, P]), ALU.subtract)\
                        .then_inc(shifted, 1)
                dve.wait_ge(pv_mm, (b + 1) * GROUPS)
                pv = [bank[6 + k][:, 0:16 * (HD + 1)].rearrange("p (h d) -> p h d", h=16) for k in range(2)]
                for k in range(2):
                    ch.step(v.reciprocal(rsum[:, 16 * k:16 * k + 16], pv[k][:, :, HD]))
                ch.sync()
                need(dve, at_mm, b)
                ch.step(v.tensor_tensor(attn[:, 0:16, :], pv[0][:, :, 0:HD],
                                        rsum[:, 0:16, None].to_broadcast([P, 16, HD]), ALU.mult))
                ch.sync()
                v.tensor_tensor(attn[:, 16:32, :], pv[1][:, :, 0:HD],
                                rsum[:, 16:32, None].to_broadcast([P, 16, HD]), ALU.mult).then_inc(attn_done, 1)
                dve.wait_ge(at_hi_done, b + 1)
                need(dve, o_mm, b)
                v.tensor_tensor(at_lo[:].rearrange("p c n -> p (c n)"), bank[4][:],
                                at_hi[:].rearrange("p c n -> p (c n)").bitcast(F32), ALU.subtract).then_inc(at_lo_done, 1)
                dve.wait_ge(o_mm, b + 1)
                ch.step(v.tensor_tensor(proj[:], bank[5][:], bout_b[:], ALU.add))
                ch.sync()
                need(dve, x1_out[j], 16 * n)
                v.scalar_tensor_tensor(out=x1[j][:], in0=proj[:], scalar=tanh2[:, 0:1], in1=x_sb[j][:],
                                       op0=ALU.mult, op1=ALU.add).then_inc(x1_done, 1)
                dve.wait_ge(x1_done, b + 1)
                ch.step(v.bn_stats(stats2[:], x1[j][:]))
                ch.sync(passed_v)
                v.bn_aggr(mean2[:], stats2[:]).then_inc(var2, 1)
                dve.wait_ge(var2, b + 1)
                dve.wait_ge(rstd2_done, b + 1)
                need(dve, scattered[j], 16 * TOPK * n)
                need(dve, nat_out[j], 16 * n)
                v.tensor_scalar(row[j][:, 0:D], x1[j][:], mean2[:, 0:1], rstd2[:, 0:1], ALU.subtract, ALU.mult)\
                    .then_inc(row_done, 1)
                dve.wait_ge(gate_mm, b + 1)
                ch.step(v.tensor_reduce(gmax[:], bank[5][:, 0:EXPERTS], AX.X, ALU.max))
                ch.sync()
                v.tensor_scalar(gneg[:], gmax[:], -1.0, None, ALU.mult).then_inc(gneg_done, 1)
                dve.wait_ge(gexp_done, b + 1)
                ch.step(v.reciprocal(grec[:], gsum[:]))
                ch.sync()
                ch.step(v.tensor_scalar(prob[:], gexp[:], grec[:, 0:1], None, ALU.mult))
                ch.sync(passed_v)
                ch.step(v.max(top[:], prob[:]))
                ch.sync(passed_v)
                ch.step(v.max_index(top_i[:], top[:], prob[:]))
                ch.sync()
                ch.step(v.tensor_copy(top_f[:], top_i[:]))
                ch.sync()
                ch.step(v.tensor_tensor(pick[:], const[:, None, C_IOTA:C_IOTA + EXPERTS].to_broadcast([P, TOPK, EXPERTS]),
                                        top_f[:, 0:TOPK, None].to_broadcast([P, TOPK, EXPERTS]), ALU.is_equal))
                ch.sync()
                v.tensor_reduce(mask[:], pick[:].rearrange("p k e -> p e k"), AX.X, ALU.add).then_inc(mask_done, 1)
                dve.wait_ge(mask_done, b + 1)
                ch.step(v.tensor_copy(row[j][:, ROW_ID:ROW_ID + 1].bitcast(I32), ids[:, bass.ds(K_ID + b, 1)]))
                ch.sync()
                v.scalar_tensor_tensor(out=row[j][:, ROW_W:ROW_W + EXPERTS], in0=prob[:], scalar=tanh2[:, 1:2],
                                       in1=mask[:], op0=ALU.mult, op1=ALU.mult).then_inc(wrow_done, 1)
                dve.wait_ge(rank_mm, b + 1)
                ch.step(v.tensor_tensor(slot_e[:], bank[5][:, 32:32 + EXPERTS], const[:, C_CAP:C_CAP + EXPERTS], ALU.add))
                ch.sync()
                ch.step(v.tensor_tensor(pick_slot[:], pick[:], slot_e[:, None, :].to_broadcast([P, TOPK, EXPERTS]),
                                        ALU.mult))
                ch.sync()
                ch.step(v.tensor_reduce(slot_f[:, 0:TOPK], pick_slot[:], AX.X, ALU.add))
                ch.sync()
                v.tensor_copy(slots[j][:], slot_f[:]).then_inc(slot_done, 1)
                v.tensor_tensor(seen[:], seen[:], mask[:], ALU.add).then_inc(seen_done, 1)
                dve.wait_ge(seen_done, b + 1)
                ch.step(v.tensor_copy(top_f[:, 0:1], top_f[:, 1:2]))
                ch.end()

            rounds(dve, BATCHES, (project, attend))

            last = [BATCHES * CHAIN2]

            def link(ins):
                last[0] += 1
                ins.then_inc(chain2, 1)
                dve.wait_ge(chain2, last[0])

            dve.wait_ge(count_mm, 1)
            link(v.tensor_copy(cnt[:], bank[4][:, 0:EXPERTS]))
            link(v.tensor_tensor(over[:], cnt[:, :, None].to_broadcast([P, EXPERTS, 8]),
                                 const[:, None, C_THR:C_THR + 8].to_broadcast([P, EXPERTS, 8]), ALU.is_gt))
            link(v.tensor_reduce(nblk[:], over[:], AX.X, ALU.add))
            link(v.tensor_tensor(ends3[:], nblk[:, None, :].to_broadcast([P, EXPERTS, EXPERTS]),
                                 const[:, C_TRI:C_TRI + 256].rearrange("p (a c) -> p a c", a=EXPERTS), ALU.mult))
            link(v.tensor_reduce(ends[:], ends3[:], AX.X, ALU.add))
            link(v.tensor_scalar(past[:], ends[:], const[:, C_G:C_G + 1], None, ALU.is_le))
            link(v.tensor_tensor(past_end[:], past[:], ends[:], ALU.mult))
            link(v.tensor_reduce(tb[:, 0:1], past[:], AX.X, ALU.add))
            link(v.tensor_reduce(tb[:, 1:2], past_end[:], AX.X, ALU.max))
            link(v.tensor_tensor(tb[:, 2:3], const[:, C_G:C_G + 1], tb[:, 1:2], ALU.subtract))
            link(v.tensor_scalar(tb[:, 3:4], tb[:, 0:1], float(EXPERTS), float(BLOCK), ALU.is_lt, ALU.mult))
            link(v.tensor_tensor(tb[:, 4:5], tb[:, 2:3], tb[:, 3:4], ALU.mult))
            link(v.scalar_tensor_tensor(out=tb[:, 5:6], in0=tb[:, 0:1], scalar=float(CAP), in1=tb[:, 4:5],
                                        op0=ALU.mult, op1=ALU.add))
            link(v.tensor_scalar(tb[:, 6:7], tb[:, 0:1], float(EXPERTS - 1), None, ALU.min))
            for k, (src, shared) in enumerate(((6, C_SE), (5, C_SROW))):
                link(v.tensor_tensor(tb[:, src:src + 1], tb[:, src:src + 1], const[:, C_RM:C_RM + 1], ALU.mult))
                link(v.tensor_tensor(tb[:, 7:8], const[:, shared:shared + 1], const[:, C_SM:C_SM + 1], ALU.mult))
                ins = v.tensor_tensor(table_p[:, k:k + 1], tb[:, src:src + 1], tb[:, 7:8], ALU.add)
                if k == 0:
                    link(ins)
                else:
                    ins.then_inc(table_done, 1)
            for s in range(SUB):
                link(v.tensor_copy(pad_row[:, s, ROW_ID:ROW_ID + 1].bitcast(I32), ids[:, K_PAD + s:K_PAD + s + 1]))
            v.tensor_copy(top_f[:, 0:1], top_f[:, 1:2]).then_inc(pads_done, 1)
            for s in range(SUB):
                link(v.tensor_tensor(pad_f[:, s, 0:EXPERTS], cnt[:], const[:, C_CAP:C_CAP + EXPERTS], ALU.add))
                link(v.tensor_scalar(pad_f[:, s, EXPERTS:EXPERTS + 1], const[:, C_P:C_P + 1], float(EXPERTS * CAP + s * P),
                                     None, ALU.add))
                link(v.tensor_scalar(pad_f[:, s, 0:EXPERTS], pad_f[:, s, 0:EXPERTS], const[:, C_P:C_P + 1],
                                     float(s * P), ALU.add, ALU.add))
            v.tensor_copy(pad_slots[:], pad_f[:]).then_inc(pads_done, 1)
            dve.wait_ge(pads_done, 2)


def phase_b(nc, sb, sem, bank, ident, table, table_in, load_weights, w1_raw, w2_raw, w1_in, w2_in, out, rows, w1, w2):
    with ExitStack() as st:
        def two(name, shape, dt=F32):
            return [sb(st, f"{name}{j}", shape, dt) for j in range(2)]

        w1_hi, w1_lo = two("w1_hi", [P, DC, 2 * WIDTH], F32R), two("w1_lo", [P, DC, 2 * WIDTH], F32R)
        w2_hi, w2_lo = two("w2_hi", [P, 3, D], F32R), two("w2_lo", [P, 3, D], F32R)
        xr = two("xr", [P, SUB, ROW])
        xe_hi, xe_lo = two("xe_hi", [P, DC, BLOCK], F32R), two("xe_lo", [P, DC, BLOCK], F32R)
        silu = two("silu", [P, 3, BLOCK])
        act_f = two("act_f", [P, 3, BLOCK])
        act_hi, act_lo = two("act_hi", [P, 3, BLOCK], F32R), two("act_lo", [P, 3, BLOCK], F32R)
        y = two("y", [P, SUB, D])
        row_w, row_id = two("row_w", [P, SUB, 1]), two("row_id", [P, SUB, 1], I32)

        xr_in = [sem(f"xr_in{j}") for j in range(2)]
        w1_hi_done, w1_lo_done, w2_hi_done, w2_lo_done = (
            sem(n) for n in ("w1_hi_done", "w1_lo_done", "w2_hi_done", "w2_lo_done"))
        xe_mm, xe_hi_done, xe_lo_done = sem("xe_mm"), sem("xe_hi_done"), sem("xe_lo_done")
        h_mm, silu_done, act_done, act_hi_done, act_lo_done = (
            sem(n) for n in ("h_mm", "silu_done", "act_done", "act_hi_done", "act_lo_done"))
        y_mm, y_done = sem("y_mm"), sem("y_done")
        weight_done, meta_done = sem("weight_done"), sem("meta_done")
        added = [sem(f"added{j}") for j in range(2)]
        out_rows = out.rearrange("b p n -> (b p) n")
        passed, passed_sp = sem("passed"), sem("passed_sp")
        block = st.enter_context(nc.Block())

        @block.sync
        def _(sp):
            def load(g, j, n):
                e = sp.value_load(table[0:1, bass.ds(g * 2, 1)], min_val=0, max_val=EXPERTS + SHARED - 1)
                first = sp.value_load(table[0:1, bass.ds(g * 2 + 1, 1)], min_val=0, max_val=ROWS - BLOCK)
                if not (isinstance(g, int) and g < 2):
                    for done, per in ((w1_hi_done, 1), (w1_lo_done, 1), (w2_hi_done, 2), (w2_lo_done, 2)):
                        waits_apart(sp, passed_sp, (done, (g - 1) * per))
                    load_weights(sp, e, j)
                    waits_apart(sp, passed_sp, (xe_mm, g - 1), (weight_done, g - 1), (meta_done, g - 1))
                sp.dma_start(xr[j][:], rows[bass.ds(first, BLOCK), :].rearrange("(s p) n -> p s n", p=P))\
                    .then_inc(xr_in[j], 16)

            rounds(sp, BLOCKS, (load,))

        @block.scalar
        def _(act):
            a = nc.scalar

            def prepare(g, j, n):
                act.wait_ge(w1_in[j], 16 * (n + 1))
                need(act, h_mm, 3 * (g - 1))
                a.activation(w1_hi[j][:], w1_raw[j][:], ACT.Copy).then_inc(w1_hi_done, 1)
                act.wait_ge(xe_mm, g + 1)
                for s in range(SUB):
                    a.activation(xe_hi[j][:, :, s * P:(s + 1) * P],
                                 bank[s][:].rearrange("p (c n) -> p c n", c=DC), ACT.Copy).then_inc(xe_hi_done, 1)

            def inner(g, j, n):
                for c, (_, m) in enumerate(WC):
                    act.wait_ge(h_mm, 3 * g + c + 1)
                    need(act, act_done, 3 * (g - 2) + c + 1)
                    a.activation(silu[j][0:m, c, :], bank[2 + c][0:m, 0:BLOCK], ACT.Silu).then_inc(silu_done, 1)
                    act.wait_ge(act_done, 3 * g + c + 1)
                    need(act, y_mm, SUB * (g - 1))
                    a.activation(act_hi[j][0:m, c, :], act_f[j][0:m, c, :], ACT.Copy).then_inc(act_hi_done, 1)

            rounds(act, BLOCKS, (prepare, inner))

        @block.gpsimd
        def _(pool):
            g_ = nc.gpsimd

            def nothing(g, j, n):
                pass

            def inner(g, j, n):
                waits_apart(pool, passed, (w2_in[j], 32 * (n + 1)), (y_mm, SUB * (g - 1)))
                g_.tensor_copy(w2_hi[j][:, 0:2, :], w2_raw[j][:, 0:2, :]).then_inc(w2_hi_done, 1)
                g_.tensor_copy(w2_hi[j][0:96, 2, :], w2_raw[j][0:96, 2, :]).then_inc(w2_hi_done, 1)
                pool.wait_ge(w2_hi_done, 2 * (g + 1))
                g_.tensor_tensor(w2_lo[j][:, 0:2, :], w2_raw[j][:, 0:2, :], w2_hi[j][:, 0:2, :].bitcast(F32),
                                 ALU.subtract).then_inc(w2_lo_done, 1)
                g_.tensor_tensor(w2_lo[j][0:96, 2, :], w2_raw[j][0:96, 2, :], w2_hi[j][0:96, 2, :].bitcast(F32),
                                 ALU.subtract).then_inc(w2_lo_done, 1)

            def add(g, j, n):
                if isinstance(g, int):
                    if g >= 1:
                        pool.wait_ge(added[1 - j], 16 * SUB * (n + j))
                else:
                    pool.wait_ge(added[1 - j], 16 * SUB * (n + j))
                for s in range(SUB):
                    waits_apart(pool, passed, (y_done, SUB * g + s + 1))
                    g_.indirect_dma_start(out_rows,
                                          bass.IndirectOffsetOnAxis(row_id[j][:, s, :].bitcast(U32), 0),
                                          y[j][:, s, :], None, compute_op=ALU.add).then_inc(added[j], 16)

            rounds(pool, BLOCKS, (nothing, inner, add))
            for j in range(2):
                pool.wait_ge(added[j], 16 * SUB * BLOCKS // 2)

        @block.tensor
        def _(pe):
            def prepare(g, j, n):
                pe.wait_ge(xr_in[j], 16 * (n + 1))
                need(pe, xe_lo_done, SUB * g)
                for s in range(SUB):
                    for c in range(DC):
                        last = nc.tensor.transpose(bank[s][:, c * P:(c + 1) * P], xr[j][:, s, c * P:(c + 1) * P], ident)
                last.then_inc(xe_mm, 1)

            def inner(g, j, n):
                pe.wait_ge(w1_lo_done, g + 1)
                pe.wait_ge(w1_hi_done, g + 1)
                pe.wait_ge(xe_lo_done, SUB * (g + 1))
                for c, (at, m) in enumerate(WC):
                    need(pe, act_done, 3 * (g - 1) + c + 1)
                    for half in range(2):
                        k = 0
                        for d in range(DC):
                            col = half * WIDTH + at
                            for w, xx in ((w1_hi, xe_hi), (w1_hi, xe_lo), (w1_lo, xe_hi)):
                                last = nc.tensor.matmul(bank[2 + c][0:m, half * BLOCK:(half + 1) * BLOCK],
                                                        w[j][:, d, col:col + m], xx[j][:, d, :],
                                                        start=(k == 0), stop=(k == 3 * DC - 1))
                                k += 1
                    last.then_inc(h_mm, 1)

            def outer(g, j, n):
                pe.wait_ge(act_lo_done, 3 * (g + 1))
                pe.wait_ge(w2_lo_done, 2 * (g + 1))
                for s in range(SUB):
                    need(pe, y_done, SUB * (g - 1) + s + 1)
                    k = 0
                    for c, (_, m) in enumerate(WC):
                        for l, w in ((act_hi, w2_hi), (act_hi, w2_lo), (act_lo, w2_hi)):
                            last = nc.tensor.matmul(bank[5 + s][:], l[j][0:m, c, s * P:(s + 1) * P], w[j][0:m, c, :],
                                                    start=(k == 0), stop=(k == 8))
                            k += 1
                    last.then_inc(y_mm, 1)

            rounds(pe, BLOCKS, (prepare, inner, outer))

        @block.vector
        def _(dve):
            v = nc.vector

            def prepare(g, j, n):
                dve.wait_ge(w1_hi_done, g + 1)
                need(dve, h_mm, 3 * (g - 1))
                v.tensor_tensor(w1_lo[j][:], w1_raw[j][:], w1_hi[j][:].bitcast(F32), ALU.subtract)\
                    .then_inc(w1_lo_done, 1)
                for s in range(SUB):
                    dve.wait_ge(xe_hi_done, SUB * g + s + 1)
                    v.tensor_tensor(xe_lo[j][:, :, s * P:(s + 1) * P], bank[s][:].rearrange("p (c n) -> p c n", c=DC),
                                    xe_hi[j][:, :, s * P:(s + 1) * P].bitcast(F32), ALU.subtract).then_inc(xe_lo_done, 1)

            def inner(g, j, n):
                e = dve.value_load(table[0:1, bass.ds(g * 2, 1)], min_val=0, max_val=EXPERTS + SHARED - 1)
                dve.wait_ge(xr_in[j], 16 * (n + 1))
                if not (isinstance(g, int) and g < 2):
                    dve.wait_ge(added[j], 16 * SUB * n)
                v.tensor_copy(row_w[j][:], xr[j][:, :, bass.ds(e + ROW_W, 1)]).then_inc(weight_done, 1)
                v.tensor_copy(row_id[j][:], xr[j][:, :, ROW_ID:ROW_ID + 1].bitcast(I32)).then_inc(meta_done, 1)
                for c, (_, m) in enumerate(WC):
                    dve.wait_ge(silu_done, 3 * g + c + 1)
                    need(dve, act_lo_done, 3 * (g - 2) + c + 1)
                    v.tensor_tensor(act_f[j][0:m, c, :], silu[j][0:m, c, :], bank[2 + c][0:m, BLOCK:2 * BLOCK], ALU.mult)\
                        .then_inc(act_done, 1)
                    dve.wait_ge(act_hi_done, 3 * g + c + 1)
                    need(dve, y_mm, SUB * (g - 1))
                    v.tensor_tensor(act_lo[j][0:m, c, :], act_f[j][0:m, c, :], act_hi[j][0:m, c, :].bitcast(F32),
                                    ALU.subtract).then_inc(act_lo_done, 1)

            def outer(g, j, n):
                dve.wait_ge(weight_done, g + 1)
                for s in range(SUB):
                    dve.wait_ge(y_mm, SUB * g + s + 1)
                    v.tensor_scalar(y[j][:, s, :], bank[5 + s][:], row_w[j][:, s, :], None, ALU.mult)\
                        .then_inc(y_done, 1)

            rounds(dve, BLOCKS, (prepare, inner, outer))


def kernel(**inputs):
    import numpy as np
    import concourse.bacc as bacc
    from concourse.bass_utils import run_bass_kernel_spmd

    def arr(name):
        return np.asarray(inputs[name])

    def chunks(w):
        return np.ascontiguousarray(w.reshape(w.shape[0] // P, P, w.shape[1]).transpose(1, 0, 2))

    w1 = arr("L0_ffn_w1")
    s1 = arr("L0_ffn_shared_w1").reshape(2, SHARED, WIDTH, D).transpose(1, 0, 2, 3).reshape(SHARED, 2 * WIDTH, D)
    w1 = np.concatenate([w1, s1]).transpose(0, 2, 1)
    w1 = np.ascontiguousarray(w1.reshape(-1, DC, P, 2 * WIDTH).transpose(0, 2, 1, 3))
    w2 = arr("L0_ffn_w2")
    s2 = arr("L0_ffn_shared_w2").reshape(D, SHARED, WIDTH).transpose(1, 0, 2)
    w2t = np.concatenate([w2, s2]).transpose(0, 2, 1)
    w2p = np.zeros((w2t.shape[0], 3 * P, D), w2t.dtype)
    w2p[:, :WIDTH] = w2t
    cf, ci = constants()
    arrays = {
        "x": arr("x"),
        "ctx_t": np.ascontiguousarray(arr("ctx_1024").transpose(0, 2, 1).reshape(BATCHES, CC, P, P).transpose(0, 2, 1, 3)),
        "pos": np.ascontiguousarray(arr("fside_BxSx2_0").transpose(1, 0, 2)),
        "wq": chunks(arr("L0_xattn_Wq")).reshape(P, -1),
        "wkv": chunks(arr("L0_xattn_Wkv")).reshape(P, -1),
        "wout": chunks(arr("L0_xattn_Wout")).reshape(P, -1),
        "bout": np.ascontiguousarray(np.broadcast_to(arr("L0_xattn_bout"), (P, D))),
        "gates": np.ascontiguousarray(np.broadcast_to(np.concatenate([arr("g_xattn"), arr("g_ffn")]), (P, 2))),
        "gate_w": chunks(arr("L0_ffn_gate_w").T),
        "w1": w1,
        "w2": w2p.reshape(-1, 3, P, D),
        "cf": cf,
        "ci": ci,
    }
    nc = bacc.Bacc("TRN2", target_bir_lowering=False, num_devices=1)
    args = [nc.dram_tensor(f"in_{n}", a.shape, mybir.dt.from_np(a.dtype), kind="ExternalInput").ap()
            for n, a in arrays.items()]
    out = nc.dram_tensor("out", (BATCHES + SUB, P, D), F32, kind="ExternalOutput").ap()
    build(nc, *args, out)
    r = run_bass_kernel_spmd(nc, [{f"in_{n}": a for n, a in arrays.items()}], core_ids=[0])
    return r.results[0]["out"][:BATCHES]
```

```python
from contextlib import ExitStack

import concourse.bass as bass
from concourse import mybir

F32 = mybir.dt.float32
F32R = mybir.dt.float32r
I32 = mybir.dt.int32
U32 = mybir.dt.uint32
ALU = mybir.AluOpType
ACT = mybir.ActivationFunctionType
AX = mybir.AxisListType

P = 128
BATCHES = 16
D = 512
DC = D // P
CTX = 256
CC = CTX // P
HEADS = 32
HD = D // HEADS
ANG = 8
GROUPS = 8
TOKENS = BATCHES * P
EXPERTS = 16
TOPK = 6
WIDTH = 352
WC = [(0, 128), (128, 128), (256, 96)]
SHARED = 2
BLOCK = 256
SUB = BLOCK // P
CAP = TOKENS + BLOCK
NAT = EXPERTS * CAP + BLOCK
ROWS = NAT + TOKENS
SHARED_BLOCKS = SHARED * TOKENS // BLOCK
ROUTED_BLOCKS = TOKENS * TOPK // BLOCK + EXPERTS
BLOCKS = SHARED_BLOCKS + ROUTED_BLOCKS
ROW_W = D
ROW_ID = D + EXPERTS + SHARED
ROW = ROW_ID + 2
EPS = 1e-5
SCALE = HD ** -0.5
TWO_PI = 6.283185307179586
TWO_PI_HI = 6.28125
NEWTON = 3
RSQRT_BITS = 1597463007.0
ROUND = 12582912.0

C_ID, C_UP, C_ONE = 0, 128, 256
C_IOTA = 384
C_CAP = C_IOTA + 16
C_THR = C_CAP + 16
C_TRI = C_THR + 8
C_EVEN = C_TRI + 256
C_ODD = C_EVEN + 1
C_G = C_ODD + 1
C_SE = C_G + 1
C_SROW = C_SE + 1
C_SM = C_SROW + 1
C_RM = C_SM + 1
C_P = C_RM + 1
C_FREQ = C_P + 1
C_N = C_FREQ + 8
K_ID, K_PAD, K_N = 0, BATCHES, BATCHES + SUB


def constants():
    import numpy as np
    c = np.zeros((P, C_N), np.float32)
    p = np.arange(P)
    c[:, C_ID:C_ID + P] = np.eye(P)
    c[:, C_UP:C_UP + P] = p[:, None] < p[None, :]
    c[:, C_ONE:C_ONE + P] = 1
    c[:, C_IOTA:C_IOTA + 16] = np.arange(16)
    c[:, C_CAP:C_CAP + 16] = np.arange(16) * CAP
    c[:, C_THR:C_THR + 8] = np.arange(8) * BLOCK
    c[:, C_TRI:C_TRI + 256] = (np.arange(16)[None, :] <= np.arange(16)[:, None]).reshape(1, 256)
    c[:, C_EVEN] = (p // HD) % 2 == 0
    c[:, C_ODD] = (p // HD) % 2 == 1
    c[:, C_G] = p - SHARED_BLOCKS
    c[:, C_SE] = EXPERTS + p // (TOKENS // BLOCK)
    c[:, C_SROW] = NAT + (p % (TOKENS // BLOCK)) * BLOCK
    c[:, C_SM] = p < SHARED_BLOCKS
    c[:, C_RM] = p >= SHARED_BLOCKS
    c[:, C_P] = p
    c[:, C_FREQ:C_FREQ + 8] = np.tile(np.float32(10000.0) ** (-np.arange(4, dtype=np.float32) / 4), 2)
    k = np.zeros((P, K_N), np.int32)
    k[:, K_ID:K_ID + BATCHES] = np.arange(BATCHES)[None, :] * P + p[:, None]
    k[:, K_PAD:K_PAD + SUB] = TOKENS + np.arange(SUB)[None, :] * P + p[:, None]
    return c, k


def need(eng, sem, value):
    if isinstance(value, int) and value <= 0:
        return
    eng.wait_ge(sem, value)


def waits_apart(eng, passed, *waits):
    for sem, v in waits:
        need(eng, sem, v)
    if any(not isinstance(v, int) for _, v in waits):
        eng.sem_inc(passed, 1)


class Chain:

    def __init__(self, eng, sem, per, block):
        self.eng, self.sem, self.per, self.base, self.k = eng, sem, per, block * per, 0

    def step(self, instruction):
        self.k += 1
        instruction.then_inc(self.sem, 1)

    def sync(self, passed=None, *others):
        if passed:
            waits_apart(self.eng, passed, (self.sem, self.base + self.k), *others)
        else:
            need(self.eng, self.sem, self.base + self.k)

    def end(self):
        assert self.k == self.per, (self.k, self.per)


def rounds(eng, blocks, depth, peeled, one_round):
    def place(r, k):
        return (r - k, (r - k) % 2, (r - k) // 2)

    for r in list(range(peeled)):
        one_round(lambda k: place(r, k) if 0 <= r - k < blocks else None)
    with eng.Fori(peeled // 2, blocks // 2) as i:
        for r in range(2):
            one_round(lambda k: (2 * i + (r - k), (r - k) % 2, i + (r - k) // 2))
    for r in range(blocks, blocks + depth - 1):
        one_round(lambda k: place(r, k) if 0 <= r - k < blocks else None)


def build(nc, x, ctx_t, pos, wq, wkv, wout, bout, gates, gate_w, w1, w2, cf, ci, out):
    rows = nc.dram_tensor("expert_rows", (ROWS, ROW), F32, kind="Internal").ap()
    table_dram = nc.dram_tensor("block_table", (BLOCKS, 2), I32, kind="Internal").ap()

    with ExitStack() as whole:
        def sb(stack, name, shape, dt=F32):
            return stack.enter_context(nc.sbuf_tensor(name, shape, dt))

        def sem(name):
            return whole.enter_context(nc.semaphore(name))

        bank = [whole.enter_context(nc.psum_tensor(f"bank{i}", [P, 512], F32)) for i in range(8)]
        w1_raw = [sb(whole, f"w1_raw{j}", [P, DC, 2 * WIDTH]) for j in range(2)]
        w2_raw = [sb(whole, f"w2_raw{j}", [P, 3, D]) for j in range(2)]
        const = sb(whole, "const", [P, C_N])
        table = sb(whole, "table", [1, 2 * BLOCKS], I32)
        ident = const[:, C_ID:C_ID + P]

        w1_in = [sem(f"w1_in{j}") for j in range(2)]
        w2_in = [sem(f"w2_in{j}") for j in range(2)]
        table_in = sem("table_in")

        def load_w1(sp, e, j):
            sp.dma_start(w1_raw[j][:], w1[e]).then_inc(w1_in[j], 16)

        def load_w2(sp, e, j):
            sp.dma_start(w2_raw[j][:, 0:2, :], w2[e, 0:2].rearrange("c p n -> p c n")).then_inc(w2_in[j], 16)
            sp.dma_start(w2_raw[j][0:96, 2, :], w2[e, 2, 0:96]).then_inc(w2_in[j], 16)

        phase_a(nc, sb, sem, bank, const, ident, table, table_in, load_w1, load_w2,
                x, ctx_t, pos, wq, wkv, wout, bout, gates, gate_w, cf, ci, out, rows, table_dram)
        phase_b(nc, sb, sem, bank, ident, table, table_in, load_w1, load_w2,
                w1_raw, w2_raw, w1_in, w2_in, out, rows, w1, w2)


def phase_a(nc, sb, sem, bank, const, ident, table, table_in, load_w1, load_w2,
            x, ctx_t, pos, wq, wkv, wout, bout, gates, gate_w, cf, ci, out, rows, table_dram):
    with ExitStack() as st:
        def t(name, shape, dt=F32):
            return sb(st, name, shape, dt)

        def two(name, shape, dt=F32):
            return [sb(st, f"{name}{j}", shape, dt) for j in range(2)]

        w_raw = t("w_raw", [P, 6144])
        w_hi = t("w_hi", [P, 6144], F32R)
        w_lo = t("w_lo", [P, 6144], F32R)
        parts = {"q": (0, 2048), "kv": (2048, 4096), "o": (4096, 6144)}
        q_w = [w[:, 0:2048].rearrange("p (c n) -> p c n", c=DC) for w in (w_hi, w_lo)]
        kv_w = [w[:, 2048:4096].rearrange("p (c n) -> p c n", c=CC) for w in (w_hi, w_lo)]
        o_w = [w[:, 4096:6144].rearrange("p (c n) -> p c n", c=DC) for w in (w_hi, w_lo)]
        gate_t = t("gate_t", [P, DC, EXPERTS])
        bout_b = t("bout_b", [P, D])
        gate2 = t("gate2", [P, 2])
        tanh2 = t("tanh2", [P, 2])
        ids = t("ids", [P, K_N], I32)
        pos_in = t("pos_in", [P, BATCHES, 2])
        ang = t("ang", [P, 2, BATCHES, ANG])
        turn = t("turn", [P, 2, BATCHES, ANG])
        sincos = t("sincos", [P, 2, BATCHES, ANG])
        pad_row = t("pad_row", [P, SUB, ROW])
        x_sb = two("x_sb", [P, D])
        x_res = two("x_res", [P, D])
        c_raw = two("c_raw", [P, CC, P])
        c_hi = t("c_hi", [P, CC, P], F32R)
        c_lo = t("c_lo", [P, CC, P], F32R)
        stats = t("stats", [P, 6])
        mean1 = t("mean1", [P, 2])
        rstd1 = t("rstd1", [P, 1])
        xn = t("xn", [P, D])
        xt_hi = t("xt_hi", [P, DC, P], F32R)
        xt_lo = t("xt_lo", [P, DC, P], F32R)
        q_cos, q_sin = t("q_cos", [P, D]), t("q_sin", [P, D])
        k_cos, k_sin = t("k_cos", [P, D]), t("k_sin", [P, D])
        q_rope, k_rope = t("q_rope", [P, D]), t("k_rope", [P, D])
        v_one = two("v_one", [P, HEADS, HD + 1])
        q_t = two("q_t", [P, DC, P])
        k_t = two("k_t", [P, DC, 2, P])
        smax = two("smax", [P, 4])
        soft = two("soft", [P, 4, P])
        soft_t = two("soft_t", [P, 4, P])
        rsum = t("rsum", [P, HEADS])
        attn = t("attn", [P, HEADS, HD])
        at_hi = t("at_hi", [P, DC, P], F32R)
        at_lo = t("at_lo", [P, DC, P], F32R)
        proj = t("proj", [P, D])
        x1 = two("x1", [P, D])
        stats2 = t("stats2", [P, 6])
        mean2 = t("mean2", [P, 2])
        rstd2 = t("rstd2", [P, 1])
        row = two("row", [P, ROW])
        x2_t = t("x2_t", [P, DC, P])
        gmax, gneg, gsum, grec = (t(n, [P, 1]) for n in ("gmax", "gneg", "gsum", "grec"))
        gexp, prob = t("gexp", [P, EXPERTS]), t("prob", [P, EXPERTS])
        top, top_i, top_f = t("top", [P, 8]), t("top_i", [P, 8], U32), t("top_f", [P, 8])
        pick = t("pick", [P, TOPK, EXPERTS])
        pick_slot = t("pick_slot", [P, TOPK, EXPERTS])
        mask = t("mask", [P, EXPERTS])
        seen = t("seen", [P, EXPERTS])
        slot_e = t("slot_e", [P, EXPERTS])
        slot_f = t("slot_f", [P, 8])
        slots = two("slots", [P, 8], U32)
        cnt = t("cnt", [P, EXPERTS])
        over = t("over", [P, EXPERTS, 8])
        nblk = t("nblk", [P, EXPERTS])
        ends3 = t("ends3", [P, EXPERTS, EXPERTS])
        ends = t("ends", [P, EXPERTS])
        past = t("past", [P, EXPERTS])
        past_end = t("past_end", [P, EXPERTS])
        tb = t("tb", [P, 8])
        table_p = t("table_p", [P, 2], I32)
        pad_f = t("pad_f", [P, SUB, EXPERTS + 1])
        pad_slots = t("pad_slots", [P, SUB, EXPERTS + 1], U32)

        small_in = sem("small_in")
        w_in = {name: sem(f"w_in_{name}") for name in parts}
        w_hi_done, w_lo_done = sem("w_hi_done"), sem("w_lo_done")
        init_done, ones_done = sem("init_done"), sem("ones_done")
        angles, sincos_done, tanh_done, init_v = sem("angles"), sem("sincos_done"), sem("tanh_done"), sem("init_v")
        x_in = [sem(f"x_in{j}") for j in range(2)]
        c_in = [sem(f"c_in{j}") for j in range(2)]
        var1, rstd1_done, xn_done = sem("var1"), sem("rstd1_done"), sem("xn_done")
        c_hi_done, c_lo_done = sem("c_hi_done"), sem("c_lo_done")
        xt_mm, xt_hi_done, xt_lo_done = sem("xt_mm"), sem("xt_hi_done"), sem("xt_lo_done")
        q_mm, k_mm, v_mm = sem("q_mm"), sem("k_mm"), sem("v_mm")
        q_rot, k_rot, q_rope_done, k_rope_done = sem("q_rot"), sem("k_rot"), sem("q_rope_done"), sem("k_rope_done")
        v_done, qt_mm, qt_done, kt_mm, kt_done = (sem(n) for n in ("v_done", "qt_mm", "qt_done", "kt_mm", "kt_done"))
        score_mm, shifted, exp_done, prob_mm, prob_done, pv_mm = (
            sem(n) for n in ("score_mm", "shifted", "exp_done", "prob_mm", "prob_done", "pv_mm"))
        attn_done, at_mm, at_hi_done, at_lo_done, o_mm, x1_done = (
            sem(n) for n in ("attn_done", "at_mm", "at_hi_done", "at_lo_done", "o_mm", "x1_done"))
        x1_out = [sem(f"x1_out{j}") for j in range(2)]
        nat_out = [sem(f"nat_out{j}") for j in range(2)]
        scattered = [sem(f"scattered{j}") for j in range(2)]
        var2, rstd2_done, row_done, x2_mm, x2_done, gate_mm = (
            sem(n) for n in ("var2", "rstd2_done", "row_done", "x2_mm", "x2_done", "gate_mm"))
        gneg_done, gexp_done, mask_done, rank_mm, slot_done, seen_done, wrow_done = (
            sem(n) for n in ("gneg_done", "gexp_done", "mask_done", "rank_mm", "slot_done", "seen_done", "wrow_done"))
        chain_tail, chain_place, table_chain, rope_q_chain, rope_k_chain = (
            sem(n) for n in ("chain_tail", "chain_place", "table_chain", "rope_q_chain", "rope_k_chain"))
        stats1_done, smax_done = sem("stats1_done"), sem("smax_done")
        res_in = [sem(f"res_in{j}") for j in range(2)]
        count_mm, table_done, pads_done, pads_out, trash_out, table_out = (
            sem(n) for n in ("count_mm", "table_done", "pads_done", "pads_out", "trash_out", "table_out"))

        neg_half, vpos, newt = t("neg_half", [P, 1]), t("vpos", [P, 1]), t("newt", [P, 1])
        newton1, newton2 = sem("newton1"), sem("newton2")
        passed_v, passed_p = sem("passed_v"), sem("passed_p")
        TAIL_STEPS = 12
        block = st.enter_context(nc.Block())

        LOAD, PROJECT, ATTEND, TAIL, PLACE = range(5)
        DEPTH, PEELED = 5, 6

        def earlier(at, u, back):
            return (at(ATTEND), u - back) if u >= back else (at(TAIL), u - back + GROUPS)

        @block.sync
        def _(sp):
            sp.dma_start(const[:], cf).then_inc(small_in, 16)
            sp.dma_start(ids[:], ci).then_inc(small_in, 16)
            sp.dma_start(pos_in[:], pos).then_inc(small_in, 16)
            sp.dma_start(gate2[:], gates).then_inc(small_in, 16)
            sp.dma_start(bout_b[:], bout).then_inc(small_in, 16)
            sp.dma_start(gate_t[:], gate_w).then_inc(small_in, 16)

            def one_round(at):
                if at(LOAD):
                    b, j, n = at(LOAD)
                    need(sp, xn_done, b - 1)
                    need(sp, c_lo_done, b - 1)
                    sp.dma_start(x_sb[j][:], x[b]).then_inc(x_in[j], 16)
                    sp.dma_start(c_raw[j][:], ctx_t[b]).then_inc(c_in[j], 16)
                    if isinstance(b, int) and b == 0:
                        for name, w in (("q", wq), ("kv", wkv), ("o", wout)):
                            a, z = parts[name]
                            sp.dma_start(w_raw[:, a:z], w).then_inc(w_in[name], 16)
                    if isinstance(b, int) and b < 2:
                        load_w1(sp, EXPERTS, b)
                        load_w2(sp, EXPERTS, b)
                if at(TAIL):
                    b, j, n = at(TAIL)
                    need(sp, x1_done, b - 1)
                    sp.dma_start(x_res[j][:], x[b]).then_inc(res_in[j], 16)
                    sp.wait_ge(x1_done, b + 1)
                    sp.dma_start(out[b], x1[j][:]).then_inc(x1_out[j], 16)
                    sp.wait_ge(wrow_done, 2 * (b + 1))
                    sp.dma_start(rows[bass.ds(b * P + NAT, P), :], row[j][:]).then_inc(nat_out[j], 16)

            rounds(sp, BATCHES, DEPTH, PEELED, one_round)
            for j in range(2):
                sp.wait_ge(x1_out[j], 8 * 16)
                sp.wait_ge(nat_out[j], 8 * 16)
            sp.wait_ge(pads_done, 1)
            for s in range(SUB):
                sp.dma_start(out[BATCHES + s], pad_row[:, s, 0:D]).then_inc(trash_out, 16)
            sp.wait_ge(table_done, 1)
            sp.dma_start(table_dram, table_p[0:BLOCKS, :]).then_inc(table_out, 16)
            sp.wait_ge(table_out, 16)
            sp.dma_start(table[:], table_dram.rearrange("(a g) c -> a (g c)", a=1)).then_inc(table_in, 16)
            sp.wait_ge(table_in, 16)
            sp.wait_ge(trash_out, 16 * SUB)

        @block.gpsimd
        def _(pool):
            g = nc.gpsimd
            for j in range(2):
                g.memset(v_one[j][:], 1.0).then_inc(ones_done, 1)
                g.memset(row[j][:], 0.0).then_inc(init_done, 1)
            g.memset(pad_row[:], 0.0).then_inc(init_done, 1)
            g.memset(seen[:], 0.0).then_inc(init_done, 1)
            g.memset(slot_f[:], 0.0).then_inc(init_done, 1)

            def pairs(out_t, cos, sin, chain, done, b):
                o = out_t[:].rearrange("p (a c) -> p a c", c=2)
                c = cos[:].rearrange("p (a c) -> p a c", c=2)
                s = sin[:].rearrange("p (a c) -> p a c", c=2)
                g.tensor_tensor(o[:, :, 0], c[:, :, 0], s[:, :, 1], ALU.subtract).then_inc(chain, 1)
                need(pool, chain, b + 1)
                g.tensor_tensor(o[:, :, 1], s[:, :, 0], c[:, :, 1], ALU.add).then_inc(done, 1)

            def rsqrt(stat, y, chain_sem, done, b):
                ch = Chain(pool, chain_sem, 2 + 3 * NEWTON, b)
                ch.step(g.tensor_scalar(neg_half[:], stat[:, 1:2], EPS, -0.5, ALU.add, ALU.mult))
                ch.sync(passed_p)
                ch.step(g.tensor_scalar(vpos[:], neg_half[:], -2.0, None, ALU.mult))
                ch.sync(passed_p)
                ch.step(g.tensor_scalar(y[:].bitcast(I32), vpos[:].bitcast(I32), -0.5, RSQRT_BITS, ALU.mult, ALU.add))
                ch.sync()
                for k in range(NEWTON):
                    ch.step(g.tensor_tensor(newt[:], y[:], y[:], ALU.mult))
                    ch.sync(passed_p)
                    ch.step(g.tensor_scalar(newt[:], newt[:], neg_half[:, 0:1], 1.5, ALU.mult, ALU.add))
                    ch.sync()
                    last = g.tensor_tensor(y[:], y[:], newt[:], ALU.mult)
                    if k < NEWTON - 1:
                        ch.step(last)
                        ch.sync()
                    else:
                        last.then_inc(done, 1)
                ch.end()

            def scatter(b, j, n, ks):
                waits_apart(pool, passed_p, (slot_done, b + 1))
                for k in ks:
                    g.indirect_dma_start(rows, bass.IndirectOffsetOnAxis(slots[j][:, k:k + 1], 0), row[j][:], None)\
                        .then_inc(scattered[j], 16)

            def one_round(at):
                if at(PROJECT):
                    b, j, n = at(PROJECT)
                    pool.wait_ge(q_rot, 2 * (b + 1))
                    need(pool, qt_mm, b)
                    pairs(q_rope, q_cos, q_sin, rope_q_chain, q_rope_done, b)
                    pool.wait_ge(k_rot, 2 * (b + 1))
                    need(pool, kt_mm, b)
                    pairs(k_rope, k_cos, k_sin, rope_k_chain, k_rope_done, b)
                if at(TAIL):
                    b, j, n = at(TAIL)
                    waits_apart(pool, passed_p, (var2, b + 1), (row_done, b))
                    rsqrt(mean2, rstd2, newton2, rstd2_done, b)
                if at(PLACE):
                    scatter(*at(PLACE), range(0, TOPK // 2))
                if at(LOAD):
                    b, j, n = at(LOAD)
                    waits_apart(pool, passed_p, (var1, b + 1), (xn_done, b))
                    rsqrt(mean1, rstd1, newton1, rstd1_done, b)
                if at(PLACE):
                    scatter(*at(PLACE), range(TOPK // 2, TOPK))

            rounds(pool, BATCHES, DEPTH, PEELED, one_round)
            pool.wait_ge(pads_done, 2)
            for e in range(EXPERTS + 1):
                for s in range(SUB):
                    g.indirect_dma_start(rows, bass.IndirectOffsetOnAxis(pad_slots[:, s, e:e + 1], 0),
                                         pad_row[:, s, :], None).then_inc(pads_out, 16)
            pool.wait_ge(pads_out, 16 * SUB * (EXPERTS + 1))
            for j in range(2):
                pool.wait_ge(scattered[j], 16 * TOPK * BATCHES // 2)

        @block.scalar
        def _(act):
            a = nc.scalar
            act.wait_ge(small_in, 16 * 6)
            a.activation(tanh2[:], gate2[:], ACT.Tanh).then_inc(tanh_done, 1)
            act.wait_ge(angles, 7)
            a.activation(sincos[:], turn[:], ACT.Sin).then_inc(sincos_done, 1)
            for name in ("q", "kv", "o"):
                lo, hi = parts[name]
                act.wait_ge(w_in[name], 16)
                a.activation(w_hi[:, lo:hi], w_raw[:, lo:hi], ACT.Copy).then_inc(w_hi_done, 1)

            def attend(at, u):
                if at(ATTEND):
                    b = at(ATTEND)[0]
                    act.wait_ge(shifted, b * GROUPS + u + 1)
                    a.activation(soft[u % 2][:], soft[u % 2][:], ACT.Exp, scale=SCALE).then_inc(exp_done, 1)
                of, v = earlier(at, u, 1)
                if of:
                    b = of[0]
                    act.wait_ge(prob_mm, b * GROUPS + v + 1)
                    need(act, pv_mm, b * GROUPS + v - 1)
                    a.activation(soft_t[v % 2][:].rearrange("p c n -> p (c n)"), bank[4 + v % 2][:], ACT.Copy)\
                        .then_inc(prob_done, 1)

            def one_round(at):
                for u in range(GROUPS):
                    attend(at, u)
                    if at(PROJECT):
                        b, j, n = at(PROJECT)
                        if u == 0:
                            act.wait_ge(xt_mm, b + 1)
                            need(act, q_mm, b)
                            a.activation(xt_hi[:].rearrange("p c n -> p (c n)"), bank[0][:], ACT.Copy)\
                                .then_inc(xt_hi_done, 1)
                        if u == 3:
                            act.wait_ge(v_mm, b + 1)
                            need(act, pv_mm, (b - 1) * GROUPS)
                            act.wait_ge(ones_done, 2)
                            a.activation(v_one[j][:, :, 0:HD], bank[0][:].rearrange("p (h d) -> p h d", h=HEADS),
                                         ACT.Copy).then_inc(v_done, 1)
                        if u == 4:
                            act.wait_ge(qt_mm, b + 1)
                            need(act, score_mm, (b - 1) * GROUPS)
                            a.activation(q_t[j][:].rearrange("p c n -> p (c n)"), bank[0][:], ACT.Copy)\
                                .then_inc(qt_done, 1)
                        if u == 5:
                            act.wait_ge(kt_mm, b + 1)
                            need(act, score_mm, (b - 1) * GROUPS)
                            k4 = bank[0][:].rearrange("p (c n) -> p c n", c=DC)
                            a.activation(k_t[j][:, :, 0, :], k4, ACT.Copy, scale=const[:, C_EVEN:C_EVEN + 1])\
                                .then_inc(kt_done, 1)
                            a.activation(k_t[j][:, :, 1, :], k4, ACT.Copy, scale=const[:, C_ODD:C_ODD + 1])\
                                .then_inc(kt_done, 1)
                    if at(LOAD) and u == 5:
                        b, j, n = at(LOAD)
                        act.wait_ge(c_in[j], 16 * (n + 1))
                        need(act, v_mm, b)
                        need(act, c_lo_done, b)
                        a.activation(c_hi[:], c_raw[j][:], ACT.Copy).then_inc(c_hi_done, 1)
                    if at(TAIL):
                        b, j, n = at(TAIL)
                        if u == 2:
                            act.wait_ge(at_mm, b + 1)
                            need(act, o_mm, b)
                            a.activation(at_hi[:].rearrange("p c n -> p (c n)"), bank[1][:], ACT.Copy)\
                                .then_inc(at_hi_done, 1)
                        if u == 5:
                            act.wait_ge(x2_mm, b + 1)
                            need(act, gate_mm, b)
                            a.activation(x2_t[:].rearrange("p c n -> p (c n)"), bank[1][:], ACT.Copy)\
                                .then_inc(x2_done, 1)
                        if u == 6:
                            act.wait_ge(gneg_done, b + 1)
                            a.activation(gexp[:], bank[1][:, 0:EXPERTS], ACT.Exp, bias=gneg[:, 0:1],
                                         accum_out=gsum[:, 0:1]).then_inc(gexp_done, 1)

            rounds(act, BATCHES, DEPTH, PEELED, one_round)

        @block.tensor
        def _(pe):
            def three(dst, lhs, rhs, chunks, lhs_at, rhs_at):
                n = 0
                for c in range(chunks):
                    for l, r in ((0, 0), (0, 1), (1, 0)):
                        last = nc.tensor.matmul(dst, lhs_at(lhs[l], c), rhs_at(rhs[r], c),
                                                start=(n == 0), stop=(n == 3 * chunks - 1))
                        n += 1
                return last

            def four_transposes(dst, src):
                for c in range(DC):
                    last = nc.tensor.transpose(dst[:, c * P:(c + 1) * P], src[:, c * P:(c + 1) * P], ident)
                return last

            xt, ct, at_parts = (xt_hi, xt_lo), (c_hi, c_lo), (at_hi, at_lo)
            pe.wait_ge(small_in, 16 * 6)
            pe.wait_ge(ones_done, 4 // 2)

            def scores(at, u):
                if at(ATTEND):
                    b, j, n = at(ATTEND)
                    if u == 0:
                        pe.wait_ge(qt_done, b + 1)
                        pe.wait_ge(kt_done, 2 * (b + 1))
                    r = 32 * (u % 4)
                    need(pe, shifted, b * GROUPS + u - 1)
                    for c in range(2):
                        ch = 2 * (u // 4) + c
                        last = nc.tensor.matmul(bank[2 + u % 2][:, c * 2 * P:(c + 1) * 2 * P],
                                                q_t[j][r:r + 32, ch, :],
                                                k_t[j][r:r + 32, ch].rearrange("p e n -> p (e n)"),
                                                start=True, stop=True)
                    last.then_inc(score_mm, 1)

            def probs(at, u):
                of, v = earlier(at, u, 1)
                if of:
                    b = of[0]
                    pe.wait_ge(exp_done, b * GROUPS + v + 1)
                    need(pe, prob_done, b * GROUPS + v - 1)
                    for h in range(4):
                        last = nc.tensor.transpose(bank[4 + v % 2][:, h * P:(h + 1) * P], soft[v % 2][:, h, :], ident)
                    last.then_inc(prob_mm, 1)

            def values(at, u):
                of, v = earlier(at, u, 2)
                if of:
                    b, j, n = of
                    pe.wait_ge(prob_done, b * GROUPS + v + 1)
                    if v == 0:
                        need(pe, attn_done, b)
                    for i in range(4):
                        h = (2 * (v // 4) + i // 2) * 8 + (v % 4) * 2 + i % 2
                        col = (h % 16) * (HD + 1)
                        last = nc.tensor.matmul(bank[6 + h // 16][:, col:col + HD + 1],
                                                soft_t[v % 2][:, i, :], v_one[j][:, h, :], start=True, stop=True)
                    last.then_inc(pv_mm, 1)

            def project(u, b, j, n):
                if u == 0:
                    pe.wait_ge(xn_done, b + 1)
                    need(pe, kt_done, 2 * b)
                    four_transposes(bank[0], xn).then_inc(xt_mm, 1)
                if u == 1:
                    if isinstance(b, int) and b == 0:
                        pe.wait_ge(w_lo_done, 1)
                    pe.wait_ge(xt_lo_done, b + 1)
                    three(bank[0][:], xt, q_w, DC, lambda t, c: t[:, c, :], lambda w, c: w[:, c, :]).then_inc(q_mm, 1)
                if u == 2:
                    if isinstance(b, int) and b == 0:
                        pe.wait_ge(w_lo_done, 2)
                    pe.wait_ge(c_lo_done, b + 1)
                    pe.wait_ge(q_rot, 2 * (b + 1))
                    three(bank[0][:], ct, kv_w, CC, lambda t, c: t[:, c, :], lambda w, c: w[:, c, 0:D])\
                        .then_inc(k_mm, 1)
                if u == 3:
                    pe.wait_ge(k_rot, 2 * (b + 1))
                    three(bank[0][:], ct, kv_w, CC, lambda t, c: t[:, c, :], lambda w, c: w[:, c, D:2 * D])\
                        .then_inc(v_mm, 1)
                if u == 4:
                    pe.wait_ge(q_rope_done, b + 1)
                    pe.wait_ge(v_done, b + 1)
                    four_transposes(bank[0], q_rope).then_inc(qt_mm, 1)
                if u == 5:
                    pe.wait_ge(k_rope_done, b + 1)
                    pe.wait_ge(qt_done, b + 1)
                    four_transposes(bank[0], k_rope).then_inc(kt_mm, 1)

            def tail(u, b, j, n):
                if u == 2:
                    pe.wait_ge(attn_done, b + 1)
                    need(pe, slot_done, b)
                    four_transposes(bank[1], attn[:].rearrange("p h d -> p (h d)")).then_inc(at_mm, 1)
                if u == 3:
                    if isinstance(b, int) and b == 0:
                        pe.wait_ge(w_lo_done, 3)
                    pe.wait_ge(at_lo_done, b + 1)
                    three(bank[1][:], at_parts, o_w, DC, lambda t, c: t[:, c, :], lambda w, c: w[:, c, :])\
                        .then_inc(o_mm, 1)
                if u == 5:
                    pe.wait_ge(row_done, b + 1)
                    four_transposes(bank[1], row[j]).then_inc(x2_mm, 1)
                if u == 6:
                    pe.wait_ge(x2_done, b + 1)
                    for c in range(DC):
                        last = nc.tensor.matmul(bank[1][:, 0:EXPERTS], x2_t[:, c, :], gate_t[:, c, :],
                                                start=(c == 0), stop=(c == DC - 1))
                    last.then_inc(gate_mm, 1)

            def one_round(at):
                for u in range(GROUPS):
                    scores(at, u)
                    if at(PROJECT):
                        project(u, *at(PROJECT))
                    probs(at, u)
                    if at(TAIL):
                        tail(u, *at(TAIL))
                    values(at, u)
                    if at(PLACE) and u == 1:
                        b = at(PLACE)[0]
                        pe.wait_ge(mask_done, b + 1)
                        need(pe, seen_done, b)
                        nc.tensor.matmul(bank[1][:, 32:32 + EXPERTS], const[:, C_UP:C_UP + P], mask[:],
                                         start=True, stop=False)
                        nc.tensor.matmul(bank[1][:, 32:32 + EXPERTS], const[:, C_ONE:C_ONE + P], seen[:],
                                         start=False, stop=True).then_inc(rank_mm, 1)

            rounds(pe, BATCHES, DEPTH, PEELED, one_round)
            pe.wait_ge(seen_done, BATCHES)
            nc.tensor.matmul(bank[1][:, 0:EXPERTS], const[:, C_ONE:C_ONE + P], seen[:], start=True, stop=True)\
                .then_inc(count_mm, 1)

        @block.vector
        def _(dve):
            v = nc.vector

            def b16(ap, n):
                return ap

            dve.wait_ge(small_in, 16 * 6)
            for p in range(2):
                o = ang[:, 0, :, 4 * p:4 * p + 4]
                v.tensor_tensor(o, pos_in[:, :, p:p + 1].to_broadcast([P, BATCHES, 4]),
                                const[:, None, C_FREQ:C_FREQ + 4].to_broadcast([P, BATCHES, 4]), ALU.mult)\
                    .then_inc(angles, 1)
            dve.wait_ge(angles, 2)
            v.tensor_scalar(ang[:, 1], ang[:, 0], TWO_PI / 4, None, ALU.add).then_inc(angles, 1)
            dve.wait_ge(angles, 3)
            v.tensor_scalar(turn[:], ang[:], 1 / TWO_PI, ROUND, ALU.mult, ALU.add).then_inc(angles, 1)
            dve.wait_ge(angles, 4)
            v.tensor_scalar(turn[:], turn[:], -ROUND, None, ALU.add).then_inc(angles, 1)
            dve.wait_ge(angles, 5)
            v.scalar_tensor_tensor(out=ang[:], in0=turn[:], scalar=-TWO_PI_HI, in1=ang[:], op0=ALU.mult, op1=ALU.add)\
                .then_inc(angles, 1)
            dve.wait_ge(angles, 6)
            v.scalar_tensor_tensor(out=turn[:], in0=turn[:], scalar=-(TWO_PI - TWO_PI_HI), in1=ang[:],
                                   op0=ALU.mult, op1=ALU.add).then_inc(angles, 1)
            for n, name in enumerate(("q", "kv", "o")):
                lo, hi = parts[name]
                dve.wait_ge(w_hi_done, n + 1)
                v.tensor_tensor(w_lo[:, lo:hi], w_raw[:, lo:hi], w_hi[:, lo:hi].bitcast(F32), ALU.subtract)\
                    .then_inc(w_lo_done, 1)
            dve.wait_ge(init_done, 5)
            dve.wait_ge(tanh_done, 1)
            for j in range(2):
                for s in range(SHARED):
                    v.tensor_copy(row[j][:, ROW_W + EXPERTS + s:ROW_W + EXPERTS + s + 1], tanh2[:, 1:2]).then_inc(init_v, 1)
            dve.wait_ge(init_v, 2 * SHARED)
            dve.wait_ge(sincos_done, 1)

            def rotate(src, cos_o, sin_o, b, done):
                s4 = src.rearrange("p (h a c) -> p h a c", h=HEADS, c=2)
                for k, dst in ((1, cos_o), (0, sin_o)):
                    one = sincos[:, k, bass.ds(b, 1), :].rearrange("p o a -> p (o a)")
                    last = v.tensor_tensor(dst[:].rearrange("p (h a c) -> p h a c", h=HEADS, c=2), s4,
                                           one[:, None, :, None].to_broadcast([P, HEADS, ANG, 2]), ALU.mult)
                    last.then_inc(done, 1)

            def load(u, b, j, n):
                if u == 5:
                    dve.wait_ge(x_in[j], 16 * (n + 1))
                    v.bn_stats(stats[:], x_sb[j][:]).then_inc(stats1_done, 1)
                    waits_apart(dve, passed_v, (stats1_done, b + 1), (xn_done, b))
                    v.bn_aggr(mean1[:], stats[:]).then_inc(var1, 1)
                if u == 6:
                    dve.wait_ge(c_hi_done, b + 1)
                    need(dve, v_mm, b)
                    v.tensor_tensor(c_lo[:], c_raw[j][:], c_hi[:].bitcast(F32), ALU.subtract).then_inc(c_lo_done, 1)
                if u == 7:
                    dve.wait_ge(var1, b + 1)
                    dve.wait_ge(rstd1_done, b + 1)
                    need(dve, xt_mm, b)
                    v.tensor_scalar(xn[:], x_sb[j][:], mean1[:, 0:1], rstd1[:, 0:1], ALU.subtract, ALU.mult)\
                        .then_inc(xn_done, 1)

            def project(u, b, j, n):
                if u == 0:
                    dve.wait_ge(xt_hi_done, b + 1)
                    need(dve, q_mm, b)
                    v.tensor_tensor(xt_lo[:].rearrange("p c n -> p (c n)"), bank[0][:],
                                    xt_hi[:].rearrange("p c n -> p (c n)").bitcast(F32), ALU.subtract)\
                        .then_inc(xt_lo_done, 1)
                if u == 1:
                    dve.wait_ge(q_mm, b + 1)
                    need(dve, q_rope_done, b)
                    rotate(bank[0][:], q_cos, q_sin, b, q_rot)
                if u == 2:
                    dve.wait_ge(k_mm, b + 1)
                    need(dve, k_rope_done, b)
                    rotate(bank[0][:], k_cos, k_sin, b, k_rot)

            def attend(u, b, j, n):
                dve.wait_ge(score_mm, b * GROUPS + u + 1)
                s3 = bank[2 + u % 2][:].rearrange("p (h n) -> p h n", h=4)
                v.tensor_reduce(smax[u % 2][:], s3, AX.X, ALU.max).then_inc(smax_done, 1)
                dve.wait_ge(smax_done, b * GROUPS + u + 1)
                need(dve, prob_mm, b * GROUPS + u - 1)
                v.tensor_tensor(soft[u % 2][:], s3, smax[u % 2][:, :, None].to_broadcast([P, 4, P]), ALU.subtract)\
                    .then_inc(shifted, 1)

            def tail(u, b, j, n, ch):
                if u == 1:
                    dve.wait_ge(pv_mm, (b + 1) * GROUPS)
                    pv = [bank[6 + k][:, 0:16 * (HD + 1)].rearrange("p (h d) -> p h d", h=16) for k in range(2)]
                    for k in range(2):
                        ch.step(v.reciprocal(rsum[:, 16 * k:16 * k + 16], pv[k][:, :, HD]))
                    ch.sync()
                    need(dve, at_mm, b)
                    ch.step(v.tensor_tensor(attn[:, 0:16, :], pv[0][:, :, 0:HD],
                                            rsum[:, 0:16, None].to_broadcast([P, 16, HD]), ALU.mult))
                    ch.sync()
                    v.tensor_tensor(attn[:, 16:32, :], pv[1][:, :, 0:HD],
                                    rsum[:, 16:32, None].to_broadcast([P, 16, HD]), ALU.mult).then_inc(attn_done, 1)
                if u == 2:
                    dve.wait_ge(at_hi_done, b + 1)
                    need(dve, o_mm, b)
                    v.tensor_tensor(at_lo[:].rearrange("p c n -> p (c n)"), bank[1][:],
                                    at_hi[:].rearrange("p c n -> p (c n)").bitcast(F32), ALU.subtract)\
                        .then_inc(at_lo_done, 1)
                if u == 3:
                    dve.wait_ge(o_mm, b + 1)
                    ch.step(v.tensor_tensor(proj[:], bank[1][:], bout_b[:], ALU.add))
                    ch.sync()
                    dve.wait_ge(res_in[j], 16 * (n + 1))
                    need(dve, x1_out[j], 16 * n)
                    v.scalar_tensor_tensor(out=x1[j][:], in0=proj[:], scalar=tanh2[:, 0:1], in1=x_res[j][:],
                                           op0=ALU.mult, op1=ALU.add).then_inc(x1_done, 1)
                    dve.wait_ge(x1_done, b + 1)
                    ch.step(v.bn_stats(stats2[:], x1[j][:]))
                    ch.sync(passed_v)
                    v.bn_aggr(mean2[:], stats2[:]).then_inc(var2, 1)
                if u == 5:
                    dve.wait_ge(var2, b + 1)
                    dve.wait_ge(rstd2_done, b + 1)
                    need(dve, scattered[j], 16 * TOPK * n)
                    need(dve, nat_out[j], 16 * n)
                    v.tensor_scalar(row[j][:, 0:D], x1[j][:], mean2[:, 0:1], rstd2[:, 0:1], ALU.subtract, ALU.mult)\
                        .then_inc(row_done, 1)
                if u == 6:
                    dve.wait_ge(gate_mm, b + 1)
                    ch.step(v.tensor_reduce(gmax[:], bank[1][:, 0:EXPERTS], AX.X, ALU.max))
                    ch.sync()
                    v.tensor_scalar(gneg[:], gmax[:], -1.0, None, ALU.mult).then_inc(gneg_done, 1)
                if u == 7:
                    dve.wait_ge(gexp_done, b + 1)
                    ch.step(v.reciprocal(grec[:], gsum[:]))
                    ch.sync()
                    ch.step(v.tensor_scalar(prob[:], gexp[:], grec[:, 0:1], None, ALU.mult))
                    ch.sync(passed_v)
                    ch.step(v.max(top[:], prob[:]))
                    ch.sync(passed_v)
                    ch.step(v.max_index(top_i[:], top[:], prob[:]))
                    ch.sync()
                    ch.step(v.tensor_copy(top_f[:], top_i[:]))
                    ch.sync()
                    ch.step(v.tensor_tensor(pick[:],
                                            const[:, None, C_IOTA:C_IOTA + EXPERTS].to_broadcast([P, TOPK, EXPERTS]),
                                            top_f[:, 0:TOPK, None].to_broadcast([P, TOPK, EXPERTS]), ALU.is_equal))
                    ch.sync()
                    v.tensor_reduce(mask[:], pick[:].rearrange("p k e -> p e k"), AX.X, ALU.add).then_inc(mask_done, 1)
                    v.tensor_copy(row[j][:, ROW_ID:ROW_ID + 1].bitcast(I32), ids[:, bass.ds(K_ID + b, 1)])\
                        .then_inc(wrow_done, 1)
                    dve.wait_ge(mask_done, b + 1)
                    v.scalar_tensor_tensor(out=row[j][:, ROW_W:ROW_W + EXPERTS], in0=prob[:], scalar=tanh2[:, 1:2],
                                           in1=mask[:], op0=ALU.mult, op1=ALU.mult).then_inc(wrow_done, 1)
                    ch.end()

            def place(b, j, n):
                ch = Chain(dve, chain_place, 3, b)
                dve.wait_ge(rank_mm, b + 1)
                ch.step(v.tensor_tensor(slot_e[:], bank[1][:, 32:32 + EXPERTS], const[:, C_CAP:C_CAP + EXPERTS],
                                        ALU.add))
                v.tensor_tensor(seen[:], seen[:], mask[:], ALU.add).then_inc(seen_done, 1)
                ch.sync()
                ch.step(v.tensor_tensor(pick_slot[:], pick[:], slot_e[:, None, :].to_broadcast([P, TOPK, EXPERTS]),
                                        ALU.mult))
                ch.sync()
                ch.step(v.tensor_reduce(slot_f[:, 0:TOPK], pick_slot[:], AX.X, ALU.add))
                ch.sync()
                need(dve, scattered[j], 16 * TOPK * n)
                v.tensor_copy(slots[j][:], slot_f[:]).then_inc(slot_done, 1)
                ch.end()

            def one_round(at):
                ch = Chain(dve, chain_tail, TAIL_STEPS, at(TAIL)[0]) if at(TAIL) else None
                for u in range(GROUPS):
                    if at(ATTEND):
                        attend(u, *at(ATTEND))
                    if at(PROJECT):
                        project(u, *at(PROJECT))
                    if at(PLACE) and u == 1:
                        place(*at(PLACE))
                    if at(TAIL):
                        tail(u, *at(TAIL), ch)
                    if at(LOAD):
                        load(u, *at(LOAD))

            rounds(dve, BATCHES, DEPTH, PEELED, one_round)

            last = [0]

            def link(ins):
                last[0] += 1
                ins.then_inc(table_chain, 1)
                dve.wait_ge(table_chain, last[0])

            dve.wait_ge(count_mm, 1)
            link(v.tensor_copy(cnt[:], bank[1][:, 0:EXPERTS]))
            link(v.tensor_tensor(over[:], cnt[:, :, None].to_broadcast([P, EXPERTS, 8]),
                                 const[:, None, C_THR:C_THR + 8].to_broadcast([P, EXPERTS, 8]), ALU.is_gt))
            link(v.tensor_reduce(nblk[:], over[:], AX.X, ALU.add))
            link(v.tensor_tensor(ends3[:], nblk[:, None, :].to_broadcast([P, EXPERTS, EXPERTS]),
                                 const[:, C_TRI:C_TRI + 256].rearrange("p (a c) -> p a c", a=EXPERTS), ALU.mult))
            link(v.tensor_reduce(ends[:], ends3[:], AX.X, ALU.add))
            link(v.tensor_scalar(past[:], ends[:], const[:, C_G:C_G + 1], None, ALU.is_le))
            link(v.tensor_tensor(past_end[:], past[:], ends[:], ALU.mult))
            link(v.tensor_reduce(tb[:, 0:1], past[:], AX.X, ALU.add))
            link(v.tensor_reduce(tb[:, 1:2], past_end[:], AX.X, ALU.max))
            link(v.tensor_tensor(tb[:, 2:3], const[:, C_G:C_G + 1], tb[:, 1:2], ALU.subtract))
            link(v.tensor_scalar(tb[:, 3:4], tb[:, 0:1], float(EXPERTS), float(BLOCK), ALU.is_lt, ALU.mult))
            link(v.tensor_tensor(tb[:, 4:5], tb[:, 2:3], tb[:, 3:4], ALU.mult))
            link(v.scalar_tensor_tensor(out=tb[:, 5:6], in0=tb[:, 0:1], scalar=float(CAP), in1=tb[:, 4:5],
                                        op0=ALU.mult, op1=ALU.add))
            link(v.tensor_scalar(tb[:, 6:7], tb[:, 0:1], float(EXPERTS - 1), None, ALU.min))
            for k, (src, shared) in enumerate(((6, C_SE), (5, C_SROW))):
                link(v.tensor_tensor(tb[:, src:src + 1], tb[:, src:src + 1], const[:, C_RM:C_RM + 1], ALU.mult))
                link(v.tensor_tensor(tb[:, 7:8], const[:, shared:shared + 1], const[:, C_SM:C_SM + 1], ALU.mult))
                ins = v.tensor_tensor(table_p[:, k:k + 1], tb[:, src:src + 1], tb[:, 7:8], ALU.add)
                if k == 0:
                    link(ins)
                else:
                    ins.then_inc(table_done, 1)
            for s in range(SUB):
                link(v.tensor_copy(pad_row[:, s, ROW_ID:ROW_ID + 1].bitcast(I32), ids[:, K_PAD + s:K_PAD + s + 1]))
            v.tensor_copy(top_f[:, 0:1], top_f[:, 1:2]).then_inc(pads_done, 1)
            for s in range(SUB):
                link(v.tensor_tensor(pad_f[:, s, 0:EXPERTS], cnt[:], const[:, C_CAP:C_CAP + EXPERTS], ALU.add))
                link(v.tensor_scalar(pad_f[:, s, EXPERTS:EXPERTS + 1], const[:, C_P:C_P + 1], float(EXPERTS * CAP + s * P),
                                     None, ALU.add))
                link(v.tensor_scalar(pad_f[:, s, 0:EXPERTS], pad_f[:, s, 0:EXPERTS], const[:, C_P:C_P + 1],
                                     float(s * P), ALU.add, ALU.add))
            v.tensor_copy(pad_slots[:], pad_f[:]).then_inc(pads_done, 1)
            dve.wait_ge(pads_done, 2)


def phase_b(nc, sb, sem, bank, ident, table, table_in, load_w1, load_w2, w1_raw, w2_raw, w1_in, w2_in, out, rows, w1, w2):
    with ExitStack() as st:
        def two(name, shape, dt=F32):
            return [sb(st, f"{name}{j}", shape, dt) for j in range(2)]

        w1_hi, w1_lo = two("w1_hi", [P, DC, 2 * WIDTH], F32R), two("w1_lo", [P, DC, 2 * WIDTH], F32R)
        w2_hi, w2_lo = two("w2_hi", [P, 3, D], F32R), two("w2_lo", [P, 3, D], F32R)
        xr = two("xr", [P, SUB, ROW])
        xe_hi, xe_lo = two("xe_hi", [P, DC, BLOCK], F32R), two("xe_lo", [P, DC, BLOCK], F32R)
        silu = two("silu", [P, 3, BLOCK])
        act_f = two("act_f", [P, 3, BLOCK])
        act_hi, act_lo = two("act_hi", [P, 3, BLOCK], F32R), two("act_lo", [P, 3, BLOCK], F32R)
        y = two("y", [P, SUB, D])
        row_w, row_id = two("row_w", [P, SUB, 1]), two("row_id", [P, SUB, 1], I32)

        xr_in = [sem(f"xr_in{j}") for j in range(2)]
        w1_hi_done, w1_lo_done, w2_hi_done, w2_lo_done = (
            sem(n) for n in ("w1_hi_done", "w1_lo_done", "w2_hi_done", "w2_lo_done"))
        xe_mm, xe_hi_done, xe_lo_done = sem("xe_mm"), sem("xe_hi_done"), sem("xe_lo_done")
        h_mm, silu_done, act_done, act_hi_done, act_lo_done = (
            sem(n) for n in ("h_mm", "silu_done", "act_done", "act_hi_done", "act_lo_done"))
        y_mm, y_done = sem("y_mm"), sem("y_done")
        meta_done = sem("meta_done")
        added = [sem(f"added{j}") for j in range(2)]
        out_rows = out.rearrange("b p n -> (b p) n")
        passed, passed_sp = sem("passed"), sem("passed_sp")
        block = st.enter_context(nc.Block())

        PREPARE, INNER, OUTER = range(3)
        DEPTH, PEELED = 3, 4

        @block.sync
        def _(sp):
            def expert(g):
                return sp.value_load(table[0:1, bass.ds(g * 2, 1)], min_val=0, max_val=EXPERTS + SHARED - 1)

            def one_round(at):
                if at(PREPARE):
                    g, j, n = at(PREPARE)
                    first = sp.value_load(table[0:1, bass.ds(g * 2 + 1, 1)], min_val=0, max_val=ROWS - BLOCK)
                    if not (isinstance(g, int) and g < 2):
                        e = expert(g)
                        waits_apart(sp, passed_sp, (w1_hi_done, g - 1))
                        waits_apart(sp, passed_sp, (w1_lo_done, g - 1))
                        load_w1(sp, e, j)
                        waits_apart(sp, passed_sp, (xe_mm, g - 1))
                        waits_apart(sp, passed_sp, (meta_done, (g - 1) * 2))
                    sp.dma_start(xr[j][:], rows[bass.ds(first, BLOCK), :].rearrange("(s p) n -> p s n", p=P))\
                        .then_inc(xr_in[j], 16)
                if at(INNER):
                    g, j, n = at(INNER)
                    if not (isinstance(g, int) and g < 2):
                        e = expert(g)
                        waits_apart(sp, passed_sp, (w2_hi_done, (g - 1) * 2))
                        waits_apart(sp, passed_sp, (w2_lo_done, (g - 1) * 2))
                        load_w2(sp, e, j)

            rounds(sp, BLOCKS, DEPTH, PEELED, one_round)

        @block.scalar
        def _(act):
            a = nc.scalar

            def prepare(g, j, n):
                act.wait_ge(w1_in[j], 16 * (n + 1))
                need(act, h_mm, 3 * (g - 1))
                a.activation(w1_hi[j][:], w1_raw[j][:], ACT.Copy).then_inc(w1_hi_done, 1)
                act.wait_ge(xe_mm, g + 1)
                for s in range(SUB):
                    a.activation(xe_hi[j][:, :, s * P:(s + 1) * P],
                                 bank[s][:].rearrange("p (c n) -> p c n", c=DC), ACT.Copy).then_inc(xe_hi_done, 1)

            def inner(g, j, n):
                act.wait_ge(w2_in[j], 32 * (n + 1))
                need(act, y_mm, SUB * (g - 1))
                a.activation(w2_hi[j][:, 0:2, :], w2_raw[j][:, 0:2, :], ACT.Copy).then_inc(w2_hi_done, 1)
                a.activation(w2_hi[j][0:96, 2, :], w2_raw[j][0:96, 2, :], ACT.Copy).then_inc(w2_hi_done, 1)
                for c, (_, m) in enumerate(WC):
                    act.wait_ge(h_mm, 3 * g + c + 1)
                    need(act, act_done, 3 * (g - 2) + c + 1)
                    a.activation(silu[j][0:m, c, :], bank[2 + c][0:m, 0:BLOCK], ACT.Silu).then_inc(silu_done, 1)
                    act.wait_ge(act_done, 3 * g + c + 1)
                    need(act, y_mm, SUB * (g - 1))
                    a.activation(act_hi[j][0:m, c, :], act_f[j][0:m, c, :], ACT.Copy).then_inc(act_hi_done, 1)

            def one_round(at):
                if at(PREPARE):
                    prepare(*at(PREPARE))
                if at(INNER):
                    inner(*at(INNER))

            rounds(act, BLOCKS, DEPTH, PEELED, one_round)

        @block.gpsimd
        def _(pool):
            g_ = nc.gpsimd

            def inner(g, j, n):
                need(pool, y_mm, SUB * (g - 1))
                pool.wait_ge(w2_hi_done, 2 * (g + 1))
                g_.tensor_tensor(w2_lo[j][:, 0:2, :], w2_raw[j][:, 0:2, :], w2_hi[j][:, 0:2, :].bitcast(F32),
                                 ALU.subtract).then_inc(w2_lo_done, 1)
                g_.tensor_tensor(w2_lo[j][0:96, 2, :], w2_raw[j][0:96, 2, :], w2_hi[j][0:96, 2, :].bitcast(F32),
                                 ALU.subtract).then_inc(w2_lo_done, 1)

            def add(g, j, n):
                if isinstance(g, int):
                    if g >= 1:
                        pool.wait_ge(added[1 - j], 16 * SUB * (n + j))
                else:
                    pool.wait_ge(added[1 - j], 16 * SUB * (n + j))
                for s in range(SUB):
                    waits_apart(pool, passed, (y_done, SUB * g + s + 1))
                    g_.indirect_dma_start(out_rows,
                                          bass.IndirectOffsetOnAxis(row_id[j][:, s, :].bitcast(U32), 0),
                                          y[j][:, s, :], None, compute_op=ALU.add).then_inc(added[j], 16)

            def one_round(at):
                if at(INNER):
                    inner(*at(INNER))
                if at(OUTER):
                    add(*at(OUTER))

            rounds(pool, BLOCKS, DEPTH, PEELED, one_round)
            for j in range(2):
                pool.wait_ge(added[j], 16 * SUB * BLOCKS // 2)

        @block.tensor
        def _(pe):
            def prepare(g, j, n):
                pe.wait_ge(xr_in[j], 16 * (n + 1))
                need(pe, xe_lo_done, SUB * g)
                for s in range(SUB):
                    for c in range(DC):
                        last = nc.tensor.transpose(bank[s][:, c * P:(c + 1) * P], xr[j][:, s, c * P:(c + 1) * P], ident)
                last.then_inc(xe_mm, 1)

            def inner(g, j, n):
                pe.wait_ge(w1_lo_done, g + 1)
                pe.wait_ge(w1_hi_done, g + 1)
                pe.wait_ge(xe_lo_done, SUB * (g + 1))
                for c, (at, m) in enumerate(WC):
                    need(pe, act_done, 3 * (g - 1) + c + 1)
                    for half in range(2):
                        k = 0
                        for d in range(DC):
                            col = half * WIDTH + at
                            for w, xx in ((w1_hi, xe_hi), (w1_hi, xe_lo), (w1_lo, xe_hi)):
                                last = nc.tensor.matmul(bank[2 + c][0:m, half * BLOCK:(half + 1) * BLOCK],
                                                        w[j][:, d, col:col + m], xx[j][:, d, :],
                                                        start=(k == 0), stop=(k == 3 * DC - 1))
                                k += 1
                    last.then_inc(h_mm, 1)

            def outer(g, j, n):
                pe.wait_ge(act_lo_done, 3 * (g + 1))
                pe.wait_ge(w2_lo_done, 2 * (g + 1))
                for s in range(SUB):
                    need(pe, y_done, SUB * (g - 1) + s + 1)
                    k = 0
                    for c, (_, m) in enumerate(WC):
                        for l, w in ((act_hi, w2_hi), (act_hi, w2_lo), (act_lo, w2_hi)):
                            last = nc.tensor.matmul(bank[5 + s][:], l[j][0:m, c, s * P:(s + 1) * P], w[j][0:m, c, :],
                                                    start=(k == 0), stop=(k == 8))
                            k += 1
                    last.then_inc(y_mm, 1)

            def one_round(at):
                for stage, work in ((PREPARE, prepare), (INNER, inner), (OUTER, outer)):
                    if at(stage):
                        work(*at(stage))

            rounds(pe, BLOCKS, DEPTH, PEELED, one_round)

        @block.vector
        def _(dve):
            v = nc.vector

            def prepare(g, j, n):
                dve.wait_ge(w1_hi_done, g + 1)
                need(dve, h_mm, 3 * (g - 1))
                v.tensor_tensor(w1_lo[j][:], w1_raw[j][:], w1_hi[j][:].bitcast(F32), ALU.subtract)\
                    .then_inc(w1_lo_done, 1)
                for s in range(SUB):
                    dve.wait_ge(xe_hi_done, SUB * g + s + 1)
                    v.tensor_tensor(xe_lo[j][:, :, s * P:(s + 1) * P], bank[s][:].rearrange("p (c n) -> p c n", c=DC),
                                    xe_hi[j][:, :, s * P:(s + 1) * P].bitcast(F32), ALU.subtract).then_inc(xe_lo_done, 1)

            def inner(g, j, n):
                e = dve.value_load(table[0:1, bass.ds(g * 2, 1)], min_val=0, max_val=EXPERTS + SHARED - 1)
                dve.wait_ge(xr_in[j], 16 * (n + 1))
                if not (isinstance(g, int) and g < 2):
                    dve.wait_ge(added[j], 16 * SUB * n)
                v.tensor_copy(row_w[j][:], xr[j][:, :, bass.ds(e + ROW_W, 1)]).then_inc(meta_done, 1)
                v.tensor_copy(row_id[j][:], xr[j][:, :, ROW_ID:ROW_ID + 1].bitcast(I32)).then_inc(meta_done, 1)
                for c, (_, m) in enumerate(WC):
                    dve.wait_ge(silu_done, 3 * g + c + 1)
                    need(dve, act_lo_done, 3 * (g - 2) + c + 1)
                    v.tensor_tensor(act_f[j][0:m, c, :], silu[j][0:m, c, :], bank[2 + c][0:m, BLOCK:2 * BLOCK], ALU.mult)\
                        .then_inc(act_done, 1)
                    dve.wait_ge(act_hi_done, 3 * g + c + 1)
                    need(dve, y_mm, SUB * (g - 1))
                    v.tensor_tensor(act_lo[j][0:m, c, :], act_f[j][0:m, c, :], act_hi[j][0:m, c, :].bitcast(F32),
                                    ALU.subtract).then_inc(act_lo_done, 1)

            def outer(g, j, n):
                dve.wait_ge(meta_done, 2 * (g + 1))
                for s in range(SUB):
                    dve.wait_ge(y_mm, SUB * g + s + 1)
                    v.tensor_scalar(y[j][:, s, :], bank[5 + s][:], row_w[j][:, s, :], None, ALU.mult)\
                        .then_inc(y_done, 1)

            def one_round(at):
                for stage, work in ((PREPARE, prepare), (INNER, inner), (OUTER, outer)):
                    if at(stage):
                        work(*at(stage))

            rounds(dve, BLOCKS, DEPTH, PEELED, one_round)


def kernel(**inputs):
    import numpy as np
    import concourse.bacc as bacc
    from concourse.bass_utils import run_bass_kernel_spmd

    def arr(name):
        return np.asarray(inputs[name])

    def chunks(w):
        return np.ascontiguousarray(w.reshape(w.shape[0] // P, P, w.shape[1]).transpose(1, 0, 2))

    w1 = arr("L0_ffn_w1")
    s1 = arr("L0_ffn_shared_w1").reshape(2, SHARED, WIDTH, D).transpose(1, 0, 2, 3).reshape(SHARED, 2 * WIDTH, D)
    w1 = np.concatenate([w1, s1]).transpose(0, 2, 1)
    w1 = np.ascontiguousarray(w1.reshape(-1, DC, P, 2 * WIDTH).transpose(0, 2, 1, 3))
    w2 = arr("L0_ffn_w2")
    s2 = arr("L0_ffn_shared_w2").reshape(D, SHARED, WIDTH).transpose(1, 0, 2)
    w2t = np.concatenate([w2, s2]).transpose(0, 2, 1)
    w2p = np.zeros((w2t.shape[0], 3 * P, D), w2t.dtype)
    w2p[:, :WIDTH] = w2t
    cf, ci = constants()
    arrays = {
        "x": arr("x"),
        "ctx_t": np.ascontiguousarray(arr("ctx_1024").transpose(0, 2, 1).reshape(BATCHES, CC, P, P).transpose(0, 2, 1, 3)),
        "pos": np.ascontiguousarray(arr("fside_BxSx2_0").transpose(1, 0, 2)),
        "wq": chunks(arr("L0_xattn_Wq")).reshape(P, -1),
        "wkv": chunks(arr("L0_xattn_Wkv")).reshape(P, -1),
        "wout": chunks(arr("L0_xattn_Wout")).reshape(P, -1),
        "bout": np.ascontiguousarray(np.broadcast_to(arr("L0_xattn_bout"), (P, D))),
        "gates": np.ascontiguousarray(np.broadcast_to(np.concatenate([arr("g_xattn"), arr("g_ffn")]), (P, 2))),
        "gate_w": chunks(arr("L0_ffn_gate_w").T),
        "w1": w1,
        "w2": w2p.reshape(-1, 3, P, D),
        "cf": cf,
        "ci": ci,
    }
    nc = bacc.Bacc("TRN2", target_bir_lowering=False, num_devices=1)
    args = [nc.dram_tensor(f"in_{n}", a.shape, mybir.dt.from_np(a.dtype), kind="ExternalInput").ap()
            for n, a in arrays.items()]
    out = nc.dram_tensor("out", (BATCHES + SUB, P, D), F32, kind="ExternalOutput").ap()
    build(nc, *args, out)
    r = run_bass_kernel_spmd(nc, [{f"in_{n}": a for n, a in arrays.items()}], core_ids=[0])
    return r.results[0]["out"][:BATCHES]
```

```python
from contextlib import ExitStack

import concourse.bass as bass
from concourse import mybir

F32 = mybir.dt.float32
F32R = mybir.dt.float32r
I32 = mybir.dt.int32
U32 = mybir.dt.uint32
ALU = mybir.AluOpType
ACT = mybir.ActivationFunctionType
AX = mybir.AxisListType

P = 128
BATCHES = 16
D = 512
DC = D // P
CTX = 256
CC = CTX // P
HEADS = 32
HD = D // HEADS
ANG = 8
GROUPS = 8
TOKENS = BATCHES * P
EXPERTS = 16
TOPK = 6
WIDTH = 352
WC = [(0, 128), (128, 128), (256, 96)]
SHARED = 2
BLOCK = 256
SUB = BLOCK // P
CAP = TOKENS + BLOCK
ROWS = EXPERTS * CAP + BLOCK
BLOCKS = TOKENS * TOPK // BLOCK + EXPERTS
ROW_W = D
ROW_ID = D + EXPERTS
ROW = ROW_ID + 2
EPS = 1e-5
SCALE = HD ** -0.5
TWO_PI = 6.283185307179586
TWO_PI_HI = 6.28125
NEWTON = 3
RSQRT_BITS = 1597463007.0
ROUND = 12582912.0

C_ID, C_UP, C_ONE = 0, 128, 256
C_IOTA = 384
C_CAP = C_IOTA + 16
C_THR = C_CAP + 16
C_TRI = C_THR + 8
C_EVEN = C_TRI + 256
C_ODD = C_EVEN + 1
C_P = C_ODD + 1
C_FREQ = C_P + 1
C_N = C_FREQ + 8
K_ID, K_PAD, K_N = 0, BATCHES, BATCHES + SUB


def constants():
    import numpy as np
    c = np.zeros((P, C_N), np.float32)
    p = np.arange(P)
    c[:, C_ID:C_ID + P] = np.eye(P)
    c[:, C_UP:C_UP + P] = p[:, None] < p[None, :]
    c[:, C_ONE:C_ONE + P] = 1
    c[:, C_IOTA:C_IOTA + 16] = np.arange(16)
    c[:, C_CAP:C_CAP + 16] = np.arange(16) * CAP
    c[:, C_THR:C_THR + 8] = np.arange(8) * BLOCK
    c[:, C_TRI:C_TRI + 256] = (np.arange(16)[None, :] <= np.arange(16)[:, None]).reshape(1, 256)
    c[:, C_EVEN] = (p // HD) % 2 == 0
    c[:, C_ODD] = (p // HD) % 2 == 1
    c[:, C_P] = p
    c[:, C_FREQ:C_FREQ + 8] = np.tile(np.float32(10000.0) ** (-np.arange(4, dtype=np.float32) / 4), 2)
    k = np.zeros((P, K_N), np.int32)
    k[:, K_ID:K_ID + BATCHES] = np.arange(BATCHES)[None, :] * P + p[:, None]
    k[:, K_PAD:K_PAD + SUB] = TOKENS + np.arange(SUB)[None, :] * P + p[:, None]
    return c, k


def need(eng, sem, value):
    if isinstance(value, int) and value <= 0:
        return
    eng.wait_ge(sem, value)


def waits_apart(eng, passed, *waits):
    for sem, v in waits:
        need(eng, sem, v)
    if any(not isinstance(v, int) for _, v in waits):
        eng.sem_inc(passed, 1)


class Chain:

    def __init__(self, eng, sem, per, block):
        self.eng, self.sem, self.per, self.base, self.k = eng, sem, per, block * per, 0

    def step(self, instruction):
        self.k += 1
        instruction.then_inc(self.sem, 1)

    def sync(self, passed=None, *others):
        if passed:
            waits_apart(self.eng, passed, (self.sem, self.base + self.k), *others)
        else:
            need(self.eng, self.sem, self.base + self.k)

    def end(self):
        assert self.k == self.per, (self.k, self.per)


def rounds(eng, blocks, depth, peeled, one_round):
    def place(r, k):
        return (r - k, (r - k) % 2, (r - k) // 2)

    for r in list(range(peeled)):
        one_round(lambda k: place(r, k) if 0 <= r - k < blocks else None)
    with eng.Fori(peeled // 2, blocks // 2) as i:
        for r in range(2):
            one_round(lambda k: (2 * i + (r - k), (r - k) % 2, i + (r - k) // 2))
    for r in range(blocks, blocks + depth - 1):
        one_round(lambda k: place(r, k) if 0 <= r - k < blocks else None)


def build(nc, x, ctx_t, pos, wq, wkv, wout, bout, gates, gate_w, w1, w2, cf, ci, out):
    rows = nc.dram_tensor("expert_rows", (ROWS, ROW), F32, kind="Internal").ap()
    table_dram = nc.dram_tensor("block_table", (BLOCKS, 2), I32, kind="Internal").ap()

    with ExitStack() as whole:
        def sb(stack, name, shape, dt=F32):
            return stack.enter_context(nc.sbuf_tensor(name, shape, dt))

        def twice(stack, raw_name, lo_name, shape):
            with nc.sbuf_tensor(raw_name, shape, F32) as raw:
                pass
            return raw, sb(stack, lo_name, shape, F32R)

        def sem(name):
            return whole.enter_context(nc.semaphore(name))

        bank = [whole.enter_context(nc.psum_tensor(f"bank{i}", [P, 512], F32)) for i in range(8)]
        w1_raw, s1_lo = zip(*[twice(whole, f"w1_raw{j}", f"s1_lo{j}", [P, DC, 2 * WIDTH]) for j in range(2)])
        w2_raw, s2_lo = zip(*[twice(whole, f"w2_raw{j}", f"s2_lo{j}", [P, 3, D]) for j in range(2)])
        const = sb(whole, "const", [P, C_N])
        table = sb(whole, "table", [1, 2 * BLOCKS], I32)
        ids = sb(whole, "ids", [P, K_N], I32)
        ident = const[:, C_ID:C_ID + P]

        w1_in = [sem(f"w1_in{j}") for j in range(2)]
        w2_in = [sem(f"w2_in{j}") for j in range(2)]
        pad_at = sb(whole, "pad_at", [P, EXPERTS], I32)
        table_p = sb(whole, "table_p", [P, 2], I32)
        table_in = sem("table_in")
        pads_out = [sem(f"pads_out{k}") for k in range(EXPERTS // 4)]
        scattered = [sem(f"scattered{j}") for j in range(2)]

        def load_w1(sp, e, j):
            sp.dma_start(w1_raw[j][:], w1[e]).then_inc(w1_in[j], 16)

        def load_w2(sp, e, j):
            sp.dma_start(w2_raw[j][:, 0:2, :], w2[e, 0:2].rearrange("c p n -> p c n")).then_inc(w2_in[j], 16)
            sp.dma_start(w2_raw[j][0:96, 2, :], w2[e, 2, 0:96]).then_inc(w2_in[j], 16)

        phase_a(nc, sb, sem, bank, const, ident, ids, table, table_dram, table_p, table_in, pad_at, pads_out,
                scattered, load_w1, load_w2, twice, s1_lo, s2_lo,
                w1_raw, w2_raw, w1_in, w2_in, x, ctx_t, pos, wq, wkv, wout, bout, gates, gate_w, cf, ci, out, rows)
        phase_b(nc, sb, sem, bank, ident, ids, table, table_in, pad_at, pads_out, scattered, load_w1, load_w2,
                w1_raw, w2_raw, w1_in, w2_in, out, rows)


def phase_a(nc, sb, sem, bank, const, ident, ids, table, table_dram, table_p, table_in, pad_at, pads_out,
            scattered, load_w1, load_w2, twice, s1_lo, s2_lo,
            w1_raw, w2_raw, w1_in, w2_in, x, ctx_t, pos, wq, wkv, wout, bout, gates, gate_w, cf, ci, out, rows):
    with ExitStack() as st:
        def t(name, shape, dt=F32):
            return sb(st, name, shape, dt)

        def two(name, shape, dt=F32):
            return [sb(st, f"{name}{j}", shape, dt) for j in range(2)]

        w_hi = t("w_hi", [P, 6144], F32R)
        w_raw, w_lo = twice(st, "w_raw", "w_lo", [P, 6144])
        s1_hi, s2_hi = two("s1_hi", [P, DC, 2 * WIDTH], F32R), two("s2_hi", [P, 3, D], F32R)
        parts = {"q": (0, 2048), "kv": (2048, 4096), "o": (4096, 6144)}
        q_w = [w[:, 0:2048].rearrange("p (c n) -> p c n", c=DC) for w in (w_hi, w_lo)]
        kv_w = [w[:, 2048:4096].rearrange("p (c n) -> p c n", c=CC) for w in (w_hi, w_lo)]
        o_w = [w[:, 4096:6144].rearrange("p (c n) -> p c n", c=DC) for w in (w_hi, w_lo)]
        gate_hi = t("gate_hi", [P, DC, EXPERTS], F32R)
        gate_raw, gate_lo = twice(st, "gate_raw", "gate_lo", [P, DC, EXPERTS])
        bout_b = t("bout_b", [P, D])
        gate2 = t("gate2", [P, 2])
        tanh2 = t("tanh2", [P, 2])
        pos_in = t("pos_in", [P, BATCHES, 2])
        sincos = t("sincos", [P, 2, BATCHES, ANG])
        x_sb = two("x_sb", [P, D])
        x_res = t("x_res", [P, D])
        c_raw = two("c_raw", [P, CC, P])
        c_hi = t("c_hi", [P, CC, P], F32R)
        c_lo = t("c_lo", [P, CC, P], F32R)
        stats = t("stats", [P, 6])
        mean1 = t("mean1", [P, 2])
        rstd1 = t("rstd1", [P, 1])
        xn = t("xn", [P, D])
        xt_hi = t("xt_hi", [P, DC, P], F32R)
        xt_lo = t("xt_lo", [P, DC, P], F32R)
        q_cos, q_sin = t("q_cos", [P, D]), t("q_sin", [P, D])
        k_cos, k_sin = t("k_cos", [P, D]), t("k_sin", [P, D])
        q_rope, k_rope = t("q_rope", [P, D]), t("k_rope", [P, D])
        v_one = two("v_one", [P, HEADS, HD + 1])
        q_t = two("q_t", [P, DC, P])
        k_t = two("k_t", [P, DC, 2, P])
        smax = two("smax", [P, 4])
        soft = two("soft", [P, 4, P])
        ang, turn = (w[:].rearrange("p a b -> p (a b)")[:, 0:2 * BATCHES * ANG]
                     .rearrange("p (t b a) -> p t b a", t=2, b=BATCHES) for w in soft)
        soft_t = two("soft_t", [P, 4, P])
        rsum = t("rsum", [P, HEADS])
        attn = t("attn", [P, HEADS, HD])
        ot0, at_hi = twice(st, "ot0", "at_hi", [P, DC, P])
        ot1, at_lo = twice(st, "ot1", "at_lo", [P, DC, P])
        ot = (ot0, ot1)
        proj = attn[:].rearrange("p h d -> p (h d)")
        x1 = two("x1", [P, D])
        stats2 = t("stats2", [P, 6])
        mean2 = t("mean2", [P, 2])
        rstd2 = t("rstd2", [P, 1])
        row = two("row", [P, ROW])
        x2_hi, x2_lo = t("x2_hi", [P, DC, P], F32R), t("x2_lo", [P, DC, P], F32R)
        inner = t("inner", [P, SHARED, WIDTH])
        in_hi, in_lo = t("in_hi", [P, SHARED, 3, P], F32R), t("in_lo", [P, SHARED, 3, P], F32R)
        gmax, gneg, gsum, grec = (t(n, [P, 1]) for n in ("gmax", "gneg", "gsum", "grec"))
        gexp, prob = t("gexp", [P, EXPERTS]), t("prob", [P, EXPERTS])
        top, top_i, top_f = t("top", [P, 8]), t("top_i", [P, 8], U32), t("top_f", [P, 8])
        pick = t("pick", [P, TOPK, EXPERTS])
        pick_slot = t("pick_slot", [P, TOPK, EXPERTS])
        mask = t("mask", [P, EXPERTS])
        seen = t("seen", [P, EXPERTS])
        cnt, nblk, ends, past, past_end = (t(n, [P, EXPERTS]) for n in ("cnt", "nblk", "ends", "past", "past_end"))
        over, ends3 = t("over", [P, EXPERTS, 8]), t("ends3", [P, EXPERTS, EXPERTS])
        tb = t("tb", [P, 8])
        pad_rows = [w[:].rearrange("p h d -> p (h d)")[:, 0:ROW] for w in v_one]
        slot_e = t("slot_e", [P, EXPERTS])
        slot_f = t("slot_f", [P, 8])
        slots = two("slots", [P, 8], U32)

        small_in = sem("small_in")
        w_in = {name: sem(f"w_in_{name}") for name in parts}
        w_hi_done, w_lo_done = sem("w_hi_done"), sem("w_lo_done")
        init_done, ones_done = sem("init_done"), sem("ones_done")
        angles, sincos_done, tanh_done = sem("angles"), sem("sincos_done"), sem("tanh_done")
        x_in = [sem(f"x_in{j}") for j in range(2)]
        c_in = [sem(f"c_in{j}") for j in range(2)]
        var1, rstd1_done, xn_done = sem("var1"), sem("rstd1_done"), sem("xn_done")
        c_hi_done, c_lo_done = sem("c_hi_done"), sem("c_lo_done")
        xt_mm, xt_hi_done, xt_lo_done = sem("xt_mm"), sem("xt_hi_done"), sem("xt_lo_done")
        q_mm, k_mm, v_mm = sem("q_mm"), sem("k_mm"), sem("v_mm")
        q_rot, k_rot, q_rope_done, k_rope_done = sem("q_rot"), sem("k_rot"), sem("q_rope_done"), sem("k_rope_done")
        v_done, qt_mm, qt_done, kt_mm, kt_done = (sem(n) for n in ("v_done", "qt_mm", "qt_done", "kt_mm", "kt_done"))
        score_mm, shifted, exp_done, prob_mm, prob_done, pv_mm = (
            sem(n) for n in ("score_mm", "shifted", "exp_done", "prob_mm", "prob_done", "pv_mm"))
        attn_done, at_mm, at_hi_done, at_lo_done, o_mm, x1_done = (
            sem(n) for n in ("attn_done", "at_mm", "at_hi_done", "at_lo_done", "o_mm", "x1_done"))
        x1_out = [sem(f"x1_out{j}") for j in range(2)]
        var2, rstd2_done, row_done, x2_mm, x2_hi_done, x2_lo_done, gate_mm = (
            sem(n) for n in ("var2", "rstd2_done", "row_done", "x2_mm", "x2_hi_done", "x2_lo_done", "gate_mm"))
        s1_hi_done, s2_hi_done, s1_lo_done, s2_lo_done = (
            sem(n) for n in ("s1_hi_done", "s2_hi_done", "s1_lo_done", "s2_lo_done"))
        sg_mm, sg_done, su_mm, inner_done, in_mm, in_hi_done, in_lo_done, shared_mm, added_shared = (
            sem(n) for n in ("sg_mm", "sg_done", "su_mm", "inner_done", "in_mm", "in_hi_done", "in_lo_done",
                             "shared_mm", "added_shared"))
        gneg_done, gexp_done, mask_done, rank_mm, slot_done, wrow_done = (
            sem(n) for n in ("gneg_done", "gexp_done", "mask_done", "rank_mm", "slot_done", "wrow_done"))
        chain_tail, chain_place, rope_q_chain, rope_k_chain = (
            sem(n) for n in ("chain_tail", "chain_place", "rope_q_chain", "rope_k_chain"))
        stats1_done, smax_done = sem("stats1_done"), sem("smax_done")
        res_in, seen_done = sem("res_in"), sem("seen_done")
        count_mm, table_chain, table_done, table_out, pad_init, pads_done = (
            sem(n) for n in ("count_mm", "table_chain", "table_done", "table_out", "pad_init", "pads_done"))
        gate_cols, rank_cols = bank[6][:, 480:480 + EXPERTS], bank[7][:, 480:480 + EXPERTS]

        neg_half, vpos, newt = t("neg_half", [P, 1]), t("vpos", [P, 1]), t("newt", [P, 1])
        newton1, newton2 = sem("newton1"), sem("newton2")
        passed_v, passed_p = sem("passed_v"), sem("passed_p")
        ot_done, half_read = [sem(f"ot_done{k}") for k in range(2)], sem("half_read")
        ot_mm, psum_zeros = sem("ot_mm"), sem("psum_zeros")
        TAIL_STEPS = 13
        block = st.enter_context(nc.Block())

        LOAD, PROJECT, ATTEND, TAIL, PLACE = range(5)
        DEPTH, PEELED = 5, 6

        def earlier(at, u, back):
            return (at(ATTEND), u - back) if u >= back else (at(TAIL), u - back + GROUPS)

        @block.sync
        def _(sp):
            sp.dma_start(x_sb[0][:], x[0]).then_inc(x_in[0], 16)
            sp.dma_start(const[:], cf).then_inc(small_in, 16)
            sp.dma_start(ids[:], ci).then_inc(small_in, 16)
            sp.dma_start(pos_in[:], pos).then_inc(small_in, 16)
            sp.dma_start(gate2[:], gates).then_inc(small_in, 16)
            sp.dma_start(bout_b[:], bout).then_inc(small_in, 16)
            sp.dma_start(gate_raw[:], gate_w).then_inc(small_in, 16)

            def first_pads(experts):
                for e in experts:
                    first = sp.value_load(pad_at[0:1, e:e + 1], min_val=e * CAP, max_val=e * CAP + TOKENS)
                    for s in range(SUB):
                        sp.dma_start(rows[bass.ds(first + s * P, P), :], pad_rows[s]).then_inc(pads_out[0], 16)

            def one_round(at):
                if at(LOAD):
                    b, j, n = at(LOAD)
                    need(sp, xn_done, b - 1)
                    need(sp, c_lo_done, b - 1)
                    if not (isinstance(b, int) and b == 0):
                        sp.dma_start(x_sb[j][:], x[b]).then_inc(x_in[j], 16)
                    sp.dma_start(c_raw[j][:], ctx_t[b]).then_inc(c_in[j], 16)
                    if isinstance(b, int) and b == 0:
                        for name, w in (("q", wq), ("kv", wkv), ("o", wout)):
                            a, z = parts[name]
                            sp.dma_start(w_raw[:, a:z], w).then_inc(w_in[name], 16)
                    if isinstance(b, int) and b < 2:
                        load_w1(sp, EXPERTS + b, b)
                        load_w2(sp, EXPERTS + b, b)
                if at(TAIL):
                    b = at(TAIL)[0]
                    need(sp, x1_done, b)
                    sp.dma_start(x_res[:], x[b]).then_inc(res_in, 16)
                if at(PLACE):
                    b, j, n = at(PLACE)
                    if isinstance(b, int) and b == BATCHES - 1:
                        sp.wait_ge(su_mm, SHARED * BATCHES)
                        load_w1(sp, 0, 0)
                        sp.wait_ge(pads_done, SUB + 1)
                        first_pads(range(0, 2))
                        sp.wait_ge(table_done, 1)
                        sp.dma_start(table_dram, table_p[0:BLOCKS, :]).then_inc(table_out, 16)
                        first_pads(range(2, 4))
                        sp.wait_ge(table_out, 16)
                        sp.dma_start(table[:], table_dram.rearrange("(a g) c -> a (g c)", a=1)).then_inc(table_in, 16)
                    sp.wait_ge(added_shared, b + 1)
                    sp.dma_start(out[b], x1[j][:]).then_inc(x1_out[j], 16)

            rounds(sp, BATCHES, DEPTH, PEELED, one_round)
            sp.wait_ge(shared_mm, BATCHES)
            load_w2(sp, 0, 0)
            sp.wait_ge(table_in, 16)
            second = sp.value_load(table[0:1, 2:3], min_val=0, max_val=EXPERTS - 1)
            load_w1(sp, second, 1)
            load_w2(sp, second, 1)
            for j in range(2):
                sp.wait_ge(x1_out[j], BATCHES // 2 * 16)

        @block.gpsimd
        def _(pool):
            g = nc.gpsimd
            for j in range(2):
                g.memset(v_one[j][:], 1.0).then_inc(ones_done, 1)
                g.memset(row[j][:], 0.0).then_inc(init_done, 1)
            g.memset(seen[:], 0.0).then_inc(init_done, 1)
            g.memset(slot_f[:], 0.0).then_inc(init_done, 1)

            def pairs(out_t, cos, sin, chain, done, b):
                o = out_t[:].rearrange("p (a c) -> p a c", c=2)
                c = cos[:].rearrange("p (a c) -> p a c", c=2)
                s = sin[:].rearrange("p (a c) -> p a c", c=2)
                g.tensor_tensor(o[:, :, 0], c[:, :, 0], s[:, :, 1], ALU.subtract).then_inc(chain, 1)
                need(pool, chain, b + 1)
                g.tensor_tensor(o[:, :, 1], s[:, :, 0], c[:, :, 1], ALU.add).then_inc(done, 1)

            def rsqrt(stat, y, chain_sem, done, b):
                ch = Chain(pool, chain_sem, 2 + 3 * NEWTON, b)
                ch.step(g.tensor_scalar(neg_half[:], stat[:, 1:2], EPS, -0.5, ALU.add, ALU.mult))
                ch.sync(passed_p)
                ch.step(g.tensor_scalar(vpos[:], neg_half[:], -2.0, None, ALU.mult))
                ch.sync(passed_p)
                ch.step(g.tensor_scalar(y[:].bitcast(I32), vpos[:].bitcast(I32), -0.5, RSQRT_BITS, ALU.mult, ALU.add))
                ch.sync()
                for k in range(NEWTON):
                    ch.step(g.tensor_tensor(newt[:], y[:], y[:], ALU.mult))
                    ch.sync(passed_p)
                    ch.step(g.tensor_scalar(newt[:], newt[:], neg_half[:, 0:1], 1.5, ALU.mult, ALU.add))
                    ch.sync()
                    last = g.tensor_tensor(y[:], y[:], newt[:], ALU.mult)
                    if k < NEWTON - 1:
                        ch.step(last)
                        ch.sync()
                    else:
                        last.then_inc(done, 1)
                ch.end()

            def split_shared(k):
                pool.wait_ge(s2_hi_done, 2 * (k + 1))
                g.tensor_tensor(s2_lo[k][:, 0:2, :], w2_raw[k][:, 0:2, :], s2_hi[k][:, 0:2, :].bitcast(F32),
                                ALU.subtract).then_inc(s2_lo_done, 1)
                g.tensor_tensor(s2_lo[k][0:96, 2, :], w2_raw[k][0:96, 2, :], s2_hi[k][0:96, 2, :].bitcast(F32),
                                ALU.subtract).then_inc(s2_lo_done, 1)

            def scatter(b, j, n):
                waits_apart(pool, passed_p, (slot_done, b + 1), (wrow_done, 2 * (b + 1)))
                for k in range(TOPK):
                    g.indirect_dma_start(rows, bass.IndirectOffsetOnAxis(slots[j][:, k:k + 1], 0), row[j][:], None)\
                        .then_inc(scattered[j], 16)

            def one_round(at):
                if at(PROJECT):
                    b, j, n = at(PROJECT)
                    pool.wait_ge(q_rot, 2 * (b + 1))
                    need(pool, qt_mm, b)
                    pairs(q_rope, q_cos, q_sin, rope_q_chain, q_rope_done, b)
                    pool.wait_ge(k_rot, 2 * (b + 1))
                    need(pool, kt_mm, b)
                    pairs(k_rope, k_cos, k_sin, rope_k_chain, k_rope_done, b)
                if at(LOAD):
                    b, j, n = at(LOAD)
                    waits_apart(pool, passed_p, (var1, b + 1), (xn_done, b))
                    rsqrt(mean1, rstd1, newton1, rstd1_done, b)
                if at(TAIL):
                    b, j, n = at(TAIL)
                    waits_apart(pool, passed_p, (var2, b + 1), (row_done, b))
                    rsqrt(mean2, rstd2, newton2, rstd2_done, b)
                if at(PLACE):
                    if isinstance(at(PLACE)[0], int) and at(PLACE)[0] == BATCHES - 1:
                        pool.wait_ge(pv_mm, GROUPS * BATCHES)
                        for zeros in pad_rows:
                            g.memset(zeros, 0.0).then_inc(pad_init, 1)
                    scatter(*at(PLACE))
                if at(PROJECT) and isinstance(at(PROJECT)[0], int) and at(PROJECT)[0] < SHARED:
                    split_shared(at(PROJECT)[0])

            rounds(pool, BATCHES, DEPTH, PEELED, one_round)

        @block.scalar
        def _(act):
            a = nc.scalar
            act.wait_ge(small_in, 16 * 6)
            a.activation(tanh2[:], gate2[:], ACT.Tanh).then_inc(tanh_done, 1)
            act.wait_ge(angles, 7)
            a.activation(sincos[:], turn[:], ACT.Sin).then_inc(sincos_done, 1)

            def split_weights(name):
                lo, hi = parts[name]
                act.wait_ge(w_in[name], 16)
                a.activation(w_hi[:, lo:hi], w_raw[:, lo:hi], ACT.Copy).then_inc(w_hi_done, 1)

            def split_shared(k):
                act.wait_ge(w1_in[k], 16)
                a.activation(s1_hi[k][:], w1_raw[k][:], ACT.Copy).then_inc(s1_hi_done, 1)
                act.wait_ge(w2_in[k], 32)
                a.activation(s2_hi[k][:, 0:2, :], w2_raw[k][:, 0:2, :], ACT.Copy).then_inc(s2_hi_done, 1)
                a.activation(s2_hi[k][0:96, 2, :], w2_raw[k][0:96, 2, :], ACT.Copy).then_inc(s2_hi_done, 1)

            def first_work(u):
                if u == 0:
                    split_weights("kv")
                if u == 1:
                    split_weights("o")
                    a.activation(gate_hi[:], gate_raw[:], ACT.Copy).then_inc(w_hi_done, 1)
                    split_shared(0)

            def attend(at, u):
                if at(ATTEND):
                    b = at(ATTEND)[0]
                    act.wait_ge(shifted, b * GROUPS + u + 1)
                    a.activation(soft[u % 2][:], soft[u % 2][:], ACT.Exp, scale=SCALE).then_inc(exp_done, 1)
                of, v = earlier(at, u, 1)
                if of:
                    b = of[0]
                    act.wait_ge(prob_mm, b * GROUPS + v + 1)
                    need(act, pv_mm, b * GROUPS + v - 1)
                    a.activation(soft_t[v % 2][:].rearrange("p c n -> p (c n)"), bank[4 + v % 2][:], ACT.Copy)\
                        .then_inc(prob_done, 1)

            def one_round(at):
                for u in range(GROUPS):
                    if at(PROJECT) and u == 0:
                        b = at(PROJECT)[0]
                        act.wait_ge(xt_mm, b + 1)
                        need(act, q_mm, b)
                        a.activation(xt_hi[:].rearrange("p c n -> p (c n)"), bank[0][:], ACT.Copy)\
                            .then_inc(xt_hi_done, 1)
                    if at(TAIL) and u == 5:
                        b = at(TAIL)[0]
                        act.wait_ge(x2_mm, b + 1)
                        need(act, su_mm, SHARED * b)
                        a.activation(x2_hi[:].rearrange("p c n -> p (c n)"), bank[1][:], ACT.Copy)\
                            .then_inc(x2_hi_done, 1)
                    if at(TAIL) and u == 3:
                        b = at(TAIL)[0]
                        act.wait_ge(at_mm, b + 1)
                        need(act, o_mm, b)
                        a.activation(at_hi[:].rearrange("p c n -> p (c n)"), bank[1][:], ACT.Copy)\
                            .then_inc(at_hi_done, 1)
                    attend(at, u)
                    if at(ATTEND) and u == 5:
                        b = at(ATTEND)[0]
                        act.wait_ge(pv_mm, b * GROUPS + 4)
                        need(act, o_mm, b)
                        a.activation(ot[0][:].rearrange("p c n -> p (c n)"), bank[6][:], ACT.Copy)\
                            .then_inc(ot_done[0], 1)
                    if at(TAIL) and u == 1:
                        b = at(TAIL)[0]
                        act.wait_ge(pv_mm, (b + 1) * GROUPS)
                        need(act, o_mm, b)
                        a.activation(ot[1][:].rearrange("p c n -> p (c n)"), bank[7][:], ACT.Copy)\
                            .then_inc(ot_done[1], 1)
                    if at(PROJECT) and isinstance(at(PROJECT)[0], int) and at(PROJECT)[0] == 0:
                        first_work(u)
                    if at(PROJECT):
                        b, j, n = at(PROJECT)
                        if u == 3:
                            act.wait_ge(v_mm, b + 1)
                            need(act, pv_mm, (b - 1) * GROUPS)
                            act.wait_ge(ones_done, 2)
                            a.activation(v_one[j][:, :, 0:HD], bank[0][:].rearrange("p (h d) -> p h d", h=HEADS),
                                         ACT.Copy).then_inc(v_done, 1)
                        if u == 4:
                            act.wait_ge(qt_mm, b + 1)
                            need(act, score_mm, (b - 1) * GROUPS)
                            a.activation(q_t[j][:].rearrange("p c n -> p (c n)"), bank[0][:], ACT.Copy)\
                                .then_inc(qt_done, 1)
                        if u == 5:
                            act.wait_ge(kt_mm, b + 1)
                            need(act, score_mm, (b - 1) * GROUPS)
                            k4 = bank[0][:].rearrange("p (c n) -> p c n", c=DC)
                            a.activation(k_t[j][:, :, 0, :], k4, ACT.Copy, scale=const[:, C_EVEN:C_EVEN + 1])\
                                .then_inc(kt_done, 1)
                            a.activation(k_t[j][:, :, 1, :], k4, ACT.Copy, scale=const[:, C_ODD:C_ODD + 1])\
                                .then_inc(kt_done, 1)
                    if at(PROJECT) and isinstance(at(PROJECT)[0], int) and at(PROJECT)[0] == 1 and u == 4:
                        split_shared(1)
                    if at(LOAD) and isinstance(at(LOAD)[0], int) and at(LOAD)[0] == 0 and u == 5:
                        split_weights("q")
                    if at(LOAD) and u == 4:
                        b, j, n = at(LOAD)
                        act.wait_ge(c_in[j], 16 * (n + 1))
                        need(act, v_mm, b)
                        need(act, c_lo_done, b)
                        a.activation(c_hi[:], c_raw[j][:], ACT.Copy).then_inc(c_hi_done, 1)
                    if at(TAIL):
                        b, j, n = at(TAIL)
                        if u == 6:
                            act.wait_ge(gneg_done, b + 1)
                            a.activation(gexp[:], gate_cols, ACT.Exp, bias=gneg[:, 0:1],
                                         accum_out=gsum[:, 0:1]).then_inc(gexp_done, 1)
                            for k in range(SHARED):
                                act.wait_ge(sg_mm, SHARED * b + k + 1)
                                need(act, in_mm, SHARED * (b - 1) + k + 1)
                                a.activation(inner[:, k, :], bank[1 - k][:, 0:WIDTH], ACT.Silu).then_inc(sg_done, 1)
                    if at(PLACE) and u < SHARED:
                        b = at(PLACE)[0]
                        act.wait_ge(in_mm, SHARED * b + u + 1)
                        need(act, shared_mm, b)
                        a.activation(in_hi[:, u].rearrange("p c n -> p (c n)"), bank[1][:, 0:3 * P], ACT.Copy)\
                            .then_inc(in_hi_done, 1)

            rounds(act, BATCHES, DEPTH, PEELED, one_round)

        @block.tensor
        def _(pe):
            def three(dst, lhs, rhs, chunks, lhs_at, rhs_at):
                n = 0
                for c in range(chunks):
                    for l, r in ((0, 0), (0, 1), (1, 0)):
                        last = nc.tensor.matmul(dst, lhs_at(lhs[l], c), rhs_at(rhs[r], c),
                                                start=(n == 0), stop=(n == 3 * chunks - 1))
                        n += 1
                return last

            def four_transposes(dst, src):
                for c in range(DC):
                    last = nc.tensor.transpose(dst[:, c * P:(c + 1) * P], src[:, c * P:(c + 1) * P], ident)
                return last

            xt, ct, at_parts, x2 = (xt_hi, xt_lo), (c_hi, c_lo), (at_hi, at_lo), (x2_hi, x2_lo)
            pe.wait_ge(small_in, 16 * 6)
            pe.wait_ge(ones_done, 2)

            def scores(at, u):
                if at(ATTEND):
                    b, j, n = at(ATTEND)
                    if u == 0:
                        pe.wait_ge(qt_done, b + 1)
                        pe.wait_ge(kt_done, 2 * (b + 1))
                    r = 32 * (u % 4)
                    need(pe, shifted, b * GROUPS + u - 1)
                    for c in range(2):
                        ch = 2 * (u // 4) + c
                        last = nc.tensor.matmul(bank[2 + u % 2][:, c * 2 * P:(c + 1) * 2 * P],
                                                q_t[j][r:r + 32, ch, :],
                                                k_t[j][r:r + 32, ch].rearrange("p e n -> p (e n)"),
                                                start=True, stop=True)
                    last.then_inc(score_mm, 1)

            def probs(at, u):
                of, v = earlier(at, u, 1)
                if of:
                    b = of[0]
                    pe.wait_ge(exp_done, b * GROUPS + v + 1)
                    need(pe, prob_done, b * GROUPS + v - 1)
                    for h in range(4):
                        last = nc.tensor.transpose(bank[4 + v % 2][:, h * P:(h + 1) * P], soft[v % 2][:, h, :], ident)
                    last.then_inc(prob_mm, 1)

            def values(at, u):
                of, v = earlier(at, u, 2)
                if of:
                    b, j, n = of
                    pe.wait_ge(prob_done, b * GROUPS + v + 1)
                    if v == 0:
                        need(pe, half_read, b)
                        if isinstance(b, int) and b == 0:
                            pe.wait_ge(psum_zeros, 2)
                    if v == 4:
                        need(pe, attn_done, b)
                        need(pe, slot_done, b - 1)
                    for i in range(4):
                        h = (2 * (v // 4) + i // 2) * 8 + (v % 4) * 2 + i % 2
                        last = nc.tensor.matmul(bank[6 + v // 4][32 * i:32 * i + HD + 1, (v % 4) * P:(v % 4 + 1) * P],
                                                v_one[j][:, h, :], soft_t[v % 2][:, i, :], start=True, stop=True)
                    last.then_inc(pv_mm, 1)

            def project(u, b, j, n):
                if u == 0:
                    pe.wait_ge(xn_done, b + 1)
                    need(pe, kt_done, 2 * b)
                    need(pe, inner_done, SHARED * (b - 2))
                    four_transposes(bank[0], xn).then_inc(xt_mm, 1)
                if u == 1:
                    if isinstance(b, int) and b == 0:
                        pe.wait_ge(w_lo_done, 1)
                    pe.wait_ge(xt_lo_done, b + 1)
                    three(bank[0][:], xt, q_w, DC, lambda t, c: t[:, c, :], lambda w, c: w[:, c, :]).then_inc(q_mm, 1)
                if u == 2:
                    if isinstance(b, int) and b == 0:
                        pe.wait_ge(w_lo_done, 2)
                    pe.wait_ge(c_lo_done, b + 1)
                    pe.wait_ge(q_rot, 2 * (b + 1))
                    three(bank[0][:], ct, kv_w, CC, lambda t, c: t[:, c, :], lambda w, c: w[:, c, 0:D])\
                        .then_inc(k_mm, 1)
                if u == 3:
                    pe.wait_ge(k_rot, 2 * (b + 1))
                    three(bank[0][:], ct, kv_w, CC, lambda t, c: t[:, c, :], lambda w, c: w[:, c, D:2 * D])\
                        .then_inc(v_mm, 1)
                if u == 4:
                    pe.wait_ge(q_rope_done, b + 1)
                    pe.wait_ge(v_done, b + 1)
                    four_transposes(bank[0], q_rope).then_inc(qt_mm, 1)
                if u == 5:
                    pe.wait_ge(k_rope_done, b + 1)
                    pe.wait_ge(qt_done, b + 1)
                    four_transposes(bank[0], k_rope).then_inc(kt_mm, 1)

            def tail(u, b, j, n):
                if u in (0, 2):
                    if u == 0:
                        need(pe, gexp_done, b)
                    pe.wait_ge(ot_done[u // 2], b + 1)
                    four_transposes(bank[6 + u // 2], ot[u // 2][:].rearrange("p c n -> p (c n)")).then_inc(ot_mm, 1)

            def transpose_values(b, j, n):
                pe.wait_ge(attn_done, b + 1)
                need(pe, in_lo_done, SHARED * b)
                four_transposes(bank[1], attn[:].rearrange("p h d -> p (h d)")).then_inc(at_mm, 1)

            def project_out(b, j, n):
                if isinstance(b, int) and b == 0:
                    pe.wait_ge(w_lo_done, 3)
                pe.wait_ge(at_lo_done, b + 1)
                three(bank[1][:], at_parts, o_w, DC, lambda t, c: t[:, c, :], lambda w, c: w[:, c, :])\
                    .then_inc(o_mm, 1)

            def tail_end(at, u, b, j, n):
                if u == 5:
                    pe.wait_ge(row_done, b + 1)
                    need(pe, added_shared, b)
                    four_transposes(bank[1], row[j]).then_inc(x2_mm, 1)
                if u == 6:
                    pe.wait_ge(x2_lo_done, b + 1)
                    if at(ATTEND):
                        pe.wait_ge(ot_done[0], at(ATTEND)[0] + 1)
                    if isinstance(b, int) and b == 0:
                        pe.wait_ge(w_lo_done, 4)
                    need(pe, gexp_done, b)
                    three(gate_cols, x2, (gate_hi, gate_lo), DC, lambda t, c: t[:, c, :], lambda w, c: w[:, c, :])\
                        .then_inc(gate_mm, 1)

            def rank(b):
                pe.wait_ge(mask_done, b + 1)
                need(pe, seen_done, b)
                need(pe, slot_done, b)
                nc.tensor.matmul(rank_cols, const[:, C_UP:C_UP + P], mask[:], start=True, stop=False)
                nc.tensor.matmul(rank_cols, const[:, C_ONE:C_ONE + P], seen[:], start=False, stop=True)\
                    .then_inc(rank_mm, 1)

            def shared_in(at, u):
                b, j, n = at(TAIL)
                if u == 6:
                    probs(at, u)
                for k in range(SHARED):
                    if u == 6:
                        if isinstance(b, int) and b == 0:
                            pe.wait_ge(s1_lo_done, k + 1)
                        if k == 0:
                            pe.wait_ge(x2_lo_done, b + 1)
                        if k == 1 and not at(ATTEND):
                            rank(b)
                        if k == 1 and at(PROJECT):
                            pe.wait_ge(kt_done, 2 * (at(PROJECT)[0] + 1))
                    else:
                        pe.wait_ge(sg_done, SHARED * b + k + 1)
                    col = (u - 6) * WIDTH
                    three(bank[1 - k][:, 0:WIDTH], x2, (s1_hi[k], s1_lo[k]), DC, lambda t, c: t[:, c, :],
                          lambda w, c: w[:, c, col:col + WIDTH]).then_inc(sg_mm if u == 6 else su_mm, 1)
                    if k == 0 and u == 7:
                        probs(at, u)
                    if k == 0 and at(ATTEND):
                        tail_end(at, u, *at(TAIL))

            def shared_out(at, u):
                b = at(PLACE)[0]
                if u < SHARED:
                    pe.wait_ge(inner_done, SHARED * b + u + 1)
                    need(pe, in_lo_done, SHARED * b + u)
                    for c, (col, m) in enumerate(WC):
                        last = nc.tensor.transpose(bank[1][0:m, c * P:(c + 1) * P], inner[:, u, col:col + m], ident)
                    last.then_inc(in_mm, 1)
                if u == 4 and isinstance(b, int) and b == BATCHES - 1:
                    pe.wait_ge(seen_done, BATCHES)
                    nc.tensor.matmul(rank_cols, const[:, C_ONE:C_ONE + P], seen[:], start=True, stop=True)\
                        .then_inc(count_mm, 1)
                if u == 4:
                    pe.wait_ge(in_lo_done, SHARED * (b + 1))
                    if at(TAIL):
                        pe.wait_ge(x1_done, at(TAIL)[0] + 1)
                    if isinstance(b, int) and b == 0:
                        pe.wait_ge(s2_lo_done, 2 * SHARED)
                    n = 0
                    for k in range(SHARED):
                        for c, (_, m) in enumerate(WC):
                            for l, w in ((in_hi, s2_hi), (in_hi, s2_lo), (in_lo, s2_hi)):
                                last = nc.tensor.matmul(bank[1][:], l[0:m, k, c, :], w[k][0:m, c, :],
                                                        start=(n == 0), stop=(n == 9 * SHARED - 1))
                                n += 1
                    last.then_inc(shared_mm, 1)

            def one_round(at):
                for u in range(GROUPS):
                    scores(at, u)
                    if at(PLACE) and at(TAIL) and u == 4:
                        rank(at(PLACE)[0])
                    if at(TAIL) and u == 2:
                        tail(u, *at(TAIL))
                    if at(TAIL) and u == 3:
                        transpose_values(*at(TAIL))
                    if u == 3:
                        probs(at, u)
                    if at(PROJECT):
                        project(u, *at(PROJECT))
                    if at(TAIL) and not at(ATTEND) and u >= 6:
                        tail_end(at, u, *at(TAIL))
                    if at(TAIL) and u >= 6:
                        shared_in(at, u)
                    else:
                        if u != 3:
                            probs(at, u)
                        if at(TAIL):
                            if u == 0:
                                tail(u, *at(TAIL))
                            tail_end(at, u, *at(TAIL))
                    if at(PLACE) and u < SHARED:
                        shared_out(at, u)
                    values(at, u)
                    if at(TAIL) and u == 3:
                        project_out(*at(TAIL))
                    if at(PLACE) and u == 4:
                        shared_out(at, u)

            rounds(pe, BATCHES, DEPTH, PEELED, one_round)

        @block.vector
        def _(dve):
            v = nc.vector

            def first_angles():
                dve.wait_ge(small_in, 16 * 6)
                for p in range(2):
                    o = ang[:, 0, :, 4 * p:4 * p + 4]
                    v.tensor_tensor(o, pos_in[:, :, p:p + 1].to_broadcast([P, BATCHES, 4]),
                                    const[:, None, C_FREQ:C_FREQ + 4].to_broadcast([P, BATCHES, 4]), ALU.mult)\
                        .then_inc(angles, 1)
                dve.wait_ge(angles, 2)
                v.tensor_scalar(ang[:, 1], ang[:, 0], TWO_PI / 4, None, ALU.add).then_inc(angles, 1)
                dve.wait_ge(angles, 3)
                v.tensor_scalar(turn[:], ang[:], 1 / TWO_PI, ROUND, ALU.mult, ALU.add).then_inc(angles, 1)
                dve.wait_ge(angles, 4)
                v.tensor_scalar(turn[:], turn[:], -ROUND, None, ALU.add).then_inc(angles, 1)
                dve.wait_ge(angles, 5)
                v.scalar_tensor_tensor(out=ang[:], in0=turn[:], scalar=-TWO_PI_HI, in1=ang[:], op0=ALU.mult, op1=ALU.add)\
                    .then_inc(angles, 1)
                dve.wait_ge(angles, 6)
                v.scalar_tensor_tensor(out=turn[:], in0=turn[:], scalar=-(TWO_PI - TWO_PI_HI), in1=ang[:],
                                       op0=ALU.mult, op1=ALU.add).then_inc(angles, 1)

            def split_weights(n, name):
                lo, hi = parts[name]
                dve.wait_ge(w_hi_done, n + 1)
                v.tensor_tensor(w_lo[:, lo:hi], w_raw[:, lo:hi], w_hi[:, lo:hi].bitcast(F32), ALU.subtract)\
                    .then_inc(w_lo_done, 1)

            def split_shared(k):
                dve.wait_ge(s1_hi_done, k + 1)
                v.tensor_tensor(s1_lo[k][:], w1_raw[k][:], s1_hi[k][:].bitcast(F32), ALU.subtract)\
                    .then_inc(s1_lo_done, 1)

            def first_work(at, u):
                if at(LOAD) and at(LOAD)[0] == 0:
                    if u == 4:
                        first_angles()
                    if u == 7:
                        split_weights(0, "q")
                        dve.wait_ge(init_done, 4)
                        dve.wait_ge(tanh_done, 1)
                if at(PROJECT) and at(PROJECT)[0] == 0:
                    if u == 0:
                        split_weights(1, "kv")
                        dve.wait_ge(sincos_done, 1)
                    if u == 2:
                        for k in range(2):
                            v.memset(bank[6 + k][:], 0.0).then_inc(psum_zeros, 1)
                if at(PROJECT) and at(PROJECT)[0] == 1:
                    if u == 2:
                        split_weights(2, "o")
                        dve.wait_ge(w_hi_done, 4)
                        v.tensor_tensor(gate_lo[:], gate_raw[:], gate_hi[:].bitcast(F32), ALU.subtract)\
                            .then_inc(w_lo_done, 1)
                    if u in (4, 6):
                        split_shared((u - 4) // 2)

            def rotate(src, cos_o, sin_o, b, done):
                s4 = src.rearrange("p (h a c) -> p h a c", h=HEADS, c=2)
                for k, dst in ((1, cos_o), (0, sin_o)):
                    one = sincos[:, k, bass.ds(b, 1), :].rearrange("p o a -> p (o a)")
                    last = v.tensor_tensor(dst[:].rearrange("p (h a c) -> p h a c", h=HEADS, c=2), s4,
                                           one[:, None, :, None].to_broadcast([P, HEADS, ANG, 2]), ALU.mult)
                    last.then_inc(done, 1)

            def load(u, b, j, n):
                if u == 2:
                    dve.wait_ge(x_in[j], 16 * (n + 1))
                    v.bn_stats(stats[:], x_sb[j][:]).then_inc(stats1_done, 1)
                    waits_apart(dve, passed_v, (stats1_done, b + 1), (xn_done, b))
                    v.bn_aggr(mean1[:], stats[:]).then_inc(var1, 1)
                if u == 5:
                    dve.wait_ge(c_hi_done, b + 1)
                    need(dve, v_mm, b)
                    v.tensor_tensor(c_lo[:], c_raw[j][:], c_hi[:].bitcast(F32), ALU.subtract).then_inc(c_lo_done, 1)
                if u == 6:
                    dve.wait_ge(var1, b + 1)
                    dve.wait_ge(rstd1_done, b + 1)
                    need(dve, xt_mm, b)
                    v.tensor_scalar(xn[:], x_sb[j][:], mean1[:, 0:1], rstd1[:, 0:1], ALU.subtract, ALU.mult)\
                        .then_inc(xn_done, 1)

            def project(u, b, j, n):
                if u == 0:
                    dve.wait_ge(xt_hi_done, b + 1)
                    need(dve, q_mm, b)
                    v.tensor_tensor(xt_lo[:].rearrange("p c n -> p (c n)"), bank[0][:],
                                    xt_hi[:].rearrange("p c n -> p (c n)").bitcast(F32), ALU.subtract)\
                        .then_inc(xt_lo_done, 1)
                if u == 1:
                    dve.wait_ge(q_mm, b + 1)
                    need(dve, q_rope_done, b)
                    rotate(bank[0][:], q_cos, q_sin, b, q_rot)
                if u == 2:
                    dve.wait_ge(k_mm, b + 1)
                    need(dve, k_rope_done, b)
                    rotate(bank[0][:], k_cos, k_sin, b, k_rot)

            def attend(u, b, j, n):
                dve.wait_ge(score_mm, b * GROUPS + u + 1)
                s3 = bank[2 + u % 2][:].rearrange("p (h n) -> p h n", h=4)
                v.tensor_reduce(smax[u % 2][:], s3, AX.X, ALU.max).then_inc(smax_done, 1)
                dve.wait_ge(smax_done, b * GROUPS + u + 1)
                need(dve, prob_mm, b * GROUPS + u - 1)
                v.tensor_tensor(soft[u % 2][:], s3, smax[u % 2][:, :, None].to_broadcast([P, 4, P]), ALU.subtract)\
                    .then_inc(shifted, 1)

            def normalised_row(b, j, n):
                dve.wait_ge(var2, b + 1)
                dve.wait_ge(rstd2_done, b + 1)
                need(dve, scattered[j], 16 * TOPK * n)
                v.tensor_scalar(row[j][:, 0:D], x1[j][:], mean2[:, 0:1], rstd2[:, 0:1], ALU.subtract, ALU.mult)\
                    .then_inc(row_done, 1)

            def tail(u, b, j, n, ch):
                if u in (0, 2):
                    k = u // 2
                    dve.wait_ge(ot_mm, 2 * b + k + 1)
                    sums = bank[6 + k][:].rearrange("p (g e) -> p g e", e=32)[:, :, HD]
                    ch.step(v.reciprocal(rsum[:, 16 * k:16 * k + 16], sums))
                    ch.sync()
                    need(dve, at_mm, b)
                    for c in range(2):
                        src, scale = (w.rearrange("p (v a c e) -> p v a c e", v=4, a=2, c=2)[:, :, c]
                                      for w in (bank[6 + k][:], rsum[:, 16 * k:16 * k + 16]))
                        last = v.tensor_tensor(
                            attn[:, 16 * k + 8 * c:16 * k + 8 * c + 8, :].rearrange("p (v c) d -> p v c d", v=4),
                            src[:, :, :, 0:HD], scale.to_broadcast([P, 4, 2, HD]), ALU.mult)
                        if c == 0:
                            ch.step(last)
                        else:
                            last.then_inc(attn_done if k else half_read, 1)
                if u == 3:
                    dve.wait_ge(at_hi_done, b + 1)
                    need(dve, o_mm, b)
                    v.tensor_tensor(at_lo[:].rearrange("p c n -> p (c n)"), bank[1][:],
                                    at_hi[:].rearrange("p c n -> p (c n)").bitcast(F32), ALU.subtract)\
                        .then_inc(at_lo_done, 1)
                if u == 4:
                    dve.wait_ge(o_mm, b + 1)
                    ch.step(v.tensor_tensor(proj, bank[1][:], bout_b[:], ALU.add))
                    ch.sync()
                    dve.wait_ge(res_in, 16 * (b + 1))
                    need(dve, x1_out[j], 16 * n)
                    v.scalar_tensor_tensor(out=x1[j][:], in0=proj, scalar=tanh2[:, 0:1], in1=x_res[:],
                                           op0=ALU.mult, op1=ALU.add).then_inc(x1_done, 1)
                    dve.wait_ge(x1_done, b + 1)
                    ch.step(v.bn_stats(stats2[:], x1[j][:]))
                    ch.sync(passed_v)
                    v.bn_aggr(mean2[:], stats2[:]).then_inc(var2, 1)
                if u == 5:
                    dve.wait_ge(x2_hi_done, b + 1)
                    v.tensor_tensor(x2_lo[:].rearrange("p c n -> p (c n)"), bank[1][:],
                                    x2_hi[:].rearrange("p c n -> p (c n)").bitcast(F32), ALU.subtract)\
                        .then_inc(x2_lo_done, 1)
                if u == 6:
                    dve.wait_ge(gate_mm, b + 1)
                    ch.step(v.tensor_reduce(gmax[:], gate_cols, AX.X, ALU.max))
                    ch.sync()
                    v.tensor_scalar(gneg[:], gmax[:], -1.0, None, ALU.mult).then_inc(gneg_done, 1)
                if u == 7:
                    dve.wait_ge(gexp_done, b + 1)
                    ch.step(v.reciprocal(grec[:], gsum[:]))
                    ch.sync()
                    ch.step(v.tensor_scalar(prob[:], gexp[:], grec[:, 0:1], None, ALU.mult))
                    ch.sync(passed_v)
                    ch.step(v.max(top[:], prob[:]))
                    ch.sync(passed_v)
                    ch.step(v.max_index(top_i[:], top[:], prob[:]))
                    ch.sync()
                    ch.step(v.tensor_copy(top_f[:], top_i[:]))
                    ch.sync()
                    ch.step(v.tensor_tensor(pick[:],
                                            const[:, None, C_IOTA:C_IOTA + EXPERTS].to_broadcast([P, TOPK, EXPERTS]),
                                            top_f[:, 0:TOPK, None].to_broadcast([P, TOPK, EXPERTS]), ALU.is_equal))
                    ch.sync()
                    v.tensor_reduce(mask[:], pick[:].rearrange("p k e -> p e k"), AX.X, ALU.add).then_inc(mask_done, 1)
                    v.tensor_copy(row[j][:, ROW_ID:ROW_ID + 1].bitcast(I32), ids[:, bass.ds(K_ID + b, 1)])\
                        .then_inc(wrow_done, 1)
                    dve.wait_ge(mask_done, b + 1)
                    v.scalar_tensor_tensor(out=row[j][:, ROW_W:ROW_W + EXPERTS], in0=prob[:], scalar=tanh2[:, 1:2],
                                           in1=mask[:], op0=ALU.mult, op1=ALU.mult).then_inc(wrow_done, 1)
                    ch.end()
                    if isinstance(b, int) and b == BATCHES - 1:
                        place(b, j, n)
                    for k in range(SHARED):
                        inner_values(b, k)

            def inner_values(b, k):
                dve.wait_ge(su_mm, SHARED * b + k + 1)
                v.tensor_tensor(inner[:, k, :], inner[:, k, :], bank[1 - k][:, 0:WIDTH], ALU.mult)\
                    .then_inc(inner_done, 1)

            def shared_out(u, b, j, n):
                if u < SHARED:
                    dve.wait_ge(in_hi_done, SHARED * b + u + 1)
                    need(dve, shared_mm, b)
                    v.tensor_tensor(in_lo[:, u].rearrange("p c n -> p (c n)"), bank[1][:, 0:3 * P],
                                    in_hi[:, u].rearrange("p c n -> p (c n)").bitcast(F32), ALU.subtract)\
                        .then_inc(in_lo_done, 1)
                if u == 5:
                    dve.wait_ge(shared_mm, b + 1)
                    dve.wait_ge(x1_done, b + 1)
                    dve.wait_ge(row_done, b + 1)
                    v.scalar_tensor_tensor(out=x1[j][:], in0=bank[1][:], scalar=tanh2[:, 1:2], in1=x1[j][:],
                                           op0=ALU.mult, op1=ALU.add).then_inc(added_shared, 1)

            def place(b, j, n):
                ch = Chain(dve, chain_place, 3, b)
                dve.wait_ge(rank_mm, b + 1)
                ch.step(v.tensor_tensor(slot_e[:], rank_cols, const[:, C_CAP:C_CAP + EXPERTS],
                                        ALU.add))
                v.tensor_tensor(seen[:], seen[:], mask[:], ALU.add).then_inc(seen_done, 1)
                ch.sync()
                ch.step(v.tensor_tensor(pick_slot[:], pick[:], slot_e[:, None, :].to_broadcast([P, TOPK, EXPERTS]),
                                        ALU.mult))
                ch.sync()
                ch.step(v.tensor_reduce(slot_f[:, 0:TOPK], pick_slot[:], AX.X, ALU.add))
                ch.sync()
                need(dve, scattered[j], 16 * TOPK * n)
                v.tensor_copy(slots[j][:], slot_f[:]).then_inc(slot_done, 1)
                ch.end()

            def block_table():
                last = [0]

                def link(ins):
                    last[0] += 1
                    ins.then_inc(table_chain, 1)
                    dve.wait_ge(table_chain, last[0])

                dve.wait_ge(pad_init, SUB)
                for s in range(SUB):
                    v.tensor_copy(pad_rows[s][:, ROW_ID:ROW_ID + 1].bitcast(I32), ids[:, K_PAD + s:K_PAD + s + 1])\
                        .then_inc(pads_done, 1)
                dve.wait_ge(count_mm, 1)
                link(v.tensor_copy(cnt[:], rank_cols))
                v.tensor_tensor(pad_at[:], cnt[:], const[:, C_CAP:C_CAP + EXPERTS], ALU.add).then_inc(pads_done, 1)

                link(v.tensor_tensor(over[:], cnt[:, :, None].to_broadcast([P, EXPERTS, 8]),
                                     const[:, None, C_THR:C_THR + 8].to_broadcast([P, EXPERTS, 8]), ALU.is_gt))
                link(v.tensor_reduce(nblk[:], over[:], AX.X, ALU.add))
                link(v.tensor_scalar(nblk[:], nblk[:], 1.0, None, ALU.max))
                link(v.tensor_tensor(ends3[:], nblk[:, None, :].to_broadcast([P, EXPERTS, EXPERTS]),
                                     const[:, C_TRI:C_TRI + 256].rearrange("p (a c) -> p a c", a=EXPERTS), ALU.mult))
                link(v.tensor_reduce(ends[:], ends3[:], AX.X, ALU.add))
                block_no = const[:, C_P:C_P + 1]
                link(v.tensor_scalar(past[:], ends[:], block_no, None, ALU.is_le))
                link(v.tensor_tensor(past_end[:], past[:], ends[:], ALU.mult))
                link(v.tensor_reduce(tb[:, 0:1], past[:], AX.X, ALU.add))
                link(v.tensor_reduce(tb[:, 1:2], past_end[:], AX.X, ALU.max))
                link(v.tensor_tensor(tb[:, 2:3], block_no, tb[:, 1:2], ALU.subtract))
                link(v.tensor_scalar(tb[:, 3:4], tb[:, 0:1], float(EXPERTS), float(BLOCK), ALU.is_lt, ALU.mult))
                link(v.tensor_tensor(tb[:, 4:5], tb[:, 2:3], tb[:, 3:4], ALU.mult))
                link(v.tensor_scalar(table_p[:, 0:1], tb[:, 0:1], float(EXPERTS - 1), None, ALU.min))
                v.scalar_tensor_tensor(out=table_p[:, 1:2], in0=tb[:, 0:1], scalar=float(CAP), in1=tb[:, 4:5],
                                       op0=ALU.mult, op1=ALU.add).then_inc(table_done, 1)

            def one_round(at):
                ch = Chain(dve, chain_tail, TAIL_STEPS, at(TAIL)[0]) if at(TAIL) else None
                for u in range(GROUPS):
                    if at(TAIL) and u in (3, 4):
                        tail(u, *at(TAIL), ch)
                    if at(PLACE) and u == 5:
                        shared_out(u, *at(PLACE))
                    if at(TAIL) and u == 5:
                        normalised_row(*at(TAIL))
                    if at(ATTEND):
                        attend(u, *at(ATTEND))
                    if at(TAIL) and u == 2:
                        tail(u, *at(TAIL), ch)
                    if at(PROJECT):
                        project(u, *at(PROJECT))
                    if at(PLACE):
                        if u == 4 and not at(TAIL):
                            block_table()
                        if u < SHARED:
                            shared_out(u, *at(PLACE))
                    if at(TAIL) and u not in (2, 3, 4):
                        tail(u, *at(TAIL), ch)
                    if at(PLACE) and at(TAIL) and u == 4:
                        place(*at(PLACE))
                    if at(LOAD):
                        load(u, *at(LOAD))
                    if all(at(k) is None or isinstance(at(k)[0], int) for k in (LOAD, PROJECT)):
                        first_work(at, u)

            rounds(dve, BATCHES, DEPTH, PEELED, one_round)


def phase_b(nc, sb, sem, bank, ident, ids, table, table_in, pad_at, pads_out, scattered, load_w1, load_w2,
            w1_raw, w2_raw, w1_in, w2_in, out, rows):
    with ExitStack() as st:
        def two(name, shape, dt=F32):
            return [sb(st, f"{name}{j}", shape, dt) for j in range(2)]

        w1_hi, w1_lo = two("w1_hi", [P, DC, 2 * WIDTH], F32R), two("w1_lo", [P, DC, 2 * WIDTH], F32R)
        w2_hi, w2_lo = two("w2_hi", [P, 3, D], F32R), two("w2_lo", [P, 3, D], F32R)
        xr = two("xr", [P, SUB, ROW])
        xe_hi, xe_lo = two("xe_hi", [P, DC, BLOCK], F32R), two("xe_lo", [P, DC, BLOCK], F32R)
        silu = two("silu", [P, 3, BLOCK])
        act_f = two("act_f", [P, 3, BLOCK])
        act_hi, act_lo = two("act_hi", [P, 3, BLOCK], F32R), two("act_lo", [P, 3, BLOCK], F32R)
        y = two("y", [P, SUB, D])
        row_w, row_id = two("row_w", [P, SUB, 1]), two("row_id", [P, SUB, 1], I32)
        pad_row = sb(st, "pad_row", [P, SUB, ROW])

        xr_in = [sem(f"xr_in{j}") for j in range(2)]
        w1_hi_done, w1_lo_done, w2_hi_done, w2_lo_done = (
            sem(n) for n in ("w1_hi_done", "w1_lo_done", "w2_hi_done", "w2_lo_done"))
        xe_mm, xe_hi_done, xe_lo_done = sem("xe_mm"), sem("xe_hi_done"), sem("xe_lo_done")
        h_mm, silu_done, act_done, act_hi_done, act_lo_done = (
            sem(n) for n in ("h_mm", "silu_done", "act_done", "act_hi_done", "act_lo_done"))
        y_mm, y_done = sem("y_mm"), sem("y_done")
        meta_done = sem("meta_done")
        added = [sem(f"added{j}") for j in range(2)]
        out_rows = out.rearrange("b p n -> (b p) n")
        passed, passed_sp = sem("passed"), sem("passed_sp")
        pad_zeros, pad_row_done, pads_behind = sem("pad_zeros"), sem("pad_row_done"), sem("pads_behind")
        block = st.enter_context(nc.Block())

        PREPARE, INNER, OUTER = range(3)
        DEPTH, PEELED = 3, 4

        @block.sync
        def _(sp):
            def pads(experts):
                for e in experts:
                    first = sp.value_load(pad_at[0:1, e:e + 1], min_val=e * CAP, max_val=e * CAP + TOKENS)
                    sp.dma_start(rows[bass.ds(first, BLOCK), :].rearrange("(s p) n -> p s n", p=P), pad_row[:])\
                        .then_inc(pads_out[e // 4], 16)

            def expert(g):
                return sp.value_load(table[0:1, bass.ds(g * 2, 1)], min_val=0, max_val=EXPERTS - 1)

            def one_round(at):
                if at(PREPARE):
                    g, j, n = at(PREPARE)
                    if isinstance(g, int) and g == 0:
                        first = 0
                        for k in range(2):
                            sp.wait_ge(scattered[k], 16 * TOPK * BATCHES // 2)
                        sp.wait_ge(pads_out[0], 16 * SUB * 4)
                    else:
                        first = sp.value_load(table[0:1, bass.ds(g * 2 + 1, 1)], min_val=0, max_val=ROWS - BLOCK)
                        if not (isinstance(g, int) and g < 2):
                            e = expert(g)
                            waits_apart(sp, passed_sp, (w1_hi_done, g - 1))
                            waits_apart(sp, passed_sp, (w1_lo_done, g - 1))
                            load_w1(sp, e, j)
                        waits_apart(sp, passed_sp, (xe_mm, g - 1))
                        waits_apart(sp, passed_sp, (meta_done, (g - 1) * 2))
                    sp.dma_start(xr[j][:], rows[bass.ds(first, BLOCK), :].rearrange("(s p) n -> p s n", p=P))\
                        .then_inc(xr_in[j], 16)
                    if isinstance(g, int) and g == 1:
                        sp.wait_ge(pad_row_done, SUB)
                        for s in range(SUB):
                            sp.dma_start(out[BATCHES + s], pad_row[:, s, 0:D]).then_inc(pads_behind, 16)
                        sp.dma_start(rows[EXPERTS * CAP:ROWS, :].rearrange("(s p) n -> p s n", p=P), pad_row[:])\
                            .then_inc(pads_behind, 16)
                    if isinstance(g, int) and g > 0:
                        pads(range(4 * g, 4 * g + 4))
                        if g == 3:
                            for done in pads_out[1:]:
                                sp.wait_ge(done, 16 * 4)
                            sp.wait_ge(pads_behind, 16 * (SUB + 1))
                if at(INNER):
                    g, j, n = at(INNER)
                    if not (isinstance(g, int) and g < 2):
                        e = expert(g)
                        waits_apart(sp, passed_sp, (w2_hi_done, (g - 1) * 2))
                        waits_apart(sp, passed_sp, (w2_lo_done, (g - 1) * 2))
                        load_w2(sp, e, j)

            rounds(sp, BLOCKS, DEPTH, PEELED, one_round)

        @block.scalar
        def _(act):
            a = nc.scalar

            def prepare(g, j, n):
                act.wait_ge(w1_in[j], 16 * (n + 2))
                need(act, h_mm, 3 * (g - 1))
                a.activation(w1_hi[j][:], w1_raw[j][:], ACT.Copy).then_inc(w1_hi_done, 1)
                act.wait_ge(xe_mm, g + 1)
                for s in range(SUB):
                    a.activation(xe_hi[j][:, :, s * P:(s + 1) * P],
                                 bank[s][:].rearrange("p (c n) -> p c n", c=DC), ACT.Copy).then_inc(xe_hi_done, 1)

            def inner(g, j, n):
                act.wait_ge(w2_in[j], 32 * (n + 2))
                need(act, y_mm, SUB * (g - 1))
                a.activation(w2_hi[j][:, 0:2, :], w2_raw[j][:, 0:2, :], ACT.Copy).then_inc(w2_hi_done, 1)
                a.activation(w2_hi[j][0:96, 2, :], w2_raw[j][0:96, 2, :], ACT.Copy).then_inc(w2_hi_done, 1)
                for c, (_, m) in enumerate(WC):
                    act.wait_ge(h_mm, 3 * g + c + 1)
                    need(act, act_done, 3 * (g - 2) + c + 1)
                    a.activation(silu[j][0:m, c, :], bank[2 + c][0:m, 0:BLOCK], ACT.Silu).then_inc(silu_done, 1)
                    act.wait_ge(act_done, 3 * g + c + 1)
                    need(act, y_mm, SUB * (g - 1))
                    a.activation(act_hi[j][0:m, c, :], act_f[j][0:m, c, :], ACT.Copy).then_inc(act_hi_done, 1)

            def one_round(at):
                if at(PREPARE):
                    prepare(*at(PREPARE))
                if at(INNER):
                    inner(*at(INNER))

            rounds(act, BLOCKS, DEPTH, PEELED, one_round)

        @block.gpsimd
        def _(pool):
            g_ = nc.gpsimd
            g_.memset(pad_row[:], 0.0).then_inc(pad_zeros, 1)

            def inner(g, j, n):
                need(pool, y_mm, SUB * (g - 1))
                pool.wait_ge(w2_hi_done, 2 * (g + 1))
                g_.tensor_tensor(w2_lo[j][:, 0:2, :], w2_raw[j][:, 0:2, :], w2_hi[j][:, 0:2, :].bitcast(F32),
                                 ALU.subtract).then_inc(w2_lo_done, 1)
                g_.tensor_tensor(w2_lo[j][0:96, 2, :], w2_raw[j][0:96, 2, :], w2_hi[j][0:96, 2, :].bitcast(F32),
                                 ALU.subtract).then_inc(w2_lo_done, 1)

            def add(g, j, n):
                if isinstance(g, int):
                    if g >= 1:
                        pool.wait_ge(added[1 - j], 16 * SUB * (n + j))
                else:
                    pool.wait_ge(added[1 - j], 16 * SUB * (n + j))
                if isinstance(g, int) and g == 0:
                    pool.wait_ge(pads_behind, 16 * (SUB + 1))
                for s in range(SUB):
                    waits_apart(pool, passed, (y_done, SUB * g + s + 1))
                    g_.indirect_dma_start(out_rows,
                                          bass.IndirectOffsetOnAxis(row_id[j][:, s, :].bitcast(U32), 0),
                                          y[j][:, s, :], None, compute_op=ALU.add).then_inc(added[j], 16)

            def one_round(at):
                if at(INNER):
                    inner(*at(INNER))
                if at(OUTER):
                    add(*at(OUTER))

            rounds(pool, BLOCKS, DEPTH, PEELED, one_round)
            for j in range(2):
                pool.wait_ge(added[j], 16 * SUB * BLOCKS // 2)

        @block.tensor
        def _(pe):
            def prepare(g, j, n):
                pe.wait_ge(xr_in[j], 16 * (n + 1))
                need(pe, xe_lo_done, SUB * g)
                for s in range(SUB):
                    for c in range(DC):
                        last = nc.tensor.transpose(bank[s][:, c * P:(c + 1) * P], xr[j][:, s, c * P:(c + 1) * P], ident)
                last.then_inc(xe_mm, 1)

            def inner(g, j, n):
                pe.wait_ge(w1_lo_done, g + 1)
                pe.wait_ge(w1_hi_done, g + 1)
                pe.wait_ge(xe_lo_done, SUB * (g + 1))
                for c, (at, m) in enumerate(WC):
                    need(pe, act_done, 3 * (g - 1) + c + 1)
                    for half in range(2):
                        k = 0
                        for d in range(DC):
                            col = half * WIDTH + at
                            for w, xx in ((w1_hi, xe_hi), (w1_hi, xe_lo), (w1_lo, xe_hi)):
                                last = nc.tensor.matmul(bank[2 + c][0:m, half * BLOCK:(half + 1) * BLOCK],
                                                        w[j][:, d, col:col + m], xx[j][:, d, :],
                                                        start=(k == 0), stop=(k == 3 * DC - 1))
                                k += 1
                    last.then_inc(h_mm, 1)

            def outer(g, j, n):
                pe.wait_ge(act_lo_done, 3 * (g + 1))
                pe.wait_ge(w2_lo_done, 2 * (g + 1))
                for s in range(SUB):
                    need(pe, y_done, SUB * (g - 1) + s + 1)
                    k = 0
                    for c, (_, m) in enumerate(WC):
                        for l, w in ((act_hi, w2_hi), (act_hi, w2_lo), (act_lo, w2_hi)):
                            last = nc.tensor.matmul(bank[5 + s][:], l[j][0:m, c, s * P:(s + 1) * P], w[j][0:m, c, :],
                                                    start=(k == 0), stop=(k == 8))
                            k += 1
                    last.then_inc(y_mm, 1)

            def one_round(at):
                for stage, work in ((PREPARE, prepare), (INNER, inner), (OUTER, outer)):
                    if at(stage):
                        work(*at(stage))

            rounds(pe, BLOCKS, DEPTH, PEELED, one_round)

        @block.vector
        def _(dve):
            v = nc.vector

            dve.wait_ge(pad_zeros, 1)
            for s in range(SUB):
                v.tensor_copy(pad_row[:, s, ROW_ID:ROW_ID + 1].bitcast(I32), ids[:, K_PAD + s:K_PAD + s + 1])\
                    .then_inc(pad_row_done, 1)

            def prepare(g, j, n):
                dve.wait_ge(w1_hi_done, g + 1)
                need(dve, h_mm, 3 * (g - 1))
                v.tensor_tensor(w1_lo[j][:], w1_raw[j][:], w1_hi[j][:].bitcast(F32), ALU.subtract)\
                    .then_inc(w1_lo_done, 1)
                for s in range(SUB):
                    dve.wait_ge(xe_hi_done, SUB * g + s + 1)
                    v.tensor_tensor(xe_lo[j][:, :, s * P:(s + 1) * P], bank[s][:].rearrange("p (c n) -> p c n", c=DC),
                                    xe_hi[j][:, :, s * P:(s + 1) * P].bitcast(F32), ALU.subtract).then_inc(xe_lo_done, 1)

            def inner(g, j, n):
                if isinstance(g, int) and g == 0:
                    dve.wait_ge(table_in, 16)
                e = dve.value_load(table[0:1, bass.ds(g * 2, 1)], min_val=0, max_val=EXPERTS - 1)
                dve.wait_ge(xr_in[j], 16 * (n + 1))
                if not (isinstance(g, int) and g < 2):
                    dve.wait_ge(added[j], 16 * SUB * n)
                v.tensor_copy(row_w[j][:], xr[j][:, :, bass.ds(e + ROW_W, 1)]).then_inc(meta_done, 1)
                v.tensor_copy(row_id[j][:], xr[j][:, :, ROW_ID:ROW_ID + 1].bitcast(I32)).then_inc(meta_done, 1)
                for c, (_, m) in enumerate(WC):
                    dve.wait_ge(silu_done, 3 * g + c + 1)
                    need(dve, act_lo_done, 3 * (g - 2) + c + 1)
                    v.tensor_tensor(act_f[j][0:m, c, :], silu[j][0:m, c, :], bank[2 + c][0:m, BLOCK:2 * BLOCK], ALU.mult)\
                        .then_inc(act_done, 1)
                    dve.wait_ge(act_hi_done, 3 * g + c + 1)
                    need(dve, y_mm, SUB * (g - 1))
                    v.tensor_tensor(act_lo[j][0:m, c, :], act_f[j][0:m, c, :], act_hi[j][0:m, c, :].bitcast(F32),
                                    ALU.subtract).then_inc(act_lo_done, 1)

            def outer(g, j, n):
                dve.wait_ge(meta_done, 2 * (g + 1))
                for s in range(SUB):
                    dve.wait_ge(y_mm, SUB * g + s + 1)
                    v.tensor_scalar(y[j][:, s, :], bank[5 + s][:], row_w[j][:, s, :], None, ALU.mult)\
                        .then_inc(y_done, 1)

            def one_round(at):
                for stage, work in ((PREPARE, prepare), (INNER, inner), (OUTER, outer)):
                    if at(stage):
                        work(*at(stage))

            rounds(dve, BLOCKS, DEPTH, PEELED, one_round)


def kernel(**inputs):
    import numpy as np
    import concourse.bacc as bacc
    from concourse.bass_utils import run_bass_kernel_spmd

    def arr(name):
        return np.asarray(inputs[name])

    def chunks(w):
        return np.ascontiguousarray(w.reshape(w.shape[0] // P, P, w.shape[1]).transpose(1, 0, 2))

    w1 = arr("L0_ffn_w1")
    s1 = arr("L0_ffn_shared_w1").reshape(2, SHARED, WIDTH, D).transpose(1, 0, 2, 3).reshape(SHARED, 2 * WIDTH, D)
    w1 = np.concatenate([w1, s1]).transpose(0, 2, 1)
    w1 = np.ascontiguousarray(w1.reshape(-1, DC, P, 2 * WIDTH).transpose(0, 2, 1, 3))
    w2 = arr("L0_ffn_w2")
    s2 = arr("L0_ffn_shared_w2").reshape(D, SHARED, WIDTH).transpose(1, 0, 2)
    w2t = np.concatenate([w2, s2]).transpose(0, 2, 1)
    w2p = np.zeros((w2t.shape[0], 3 * P, D), w2t.dtype)
    w2p[:, :WIDTH] = w2t
    cf, ci = constants()
    arrays = {
        "x": arr("x"),
        "ctx_t": np.ascontiguousarray(arr("ctx_1024").transpose(0, 2, 1).reshape(BATCHES, CC, P, P).transpose(0, 2, 1, 3)),
        "pos": np.ascontiguousarray(arr("fside_BxSx2_0").transpose(1, 0, 2)),
        "wq": chunks(arr("L0_xattn_Wq")).reshape(P, -1),
        "wkv": chunks(arr("L0_xattn_Wkv")).reshape(P, -1),
        "wout": chunks(arr("L0_xattn_Wout")).reshape(P, -1),
        "bout": np.ascontiguousarray(np.broadcast_to(arr("L0_xattn_bout"), (P, D))),
        "gates": np.ascontiguousarray(np.broadcast_to(np.concatenate([arr("g_xattn"), arr("g_ffn")]), (P, 2))),
        "gate_w": chunks(arr("L0_ffn_gate_w").T),
        "w1": w1,
        "w2": w2p.reshape(-1, 3, P, D),
        "cf": cf,
        "ci": ci,
    }
    nc = bacc.Bacc("TRN2", target_bir_lowering=False, num_devices=1)
    args = [nc.dram_tensor(f"in_{n}", a.shape, mybir.dt.from_np(a.dtype), kind="ExternalInput").ap()
            for n, a in arrays.items()]
    out = nc.dram_tensor("out", (BATCHES + SUB, P, D), F32, kind="ExternalOutput").ap()
    build(nc, *args, out)
    r = run_bass_kernel_spmd(nc, [{f"in_{n}": a for n, a in arrays.items()}], core_ids=[0])
    return r.results[0]["out"][:BATCHES]
```
